# Optimizing a Trainium2 kernel written in Bass

```python
import numpy as np
import jax
import jax.numpy as jnp

def _softmax(x, axis=-1):
    return jax.nn.softmax(x, axis=axis)

def _gelu(x):
    return jax.nn.gelu(x, approximate=True)

def _silu(x):
    return jax.nn.silu(x)

def _sigmoid(x):
    return jax.nn.sigmoid(x)

def _layernorm(x, axis=-1, eps=1e-05):
    m = jnp.mean(x, axis=axis, keepdims=True)
    v = jnp.var(x, axis=axis, keepdims=True)
    return (x - m) / jnp.sqrt(v + eps)

def _scatter_add(tgt, idx, src, axis=0):
    return tgt.at[idx].add(src)

def _segment_sum(src, seg, n):
    return jax.ops.segment_sum(src, seg, n)
kernel_name = 'mk_vit_tower_d2_tok_img1024_r4_77c084'

def setup_inputs(seed: int=0):
    np.random.seed(seed)
    _w = jnp.asarray

    def _rec_inputs():
        import jax
        import jax.numpy as jnp
        _rk = jax.random.key(seed)
        x = -0.00016672 + 0.999947 * jax.random.normal(jax.random.fold_in(_rk, 1), (32, 3, 96, 96), jnp.float32)
        return x
    x = _rec_inputs()

    def _L0_tok_setup():
        import jax, jax.numpy as jnp
        import numpy as np
        B, C, H, W = (64, 3, 96, 96)
        P = 16
        NP = H // P * (W // P)
        PD = C * P * P
        ED = 256
        NCLS = 1

        def _layernorm(x, g, b, eps=1e-05):
            mu = jnp.mean(x, axis=-1, keepdims=True)
            var = jnp.mean(jnp.square(x - mu), axis=-1, keepdims=True)
            return (x - mu) * jax.lax.rsqrt(var + eps) * g + b
        key = jax.random.key(seed)
        ks = jax.random.split(key, 8)
        x = jax.random.normal(ks[0], (B, C, H, W), dtype=jnp.float32)
        ln1_g = jnp.ones((PD,), jnp.float32)
        ln1_b = jnp.zeros((PD,), jnp.float32)
        W_proj = jax.random.normal(ks[1], (PD, ED), jnp.float32) / np.sqrt(PD)
        b_proj = jnp.zeros((ED,), jnp.float32)
        ln2_g = jnp.ones((ED,), jnp.float32)
        ln2_b = jnp.zeros((ED,), jnp.float32)
        cls_token = jax.random.normal(ks[2], (1, NCLS, ED), jnp.float32)
        pos_emb = jax.random.normal(ks[3], (1, NP + NCLS, ED), jnp.float32)
        return {'x': x, 'ln1_g': ln1_g, 'ln1_b': ln1_b, 'W_proj': W_proj, 'b_proj': b_proj, 'ln2_g': ln2_g, 'ln2_b': ln2_b, 'cls_token': cls_token, 'pos_emb': pos_emb}
    _L0_tok_all = _L0_tok_setup()
    _L0_tok_in = {k: v for k, v in _L0_tok_all.items() if k in ('ln1_g', 'ln1_b', 'W_proj', 'b_proj', 'ln2_g', 'ln2_b', 'cls_token', 'pos_emb')}
    del _L0_tok_all

    def _L0_attn_setup():
        import jax, jax.numpy as jnp
        import numpy as np
        import math
        D_MODEL = 256
        N_HEADS = 16
        SPARSITY = 0.3
        key = jax.random.key(seed)
        ks = jax.random.split(key, 12)
        B, S, D = (4, 512, D_MODEL)
        Dh = D // 2
        sc = 0.02
        inp = {'x': jax.random.normal(ks[0], (B, S, D), dtype=jnp.float32), 'wq': jax.random.normal(ks[1], (D, D), dtype=jnp.float32) * sc, 'bq': jnp.zeros((D,), jnp.float32), 'wk': jax.random.normal(ks[2], (D, D), dtype=jnp.float32) * sc, 'bk': jnp.zeros((D,), jnp.float32), 'wv': jax.random.normal(ks[3], (D, D), dtype=jnp.float32) * sc, 'bv': jnp.zeros((D,), jnp.float32), 'wo': jax.random.normal(ks[4], (D, D), dtype=jnp.float32) * sc, 'bo': jnp.zeros((D,), jnp.float32), 'wi1': jax.random.normal(ks[5], (Dh, D), dtype=jnp.float32) * sc, 'bi1': jnp.zeros((Dh,), jnp.float32), 'wi2': jax.random.normal(ks[6], (1, Dh), dtype=jnp.float32) * sc, 'bi2': jnp.zeros((1,), jnp.float32)}
        return inp
    _L0_attn_all = _L0_attn_setup()
    _L0_attn_in = {k: v for k, v in _L0_attn_all.items() if k in ('wq', 'bq', 'wk', 'bk', 'wv', 'bv', 'wo', 'bo', 'wi1', 'bi1', 'wi2', 'bi2')}
    del _L0_attn_all

    def _L0_ffn_setup():
        import jax, jax.numpy as jnp
        import numpy as np
        EPS = 1e-05

        def _quantize(W):
            gamma = jnp.mean(jnp.abs(W))
            return jnp.clip(jnp.round(W / (gamma + EPS)), -1.0, 1.0)
        key = jax.random.key(seed)
        k_x, k_w1, k_b1, k_w2, k_b2 = jax.random.split(key, 5)
        n_embd = 256
        d_ff = 4 * n_embd
        B, S = (4, 1024)
        bound1 = 1.0 / np.sqrt(n_embd)
        bound2 = 1.0 / np.sqrt(d_ff)
        x = jax.random.normal(k_x, (B, S, n_embd), dtype=jnp.float32)
        W1 = jax.random.uniform(k_w1, (d_ff, n_embd), jnp.float32, -bound1, bound1)
        b1 = jax.random.uniform(k_b1, (d_ff,), jnp.float32, -bound1, bound1)
        W2 = jax.random.uniform(k_w2, (n_embd, d_ff), jnp.float32, -bound2, bound2)
        b2 = jax.random.uniform(k_b2, (n_embd,), jnp.float32, -bound2, bound2)
        return {'x': x, 'W1': W1, 'b1': b1, 'W2': W2, 'b2': b2}
    _L0_ffn_all = _L0_ffn_setup()
    _L0_ffn_in = {k: v for k, v in _L0_ffn_all.items() if k in ('W1', 'b1', 'W2', 'b2')}
    del _L0_ffn_all

    def _L1_attn_setup():
        import jax, jax.numpy as jnp
        import numpy as np
        import math
        B, T, C, NH = (4, 512, 256, 16)
        HS = C // NH

        def rope_cache(dim, max_pos):
            half = dim // 2
            inv_freq = 1.0 / 10000.0 ** (jnp.arange(half, dtype=jnp.float32) * 2.0 / dim)
            ang = jnp.arange(max_pos, dtype=jnp.float32)[:, None] * inv_freq[None, :]
            return (jnp.cos(ang), jnp.sin(ang))

        def apply_rope(x, cos, sin):
            x0 = x[..., 0::2]
            x1 = x[..., 1::2]
            c = cos[None, None, :, :]
            s = sin[None, None, :, :]
            r0 = x0 * c - x1 * s
            r1 = x0 * s + x1 * c
            return jnp.stack([r0, r1], axis=-1).reshape(x.shape)
        key = jax.random.key(seed)
        ks = jax.random.split(key, 5)
        sc = 1.0 / math.sqrt(C)
        return {'x': jax.random.normal(ks[0], (B, T, C), jnp.float32), 'Wq': jax.random.normal(ks[1], (C, C), jnp.float32) * sc, 'bq': jnp.zeros((C,), jnp.float32), 'Wk': jax.random.normal(ks[2], (C, C), jnp.float32) * sc, 'bk': jnp.zeros((C,), jnp.float32), 'Wv': jax.random.normal(ks[3], (C, C), jnp.float32) * sc, 'bv': jnp.zeros((C,), jnp.float32), 'Wp': jax.random.normal(ks[4], (C, C), jnp.float32) * sc, 'bp': jnp.zeros((C,), jnp.float32)}
    _L1_attn_all = _L1_attn_setup()
    _L1_attn_in = {k: v for k, v in _L1_attn_all.items() if k in ('Wq', 'bq', 'Wk', 'bk', 'Wv', 'bv', 'Wp', 'bp')}
    del _L1_attn_all

    def _L1_ffn_setup():
        import jax, jax.numpy as jnp
        import numpy as np
        B, S, D, H, F = (4, 1024, 256, 16, 1024)
        CAP = 0.125
        ROPE_BASE = 10000.0

        def rmsnorm(x, g):
            return x * jax.lax.rsqrt(jnp.mean(x * x, -1, keepdims=True) + 1e-06) * g

        def rope(t, pos):
            hd = t.shape[-1]
            inv = 1.0 / ROPE_BASE ** (jnp.arange(0, hd, 2, dtype=jnp.float32) / hd)
            f = pos[:, None, :, None].astype(jnp.float32) * inv
            emb = jnp.concatenate([f, f], axis=-1)
            cos, sin = (jnp.cos(emb), jnp.sin(emb))
            rot = jnp.concatenate([-t[..., hd // 2:], t[..., :hd // 2]], axis=-1)
            return t * cos + rot * sin
        key = jax.random.key(seed)
        ks = jax.random.split(key, 9)
        scale = 0.02
        x = jax.random.normal(ks[0], (B, S, D), jnp.float32)
        causal = jnp.where(jnp.tril(jnp.ones((S, S), bool)), 0.0, -1000000000.0).astype(jnp.float32)
        attention_mask = jnp.broadcast_to(causal[None, None], (B, 1, S, S))
        position_ids = jnp.broadcast_to(jnp.arange(S, dtype=jnp.int32), (B, S))
        return {'x': x, 'attention_mask': attention_mask, 'position_ids': position_ids, 'router_w': jax.random.normal(ks[1], (D, 1), jnp.float32) * scale, 'router_b': jnp.zeros((1,), jnp.float32), 'wq': jax.random.normal(ks[2], (D, D), jnp.float32) * scale, 'wk': jax.random.normal(ks[3], (D, D), jnp.float32) * scale, 'wv': jax.random.normal(ks[4], (D, D), jnp.float32) * scale, 'wo': jax.random.normal(ks[5], (D, D), jnp.float32) * scale, 'w1': jax.random.normal(ks[6], (D, F), jnp.float32) * scale, 'w2': jax.random.normal(ks[7], (F, D), jnp.float32) * scale, 'ln1': jnp.ones((D,), jnp.float32), 'ln2': jnp.ones((D,), jnp.float32)}
    _L1_ffn_all = _L1_ffn_setup()
    _L1_ffn_in = {k: v for k, v in _L1_ffn_all.items() if k in ('attention_mask', 'position_ids', 'router_w', 'router_b', 'wq', 'wk', 'wv', 'wo', 'w1', 'w2', 'ln1', 'ln2')}
    del _L1_ffn_all
    return {'x': x, 'L0_tok_ln1_g': _L0_tok_in['ln1_g'], 'L0_tok_ln1_b': _L0_tok_in['ln1_b'], 'L0_tok_W_proj': _L0_tok_in['W_proj'], 'L0_tok_b_proj': _L0_tok_in['b_proj'], 'L0_tok_ln2_g': _L0_tok_in['ln2_g'], 'L0_tok_ln2_b': _L0_tok_in['ln2_b'], 'L0_tok_cls_token': _L0_tok_in['cls_token'], 'L0_tok_pos_emb': _L0_tok_in['pos_emb'], 'L0_attn_wq': _L0_attn_in['wq'], 'L0_attn_bq': _L0_attn_in['bq'], 'L0_attn_wk': _L0_attn_in['wk'], 'L0_attn_bk': _L0_attn_in['bk'], 'L0_attn_wv': _L0_attn_in['wv'], 'L0_attn_bv': _L0_attn_in['bv'], 'L0_attn_wo': _L0_attn_in['wo'], 'L0_attn_bo': _L0_attn_in['bo'], 'L0_attn_wi1': _L0_attn_in['wi1'], 'L0_attn_bi1': _L0_attn_in['bi1'], 'L0_attn_wi2': _L0_attn_in['wi2'], 'L0_attn_bi2': _L0_attn_in['bi2'], 'L0_ffn_W1': _L0_ffn_in['W1'], 'L0_ffn_b1': _L0_ffn_in['b1'], 'L0_ffn_W2': _L0_ffn_in['W2'], 'L0_ffn_b2': _L0_ffn_in['b2'], 'L1_attn_Wq': _L1_attn_in['Wq'], 'L1_attn_bq': _L1_attn_in['bq'], 'L1_attn_Wk': _L1_attn_in['Wk'], 'L1_attn_bk': _L1_attn_in['bk'], 'L1_attn_Wv': _L1_attn_in['Wv'], 'L1_attn_bv': _L1_attn_in['bv'], 'L1_attn_Wp': _L1_attn_in['Wp'], 'L1_attn_bp': _L1_attn_in['bp'], 'L1_ffn_attention_mask': _L1_ffn_in['attention_mask'], 'L1_ffn_position_ids': _L1_ffn_in['position_ids'], 'L1_ffn_router_w': _L1_ffn_in['router_w'], 'L1_ffn_router_b': _L1_ffn_in['router_b'], 'L1_ffn_wq': _L1_ffn_in['wq'], 'L1_ffn_wk': _L1_ffn_in['wk'], 'L1_ffn_wv': _L1_ffn_in['wv'], 'L1_ffn_wo': _L1_ffn_in['wo'], 'L1_ffn_w1': _L1_ffn_in['w1'], 'L1_ffn_w2': _L1_ffn_in['w2'], 'L1_ffn_ln1': _L1_ffn_in['ln1'], 'L1_ffn_ln2': _L1_ffn_in['ln2']}

def reference(x, L0_tok_ln1_g, L0_tok_ln1_b, L0_tok_W_proj, L0_tok_b_proj, L0_tok_ln2_g, L0_tok_ln2_b, L0_tok_cls_token, L0_tok_pos_emb, L0_attn_wq, L0_attn_bq, L0_attn_wk, L0_attn_bk, L0_attn_wv, L0_attn_bv, L0_attn_wo, L0_attn_bo, L0_attn_wi1, L0_attn_bi1, L0_attn_wi2, L0_attn_bi2, L0_ffn_W1, L0_ffn_b1, L0_ffn_W2, L0_ffn_b2, L1_attn_Wq, L1_attn_bq, L1_attn_Wk, L1_attn_bk, L1_attn_Wv, L1_attn_bv, L1_attn_Wp, L1_attn_bp, L1_ffn_attention_mask, L1_ffn_position_ids, L1_ffn_router_w, L1_ffn_router_b, L1_ffn_wq, L1_ffn_wk, L1_ffn_wv, L1_ffn_wo, L1_ffn_w1, L1_ffn_w2, L1_ffn_ln1, L1_ffn_ln2):
    import jax
    import jax.numpy as jnp

    def _L0_tok_ref(x, ln1_g, ln1_b, W_proj, b_proj, ln2_g, ln2_b, cls_token, pos_emb):
        import jax, jax.numpy as jnp
        import numpy as np
        B, C, H, W = (64, 3, 96, 96)
        P = 16
        NP = H // P * (W // P)
        PD = C * P * P
        ED = 256
        NCLS = 1

        def _layernorm(x, g, b, eps=1e-05):
            mu = jnp.mean(x, axis=-1, keepdims=True)
            var = jnp.mean(jnp.square(x - mu), axis=-1, keepdims=True)
            return (x - mu) * jax.lax.rsqrt(var + eps) * g + b
        b = x.shape[0]
        h, w = (H // P, W // P)
        patches = x.reshape(b, C, h, P, w, P)
        patches = patches.transpose(0, 2, 4, 3, 5, 1).reshape(b, h * w, P * P * C)
        z = _layernorm(patches, ln1_g, ln1_b)
        z = jnp.einsum('bnp,pe->bne', z, W_proj) + b_proj
        z = _layernorm(z, ln2_g, ln2_b)
        cls = jnp.broadcast_to(cls_token, (b, NCLS, ED))
        z = jnp.concatenate([cls, z], axis=1)
        z = z + pos_emb
        return z

    def _L0_attn_ref(x, wq, bq, wk, bk, wv, bv, wo, bo, wi1, bi1, wi2, bi2):
        import jax, jax.numpy as jnp
        import numpy as np
        import math
        D_MODEL = 256
        N_HEADS = 16
        SPARSITY = 0.3
        B, S, D = x.shape
        H = N_HEADS
        hd = D // H
        k = max(1, int(S * SPARSITY))
        Q = (x @ wq.T + bq).reshape(B, S, H, hd).transpose(0, 2, 1, 3)
        K = (x @ wk.T + bk).reshape(B, S, H, hd).transpose(0, 2, 1, 3)
        V = (x @ wv.T + bv).reshape(B, S, H, hd).transpose(0, 2, 1, 3)
        h = jnp.maximum(x @ wi1.T + bi1, 0.0)
        importance = (h @ wi2.T + bi2)[..., 0]
        _, top_idx = jax.lax.top_k(importance, k)
        sparse_mask = jnp.zeros((B, S), dtype=x.dtype).at[jnp.arange(B)[:, None], top_idx].set(1.0)
        scores = jnp.einsum('bhqd,bhkd->bhqk', Q, K) / math.sqrt(hd)
        scores = jnp.where(sparse_mask[:, None, None, :] == 0, -jnp.inf, scores)
        attn = jax.nn.softmax(scores, axis=-1)
        out = jnp.einsum('bhqk,bhkd->bhqd', attn, V)
        out = out.transpose(0, 2, 1, 3).reshape(B, S, D)
        return out @ wo.T + bo

    def _L0_ffn_ref(x, W1, b1, W2, b2):
        import jax, jax.numpy as jnp
        import numpy as np
        EPS = 1e-05

        def _quantize(W):
            gamma = jnp.mean(jnp.abs(W))
            return jnp.clip(jnp.round(W / (gamma + EPS)), -1.0, 1.0)
        Wq1 = _quantize(W1)
        Wq2 = _quantize(W2)
        h = jax.nn.relu(jnp.einsum('bsd,fd->bsf', x, Wq1) + b1)
        out = jnp.einsum('bsf,df->bsd', h, Wq2) + b2
        return out

    def _L1_attn_ref(x, Wq, bq, Wk, bk, Wv, bv, Wp, bp):
        import jax, jax.numpy as jnp
        import numpy as np
        import math
        B, T, C, NH = (4, 512, 256, 16)
        HS = C // NH

        def rope_cache(dim, max_pos):
            half = dim // 2
            inv_freq = 1.0 / 10000.0 ** (jnp.arange(half, dtype=jnp.float32) * 2.0 / dim)
            ang = jnp.arange(max_pos, dtype=jnp.float32)[:, None] * inv_freq[None, :]
            return (jnp.cos(ang), jnp.sin(ang))

        def apply_rope(x, cos, sin):
            x0 = x[..., 0::2]
            x1 = x[..., 1::2]
            c = cos[None, None, :, :]
            s = sin[None, None, :, :]
            r0 = x0 * c - x1 * s
            r1 = x0 * s + x1 * c
            return jnp.stack([r0, r1], axis=-1).reshape(x.shape)
        Bx, Tx, Cx = x.shape

        def split_heads(y):
            return y.reshape(Bx, Tx, NH, HS).transpose(0, 2, 1, 3)
        q = split_heads(x @ Wq + bq)
        k = split_heads(x @ Wk + bk)
        v = split_heads(x @ Wv + bv)
        cos, sin = rope_cache(HS, Tx)
        q = apply_rope(q, cos, sin)
        k = apply_rope(k, cos, sin)
        att = jnp.einsum('bhqd,bhkd->bhqk', q, k) * (1.0 / math.sqrt(HS))
        causal = jnp.tril(jnp.ones((Tx, Tx), bool))
        att = jnp.where(causal[None, None, :, :], att, jnp.float32(-10000000000.0))
        att = jax.nn.softmax(att, axis=-1)
        y = jnp.einsum('bhqk,bhkd->bhqd', att, v)
        y = y.transpose(0, 2, 1, 3).reshape(Bx, Tx, Cx)
        return y @ Wp + bp

    def _L1_ffn_ref(x, attention_mask, position_ids, router_w, router_b, wq, wk, wv, wo, w1, w2, ln1, ln2):
        import jax, jax.numpy as jnp
        import numpy as np
        B, S, D, H, F = (4, 1024, 256, 16, 1024)
        CAP = 0.125
        ROPE_BASE = 10000.0

        def rmsnorm(x, g):
            return x * jax.lax.rsqrt(jnp.mean(x * x, -1, keepdims=True) + 1e-06) * g

        def rope(t, pos):
            hd = t.shape[-1]
            inv = 1.0 / ROPE_BASE ** (jnp.arange(0, hd, 2, dtype=jnp.float32) / hd)
            f = pos[:, None, :, None].astype(jnp.float32) * inv
            emb = jnp.concatenate([f, f], axis=-1)
            cos, sin = (jnp.cos(emb), jnp.sin(emb))
            rot = jnp.concatenate([-t[..., hd // 2:], t[..., :hd // 2]], axis=-1)
            return t * cos + rot * sin
        b, s, d = x.shape
        hd = d // H
        weights = (x @ router_w)[..., 0] + router_b[0]
        k = int(CAP * s)
        topv, topi = jax.lax.top_k(weights, k)
        thr = topv[:, -1]
        sel_mask = (weights > thr[:, None]).astype(x.dtype)
        kc = k - 1
        sel_idx = jnp.sort(topi[:, :kc], axis=1)
        bidx = jnp.arange(b)[:, None]
        x_sel = x[bidx, sel_idx]
        pos_sel = position_ids[bidx, sel_idx]
        w_sel = weights[bidx, sel_idx]
        m = attention_mask[:, 0]
        m_sel = m[bidx[:, :, None], sel_idx[:, :, None], sel_idx[:, None, :]]
        hn = rmsnorm(x_sel, ln1)

        def heads(t):
            return t.reshape(b, kc, H, hd).transpose(0, 2, 1, 3)
        q = rope(heads(hn @ wq), pos_sel)
        kk = rope(heads(hn @ wk), pos_sel)
        v = heads(hn @ wv)
        sc = jnp.einsum('bhqd,bhkd->bhqk', q, kk) / np.sqrt(hd).astype(np.float32)
        sc = sc + m_sel[:, None]
        a = jax.nn.softmax(sc, axis=-1)
        o = jnp.einsum('bhqk,bhkd->bhqd', a, v).transpose(0, 2, 1, 3).reshape(b, kc, d) @ wo
        x1 = x_sel + o
        x2 = x1 + jax.nn.gelu(rmsnorm(x1, ln2) @ w1) @ w2
        proc = x2 * w_sel[..., None]
        out = jnp.zeros_like(x).at[bidx, sel_idx].set(proc)
        return out + x * (1.0 - sel_mask)[..., None]
    h = _L0_tok_ref(x, L0_tok_ln1_g, L0_tok_ln1_b, L0_tok_W_proj, L0_tok_b_proj, L0_tok_ln2_g, L0_tok_ln2_b, L0_tok_cls_token, L0_tok_pos_emb)
    h = h + _L0_attn_ref(_layernorm(h, axis=-1), L0_attn_wq, L0_attn_bq, L0_attn_wk, L0_attn_bk, L0_attn_wv, L0_attn_bv, L0_attn_wo, L0_attn_bo, L0_attn_wi1, L0_attn_bi1, L0_attn_wi2, L0_attn_bi2)
    h = h + _L0_ffn_ref(_layernorm(h, axis=-1), L0_ffn_W1, L0_ffn_b1, L0_ffn_W2, L0_ffn_b2)
    h = h + _L1_attn_ref(_layernorm(h, axis=-1), L1_attn_Wq, L1_attn_bq, L1_attn_Wk, L1_attn_bk, L1_attn_Wv, L1_attn_bv, L1_attn_Wp, L1_attn_bp)
    h = h + _L1_ffn_ref(_layernorm(h, axis=-1), L1_ffn_attention_mask, L1_ffn_position_ids, L1_ffn_router_w, L1_ffn_router_b, L1_ffn_wq, L1_ffn_wk, L1_ffn_wv, L1_ffn_wo, L1_ffn_w1, L1_ffn_w2, L1_ffn_ln1, L1_ffn_ln2)
    return h

_drawn_inputs = setup_inputs


def setup_inputs(seed=0):
    import zlib

    import numpy as np

    out = dict(_drawn_inputs(seed))
    spreads = {'L0_tok_ln1_g': (1.0, 0.2),
     'L0_tok_ln1_b': (0.0, 0.1),
     'L0_tok_b_proj': (0.0, 0.1),
     'L0_tok_ln2_g': (1.0, 0.2),
     'L0_tok_ln2_b': (0.0, 0.1),
     'L0_attn_bq': (0.0, 0.8),
     'L0_attn_bk': (0.0, 2.0),
     'L0_attn_bv': (0.0, 0.404),
     'L0_attn_bo': (0.0, 0.1),
     'L0_attn_bi1': (0.0, 0.651),
     'L1_attn_bq': (0.0, 0.8),
     'L1_attn_bk': (0.0, 0.8),
     'L1_attn_bv': (0.0, 2.0),
     'L1_attn_bp': (0.0, 2.0),
     'L1_ffn_ln1': (1.0, 0.6),
     'L1_ffn_ln2': (1.0, 0.6)}
    factors = {'L0_attn_wq': 8.0,
     'L0_attn_wk': 8.0,
     'L0_attn_wi1': 2.686,
     'L0_ffn_b1': 8.0,
     'L0_ffn_b2': 200.0,
     'L1_attn_Wq': 8.0,
     'L1_attn_Wk': 8.0,
     'L1_attn_Wv': 8.0,
     'L1_attn_Wp': 8.0,
     'L1_ffn_router_w': 8.0,
     'L1_ffn_wq': 8.0,
     'L1_ffn_wk': 8.0,
     'L1_ffn_wv': 8.0,
     'L1_ffn_wo': 8.0,
     'L1_ffn_w1': 8.0,
     'L1_ffn_w2': 8.0}
    for name, (base, spread) in spreads.items():
        noise = np.random.default_rng([zlib.crc32(name.encode()), seed]).standard_normal(out[name].shape)
        drawn = base * np.exp(spread * noise) if base else spread * noise
        out[name] = jnp.asarray(drawn.astype(out[name].dtype))
    for name, factor in factors.items():
        out[name] = (out[name] * factor).astype(out[name].dtype)
    return out
```

```python
from contextlib import ExitStack

import numpy as np

import concourse.bass as bass
from concourse import mybir

F32 = mybir.dt.float32
F32R = mybir.dt.float32r
BF16 = mybir.dt.bfloat16
I32 = mybir.dt.int32
ALU = mybir.AluOpType
ACT = mybir.ActivationFunctionType
AX = mybir.AxisListType

IMAGES, S, D, H, HD = 32, 37, 256, 16, 16
PATCHES, PD = 36, 768
IM = 3
R = IM * S
RP = R + 1
T = -(-IMAGES // IM)
ROWS = IMAGES * S
R_LAST = ROWS - (T - 1) * R
DC = D // 128
PC = PD // 128
HC = H // DC
K0 = max(1, int(S * 0.3))
KK = IM * K0
F = 4 * D
FC = F // 128
PAIRS = H // 2
KSEL = int(0.125 * S)
NSEL = KSEL - 1
W3 = IMAGES * NSEL
MB = 4
XA = D + 2 + S
SCALE = 1.0 / HD ** 0.5
LN_EPS = 1e-5
RMS_EPS = 1e-6
FAR = -1e30
CAUSAL = -1e10

_at = {}
_n = 0
for _name, _w in (("ident", 128), ("same", R), ("tok", S), ("before", S), ("slot0", KK),
                  ("slot1", 2 * W3 + 3), ("notcls", 1), ("iscls", 1), ("other0", KK),
                  ("causal", S), ("head", HC), ("pair0", 2), ("pair1", 2), ("cos", HD),
                  ("sin", HD), ("inv", HD), ("sign", HD), ("other1", W3)):
    _at[_name] = (_n, _w)
    _n += _w
N_CONST = _n
_vat = {}
_n = 0
for _name, _w in (("ln1_g", PC), ("ln1_b", PC), ("bq", DC), ("bk", DC), ("bi1", 1), ("wi2", 1),
                  ("bi2", 1), ("router_b", 1), ("part1", 1), ("part2", 1)):
    _vat[_name] = (_n, _w)
    _n += _w
N_VEC = _n
_rat = {}
_n = 0
for _name in ("b_proj", "ln2_g", "ln2_b", "cls", "bv", "bo", "b2", "bp", "router_w", "ln1", "ln2"):
    _rat[_name] = (_n, D)
    _n += D
N_ROW = _n
B1_AT, BQKV_AT = 0, F
N_ROWS = F + 3 * D


def shape_constants():
    c = np.zeros((128, N_CONST), np.float32)

    def put(name, a):
        at, w = _at[name]
        a = np.asarray(a, np.float32)
        c[:a.shape[0], at:at + w] = a

    p = np.arange(128)
    r = np.arange(R)
    im, tok = r // S, r % S
    put("ident", np.eye(128))
    put("same", im[:, None] == im[None, :])
    put("tok", tok[:, None] == np.arange(S))
    put("before", np.arange(S) < tok[:, None])
    k = np.arange(KK)
    put("slot0", np.where(im[:, None] == k // K0, k % K0, -1))
    put("other0", np.where(im[:, None] == k // K0, 0.0, FAR))
    g = np.arange(2 * W3 + 3) - (T - 1) * IM * NSEL
    put("slot1", np.where(im[:, None] == g // NSEL, g % NSEL, -1))
    put("notcls", (tok != 0)[:, None])
    put("iscls", (tok == 0)[:, None])
    put("causal", np.where(np.arange(S) <= tok[:, None], 0.0, CAUSAL))
    put("head", (p[:, None] % 128) // HD == np.arange(HC))
    put("pair0", (p[:2 * KK, None] // KK) == np.arange(2))
    put("pair1", (p[:2 * S, None] // S) == np.arange(2))
    half = HD // 2
    inv = (1.0 / np.float32(10000.0) ** (np.arange(half, dtype=np.float32) * np.float32(2.0 / HD))).astype(np.float32)
    ang = (tok.astype(np.float32)[:, None] * inv[None, :]).astype(np.float32)
    put("cos", np.repeat(np.cos(ang), 2, axis=1))
    put("sin", (np.sin(ang)[:, :, None] * np.array([-1.0, 1.0])).reshape(R, HD))
    put("inv", np.tile(np.concatenate([inv, inv]), (128, 1)))
    put("sign", np.tile(np.concatenate([-np.ones(half), np.ones(half)]), (128, 1)))
    w = np.arange(W3)
    put("other1", np.where(w[:, None] // NSEL == w // NSEL, 0.0, FAR))
    return c


def vit_tower(nc, patches, W_proj, consts, vectors, rows, wide_rows, pos3, wqT, wkT, wvT, woT, wi1T,
              W1T, W2T, wqkv1, wp1, mask, positions, wqkv2, wo2, w1f, w2f, out):
    with ExitStack() as ctx:
        def sb(name, shape, dt=F32):
            return ctx.enter_context(nc.sbuf_tensor(name, shape, dt))

        def sem(name):
            return ctx.enter_context(nc.semaphore(name))

        ps = ctx.enter_context(nc.psum_tensor("ps", [128, 8, 512], F32))

        cst = sb("cst", [128, N_CONST])
        vec = sb("vec", [128, N_VEC])
        row = sb("row", [128, N_ROW])
        pos = sb("pos", [R, D])
        early = sb("early", [128, PC * D + 4 * DC * D])
        wi1 = sb("wi1", [128, DC, 128])
        wide = sb("wide", [128, 2 * FC * D])
        w1q = sb("w1q", [128, DC, F], F32R)
        w2q = sb("w2q", [128, FC, D], F32R)
        wqkv = sb("wqkv", [128, DC, 3 * D])
        wp = sb("wp", [128, DC, D])
        wqkv_l = sb("wqkv_l", [128, DC, 3 * D])
        wo_l = sb("wo_l", [128, DC, D])
        maskrow = sb("maskrow", [R, 2, S])
        posi = sb("posi", [R, 2, 1], I32)

        ident_b = sb("ident_b", [R, R], BF16)
        other_b = sb("other_b", [R, KK], BF16)
        causal_b = sb("causal_b", [R, S], BF16)
        ones = sb("ones", [128, 128])
        ones_b = sb("ones_b", [3, 128], BF16)
        mhalf = sb("mhalf", [128, 1])
        bp0 = sb("bp0", [R, D])
        posb = sb("posb", [R, D])
        brow = sb("brow", [3, N_ROWS], BF16)
        gam = sb("gam", [128, 8])

        h = sb("h", [R, T, D])
        xa = sb("xa", [R, T, XA])
        xT = sb("xT", [128, T, DC, RP])
        q6 = sb("q6", [128, T, DC, RP])
        v1 = sb("v1", [R, T, D])
        ohT = sb("ohT", [W3, T, RP])
        st = sb("st", [R, T, 12])
        mv = sb("mv", [R, T, 2])
        rs = sb("rs", [R, T, 2])
        xhi = sb("xhi", [128, 2, DC, RP], F32R)
        xlo = sb("xlo", [128, 2, DC, RP], F32R)
        hhi = sb("hhi", [128, 2, FC, RP], F32R)
        hlo = sb("hlo", [128, 2, FC, RP], F32R)

        A_SIZE, B_SIZE = 6608, 3664
        arena_a = sb("arena_a", [128, A_SIZE])
        arena_b = sb("arena_b", [128, B_SIZE])

        def cut(whole, at, shape):
            n = int(np.prod(shape[1:]))
            ap = whole[0:shape[0], at[0]:at[0] + n]
            at[0] += n
            assert at[0] <= whole.shape[1], (at, whole.shape)
            if len(shape) == 2:
                return ap
            names = "abcd"[:len(shape) - 1]
            sizes = {x: v for x, v in zip(names, shape[1:])}
            return ap.rearrange(f"p ({' '.join(names)}) -> p {' '.join(names)}", **sizes)

        at = [0]
        w_proj = cut(early, at, [128, PC, D])
        wq0, wk0, wv0, wo0 = (cut(early, at, [128, DC, D]) for _ in range(4))
        kbd7 = cut(early, [0], [128, 2, DC, IM * HC * S])
        at = [0]
        w1raw = cut(wide, at, [128, DC, F])
        w2raw = cut(wide, at, [128, FC, D])
        at = [0]
        vm7 = cut(wide, at, [2 * S, 3, IM * D])
        PT7 = cut(wide, at, [2 * S, 2, PAIRS, RP])
        at = [0]
        pat = cut(arena_a, at, [R, 3, PD])
        pT = cut(arena_a, at, [128, 2, PC, RP])
        zb = cut(arena_a, at, [R, 2, D])
        zn = cut(arena_a, at, [R, 2, D])
        at = [0]
        qT0 = cut(arena_a, at, [128, 2, DC, RP])
        kbd0 = cut(arena_a, at, [128, 2, DC, HC * KK])
        vt = cut(arena_a, at, [2 * KK, 2, D])
        vm0 = cut(arena_a, at, [2 * KK, 3, D])
        pr0 = cut(arena_a, at, [R, 3, H * KK])
        PT0 = cut(arena_a, at, [2 * KK, 2, PAIRS, RP])
        oT0 = cut(arena_a, at, [128, 2, DC, RP])
        sm0 = sb("sm0", [R, 2, 3, H])
        at = [0]
        xT6 = cut(arena_a, at, [128, 2, DC, RP])
        rot = cut(arena_a, at, [R, 2, 2, 2 * D])
        at = [0]
        hT = cut(arena_b, at, [128, 2, RP])
        rk0 = cut(arena_b, at, [R, 2, 8 + 4 * S])
        oh0 = cut(arena_b, at, [R, 2, KK])
        xsT = cut(arena_b, at, [128, T, DC, 2 * KK])
        at = [0]
        qTm = cut(arena_b, at, [128, 2, DC, IM, RP])
        pr7 = cut(arena_b, at, [R, 3, H * S])
        oT7 = cut(arena_b, at, [128, 2, DC, RP])
        sm7 = cut(arena_b, at, [R, 2, 3, H])

        names = """cst vec row pos wproj w0 w1raw w2raw wl1 mrow w2nd wlast brows stored
            pool_set cast posb biasps bp0 gw absum gamps thr low quant parts
            st1 rs1 xh1 tr1 xT1 pj z rs2 zn h0
            ln_stats ln_scale xn hb T2 xT2 hidp hid imp vE G rank gx xs
            q kv q0 kb0 vt vm0 S0 smx0 ex0 sum0 pn0 pt0 PT0 pv0 oT0 op0 h4
            T5 xhi xlo w1a w1b hia hib loa lob w2 h5
            T6 xT6 qkv rope rope_sum v6 tq tqe tke qz
            qm7 kbA kbB vm7 S7 smx7 ex7 sum7 pn7 pt7 PT7 pv7 oT7 op7 h7
            rw G9 rank9 acc oht ohte base aug
            tv sc fin t_ang t_sin t_hn t_T t_hnT t_mrow t_mm t_qkv t_v t_rot t_Tr t_qkT t_kbd t_S t_sub
            t_exp t_pT t_PT t_O t_o t_To t_oT t_wo t_w1 t_g t_w2 t_y t_put""".split()
        s = {n: sem(n) for n in names}
        s_pat = [sem(f"pat{i}") for i in range(3)]
        s_vrep = [sem(f"vrep{i}") for i in range(3)]
        N_ST1, N_RS1, N_Z, N_RS2, N_H0, N_LNA, N_LNR, N_VE, N_RANK, N_SUM, N_RW, N_RANK9 = \
            3, 2, 3, 3, 2, 2, 2, 2, 5, 2, 3, 8

        def C(name, rows=128):
            a, w = _at[name]
            return cst[0:rows, a:a + w]

        def V(name):
            a, w = _vat[name]
            return vec[:, a:a + w]

        def B(name, rows=R):
            a, w = _rat[name]
            return row[0:rows, a:a + w]

        def spread(ap, axis, shape):
            return ap.unsqueeze(axis).broadcast_to(shape)

        def link(eng, name, start):
            n = [start]

            def f(ins, wait=True):
                n[0] += 1
                ins.then_inc(s[name], 1)
                if wait:
                    eng.wait_ge(s[name], n[0])
            return f

        def sweep(*steps):
            for it in range(T + max(lag for _, lag in steps)):
                for step, lag in steps:
                    if 0 <= it - lag < T:
                        step(it - lag)

        at = [0]
        t_x = cut(arena_a, at, [W3, XA])
        t_hn = cut(arena_a, at, [W3, D])
        t_hnT = cut(arena_a, at, [128, DC, W3])
        t_rot = cut(arena_a, at, [W3, 2, 2 * D])
        t_v = cut(arena_a, at, [W3, D])
        t_kbd = cut(arena_a, at, [128, DC, HC * W3])
        t_g = cut(arena_a, at, [128, FC, W3])
        t_cmp = cut(arena_a, at, [S, 2 * W3])
        junk = cut(arena_a, at, [R, D])
        rk9 = cut(arena_a, at, [R, 2, 12 + 4 * S])
        oh9 = cut(arena_a, at, [R, 2, W3])
        at = [0]
        t_p = cut(arena_b, at, [W3, H * W3])
        t_PT = cut(arena_b, at, [W3, H * W3])
        at = [0]
        xTflat = xT[:].rearrange("p t c r -> p (t c r)")
        t_qkT = cut(xTflat, at, [128, 4, W3])
        t_oT = cut(xTflat, at, [128, DC, W3])
        t_sc = cut(xTflat, at, [W3, 16])
        t_f = cut(xTflat, at, [W3, 6, HD])
        t_mm = cut(xTflat, at, [W3, W3])
        t_mx = cut(xTflat, at, [W3, 3, H])
        t_o = cut(xTflat, at, [W3, D])
        t_x1 = cut(xTflat, at, [W3, D])
        t_y = cut(xTflat, at, [W3, D])

        bias_rows = cut(q6[:].rearrange("p t c r -> p (t c r)"), [0], [3, N_ROWS])
        bias_part = cut(v1[:].rearrange("p t d -> p (t d)"), [0], [3, N_ROWS])
        gW = cut(xTflat, [0], [128, PC, D])
        low = cut(arena_a, [0], [128, 2, 2 * F])

        block = ctx.enter_context(nc.Block())

        @block.sync
        def _(sp):
            def load(dst, src, on):
                sp.dma_start(dst, src).then_inc(on, 16)

            def matrix(dst, src, on):
                load(dst, src.rearrange("(c p) n -> p c n", p=128), s[on])

            def patch(t):
                if t >= 3:
                    sp.wait_ge(s["tr1"], t - 2)
                load(pat[:, t % 3, :], patches[t * R:(t + 1) * R, :], s_pat[t % 3])

            patch(0)
            load(cst[:], consts, s["cst"])
            load(vec[:], vectors, s["vec"])
            matrix(w_proj, W_proj, "wproj")
            patch(1)
            load(row[:], rows[0, :].partition_broadcast(128), s["row"])
            load(pos[:], pos3, s["pos"])
            patch(2)
            matrix(w1raw, W1T, "w1raw")
            matrix(w2raw, W2T, "w2raw")
            matrix(wi1[:], wi1T, "w0")
            for dst, src in ((wq0, wqT), (wk0, wkT), (wv0, wvT), (wo0, woT)):
                matrix(dst, src, "w0")
            load(bias_rows, wide_rows[0, :].partition_broadcast(3), s["brows"])
            for t in range(3, T):
                patch(t)
            matrix(wqkv[:], wqkv1, "wl1")
            matrix(wp[:], wp1, "wl1")
            for i in range(IM):
                a = slice(i * S, (i + 1) * S)
                for n, batch in ((0, i), (1, MB - 1)):
                    load(maskrow[a, n, :], mask[batch, 0, 0:S, 0:S], s["mrow"])
                    load(posi[a, n, :], positions[batch, 0:S].rearrange("(s a) -> s a", a=1), s["mrow"])
            matrix(wqkv_l[:], wqkv2, "w2nd")
            matrix(wo_l[:], wo2, "w2nd")
            for t in range(T):
                sp.wait_ge(s["v6"], t + 1)
                if t >= 3:
                    sp.wait_ge(s["pv7"], t - 2)
                else:
                    sp.wait_ge(s["quant"], 2)
                for i in range(IM):
                    for j in range(2):
                        load(vm7[j * S:(j + 1) * S, t % 3, i * D:(i + 1) * D],
                             v1[i * S:(i + 1) * S, t, :], s_vrep[t % 3])
            sp.wait_ge(s["pv7"], T)
            matrix(w1raw, w1f, "wlast")
            matrix(w2raw, w2f, "wlast")
            for t in range(T):
                n = R if t < T - 1 else R_LAST
                sp.wait_ge(s["fin"], t + 1)
                load(out[t * R:t * R + n, :], h[0:n, t, :], s["stored"])
            sp.wait_ge(s["stored"], 16 * T)

        @block.gpsimd
        def _(pool):
            g = nc.gpsimd

            def rsqrt(k, on, n_on, name, n_name, mask_cls=False):
                pool.wait_ge(s[on], n_on * (k + 1))
                l = link(pool, name, n_name * k)
                t = k % T
                l(g.tensor_scalar(rs[:, t, 0:1], mv[:, t, 1:2], LN_EPS, None, ALU.add))
                l(g.tensor_tensor(rs[:, t, 1:2], rs[:, t, 0:1], mhalf[0:R, :], ALU.pow), mask_cls)
                if mask_cls:
                    l(g.tensor_scalar(rs[:, t, 1:2], rs[:, t, 1:2], C("notcls", R), None, ALU.mult), False)

            def add_bias(t, layer, name):
                pool.wait_ge(s["xn"], layer * T + t + 1)
                g.tensor_tensor(h[:, t, :], h[:, t, :], B(name), ALU.add).then_inc(s["hb"], 1)

            def pairs_apart(dst, src, name, rows_n, n, sem_name):
                g.tensor_tensor(dst.rearrange("p (n j d) -> p n j d", j=2, d=HD),
                                src.rearrange("p (n j d) -> p n j d", j=2, d=HD),
                                C(name, rows_n).unsqueeze(1).unsqueeze(3).broadcast_to([rows_n, n, 2, HD]),
                                ALU.mult).then_inc(s[sem_name], 1)

            g.memset(mhalf[:], -0.5).then_inc(s["pool_set"], 1)
            g.memset(ones[:], 1.0).then_inc(s["pool_set"], 1)
            g.memset(ones_b[:], 1.0).then_inc(s["pool_set"], 1)
            g.memset(xhi[:, :, :, R:RP].bitcast(F32), 0.0).then_inc(s["pool_set"], 1)
            g.memset(xlo[:, :, :, R:RP].bitcast(F32), 0.0).then_inc(s["pool_set"], 1)
            pool.wait_ge(s["pool_set"], 5)
            pool.wait_ge(s["cst"], 16)
            g.tensor_copy(ident_b[:], C("ident", R)[:, 0:R]).then_inc(s["cast"], 1)
            g.tensor_copy(other_b[:], C("other0", R)).then_inc(s["cast"], 1)
            g.tensor_copy(causal_b[:], C("causal", R)).then_inc(s["cast"], 1)

            def h0(t):
                if t == 0:
                    pool.wait_ge(s["row"], 16)
                    pool.wait_ge(s["pos"], 16)
                    l = link(pool, "posb", 0)
                    l(g.tensor_scalar(posb[:], B("ln2_b"), C("notcls", R), None, ALU.mult), False)
                    l(g.tensor_scalar(B("cls"), B("cls"), C("iscls", R), None, ALU.mult))
                    l(g.tensor_tensor(posb[:], posb[:], pos[:], ALU.add))
                    l(g.tensor_tensor(posb[:], posb[:], B("cls"), ALU.add))
                pool.wait_ge(s["zn"], t + 1)
                l = link(pool, "h0", N_H0 * t)
                l(g.tensor_tensor(zn[:, t % 2, :], zn[:, t % 2, :], B("ln2_g"), ALU.mult))
                l(g.tensor_tensor(h[:, t, :], zn[:, t % 2, :], posb[:], ALU.add), False)

            sweep((lambda t: rsqrt(t, "st1", N_ST1, "rs1", N_RS1), 0),
                  (lambda t: rsqrt(t, "z", N_Z, "rs2", N_RS2, True), 2), (h0, 3))

            def setup(t):
                if t in (1, 2):
                    pool.wait_ge(s["thr"], 2)
                    for n in range(2):
                        half = slice(n * F, (n + 1) * F)
                        g.tensor_scalar(low[:, t - 1, half], wide[:, (t - 1) * 2 * F:t * 2 * F][:, half],
                                        gam[:, 5 + t:6 + t], None, ALU.is_lt).then_inc(s["low"], 1)
                if t == 3:
                    pool.wait_ge(s["brows"], 16)
                    l = link(pool, "parts", 0)
                    for i in range(2):
                        l(g.tensor_copy(brow[:], bias_rows))
                        l(g.tensor_scalar(bias_part, brow[:], V(f"part{i + 1}")[0:3, :], None, ALU.mult))
                        l(g.tensor_tensor(bias_rows, bias_rows, bias_part, ALU.subtract))
                    l(g.tensor_copy(brow[:], bias_rows), False)

            sweep((lambda t: rsqrt(t, "ln_stats", N_LNA, "ln_scale", N_LNR), 0),
                  (lambda t: add_bias(t, 0, "bo"), 1), (setup, 2))

            def vm0_(t):
                pool.wait_ge(s["vt"], t + 1)
                if t >= 3:
                    pool.wait_ge(s["pv0"], t - 2)
                pairs_apart(vm0[:, t % 3, :], vt[:, t % 2, :], "pair0", 2 * KK, PAIRS, "vm0")

            def pn0(t):
                pool.wait_ge(s["sum0"], N_SUM * (t + 1))
                p3 = pr0[:, t % 3, :].rearrange("p (n k) -> p n k", k=KK)
                g.tensor_tensor(p3, p3, spread(sm0[:, t % 2, 2, :], 2, [R, H, KK]), ALU.mult).then_inc(s["pn0"], 1)

            sweep((pn0, 2), (vm0_, 0))

            pool.wait_ge(s["mrow"], 16 * 4 * IM)
            for a, b, n in ((0, 1, 0), (1, T, 1)):
                g.tensor_copy(xa[:, a:b, D + 1:D + 2], posi[:, n:n + 1, :].broadcast_to([R, b - a, 1])).then_inc(s["aug"], 1)
                g.tensor_copy(xa[:, a:b, D + 2:XA], maskrow[:, n:n + 1, :].broadcast_to([R, b - a, S])).then_inc(s["aug"], 1)

            sweep((lambda t: rsqrt(t + 1 * T, "ln_stats", N_LNA, "ln_scale", N_LNR), 0),
                  (lambda t: add_bias(t, 1, "b2"), 1))

            g.memset(qTm[:], 0.0).then_inc(s["qz"], 1)

            def rope_sum(t):
                pool.wait_ge(s["rope"], 2 * (t + 1))
                g.tensor_tensor(rot[:, t % 2, 0, :], rot[:, t % 2, 0, :], rot[:, t % 2, 1, :],
                                ALU.add).then_inc(s["rope_sum"], 1)

            sweep((lambda t: rsqrt(t + 2 * T, "ln_stats", N_LNA, "ln_scale", N_LNR), 0),
                  (lambda t: add_bias(t, 2, "bp"), 1), (rope_sum, 2))

            def kbA(t):
                pool.wait_ge(s["tke"], T)
                if t >= 2:
                    pool.wait_ge(s["S7"], t - 1)
                g.tensor_tensor(kbd7[:, t % 2, 0, :].rearrange("p (i n k) -> p i n k", i=IM, n=HC),
                                xT[:, t, 0, 0:R].rearrange("p (i k) -> p i k", i=IM).unsqueeze(2).broadcast_to([128, IM, HC, S]),
                                C("head").unsqueeze(1).unsqueeze(3).broadcast_to([128, IM, HC, S]),
                                ALU.mult).then_inc(s["kbA"], 1)

            def vm7_(t):
                pool.wait_ge(s_vrep[t % 3], 16 * 2 * IM * (t // 3 + 1))
                pairs_apart(vm7[:, t % 3, :], vm7[:, t % 3, :], "pair1", 2 * S, IM * PAIRS, "vm7")

            def pn7(t):
                pool.wait_ge(s["sum7"], N_SUM * (t + 1))
                p3 = pr7[:, t % 3, :].rearrange("p (n k) -> p n k", k=S)
                g.tensor_tensor(p3, p3, spread(sm7[:, t % 2, 2, :], 2, [R, H, S]), ALU.mult).then_inc(s["pn7"], 1)

            sweep((kbA, 0), (vm7_, 1), (pn7, 2))

            sweep((lambda t: rsqrt(t + 3 * T, "ln_stats", N_LNA, "ln_scale", N_LNR), 0),)
            for i in range(2):
                pool.wait_ge(s["sc"], 1 + 3 * i)
                g.tensor_scalar(t_sc[:, 2 + 4 * i:3 + 4 * i], t_sc[:, 1 + 4 * i:2 + 4 * i], 1.0 / D, RMS_EPS,
                                ALU.mult, ALU.add).then_inc(s["sc"], 1)
                pool.wait_ge(s["sc"], 2 + 3 * i)
                g.tensor_tensor(t_sc[:, 3 + 4 * i:4 + 4 * i], t_sc[:, 2 + 4 * i:3 + 4 * i], mhalf[0:W3, :],
                                ALU.pow).then_inc(s["sc"], 1)

        @block.vector
        def _(dve):
            v = nc.vector

            def norm_stats(t, layer, on, n_on):
                dve.wait_ge(s[on], n_on * (t + 1))
                l = link(dve, "ln_stats", N_LNA * (layer * T + t))
                l(v.bn_stats(st[:, t, 0:6], h[:, t, :]))
                l(v.bn_aggr(mv[:, t, :], st[:, t, 0:6]), False)

            def norm(t, layer):
                dve.wait_ge(s["ln_scale"], N_LNR * (layer * T + t + 1))
                v.tensor_scalar(xa[:, t, 0:D], h[:, t, :], mv[:, t, 0:1], rs[:, t, 1:2],
                                ALU.subtract, ALU.mult).then_inc(s["xn"], 1)

            def ranks(l, rk, G):
                l(v.tensor_tensor_reduce(rk[:, 119:119 + S], G, C("tok", R), 1.0, 0.0, ALU.mult, ALU.add,
                                         rk[:, 1:2]))
                l(v.tensor_scalar(rk[:, 45:45 + S], G, rk[:, 1:2], None, ALU.is_gt), False)
                l(v.scalar_tensor_tensor(rk[:, 82:82 + S], G, rk[:, 1:2], C("before", R), ALU.is_equal, ALU.mult))
                l(v.tensor_tensor_reduce(rk[:, 119:119 + S], rk[:, 45:45 + S], rk[:, 82:82 + S], 1.0, 0.0,
                                         ALU.add, ALU.add, rk[:, 2:3]))

            def n1(t):
                dve.wait_ge(s_pat[t % 3], 16 * (t // 3 + 1))
                l = link(dve, "st1", N_ST1 * t)
                l(v.bn_stats(st[:, t, 0:6], pat[:, t % 3, 0:PD // 2]), False)
                l(v.bn_stats(st[:, t, 6:12], pat[:, t % 3, PD // 2:PD]))
                l(v.bn_aggr(mv[:, t, :], st[:, t, :]), False)

            def x1(t):
                dve.wait_ge(s["rs1"], N_RS1 * (t + 1))
                v.tensor_scalar(pat[:, t % 3, :], pat[:, t % 3, :], mv[:, t, 0:1], rs[:, t, 1:2],
                                ALU.subtract, ALU.mult).then_inc(s["xh1"], 1)

            def z(t):
                if t == 0:
                    dve.wait_ge(s["biasps"], 1)
                    dve.wait_ge(s["row"], 16)
                    v.tensor_tensor(bp0[:], ps[0:R, 4, 0:D], B("b_proj"), ALU.add).then_inc(s["bp0"], 1)
                    dve.wait_ge(s["bp0"], 1)
                dve.wait_ge(s["pj"], t + 1)
                if t >= 2:
                    dve.wait_ge(s["zn"], t - 1)
                l = link(dve, "z", N_Z * t)
                l(v.tensor_tensor(zb[:, t % 2, :], ps[0:R, 2 + t % 2, 0:D], bp0[:], ALU.add))
                l(v.bn_stats(st[:, t, 0:6], zb[:, t % 2, :]))
                l(v.bn_aggr(mv[:, t, :], st[:, t, 0:6]), False)

            def zn_(t):
                dve.wait_ge(s["rs2"], N_RS2 * (t + 1))
                if t >= 2:
                    dve.wait_ge(s["h0"], N_H0 * (t - 1))
                v.tensor_scalar(zn[:, t % 2, :], zb[:, t % 2, :], mv[:, t, 0:1], rs[:, t, 1:2],
                                ALU.subtract, ALU.mult).then_inc(s["zn"], 1)

            def absum(t):
                if t in (4, 5):
                    n = t - 4
                    dve.wait_ge(s[("w1raw", "w2raw")[n]], 16)
                    v.tensor_reduce(gam[:, n:n + 1], wide[:, n * 2 * F:(n + 1) * 2 * F], AX.X, ALU.add,
                                    apply_absolute_value=True).then_inc(s["absum"], 1)

            sweep((n1, 0), (x1, 1), (z, 2), (zn_, 3), (absum, 0))

            def vE(t):
                dve.wait_ge(s["imp"], t + 1)
                rk = rk0[:, t % 2, :]
                l = link(dve, "vE", N_VE * t)
                l(v.tensor_scalar(rk[:, 0:1], ps[0:R, 6, 2 * (t % 2):2 * (t % 2) + 1], V("bi2")[0:R, :],
                                  None, ALU.add))
                l(v.tensor_scalar(rk[:, 8:8 + S], C("tok", R), rk[:, 0:1], None, ALU.mult), False)

            def rank(t):
                dve.wait_ge(s["G"], t + 1)
                rk = rk0[:, t % 2, :]
                l = link(dve, "rank", N_RANK * t)
                ranks(l, rk, ps[0:R, 2, 0:S])
                if t >= 2:
                    dve.wait_ge(s["gx"], t - 1)
                l(v.tensor_scalar(oh0[:, t % 2, :], C("slot0", R), rk[:, 2:3], None, ALU.is_equal), False)

            def quantize(t):
                if t == 0:
                    dve.wait_ge(s["gamps"], 1)
                    l = link(dve, "thr", 0)
                    l(v.tensor_scalar(gam[:, 4:6], ps[:, 7, 508:510], 0.5 / (D * F), 0.5e-5, ALU.mult, ALU.add))
                    l(v.tensor_scalar(gam[:, 6:8], gam[:, 4:6], -1.0, None, ALU.mult), False)
                if t in (3, 5):
                    n = (t - 3) // 2
                    dve.wait_ge(s["low"], 2 * (n + 1))
                    dst = (w1q, w2q)[n]
                    v.scalar_tensor_tensor(dst[:].rearrange("p c n -> p (c n)"), wide[:, n * 2 * F:(n + 1) * 2 * F],
                                           gam[:, 4 + n:5 + n], low[:, n, :], ALU.is_gt, ALU.subtract
                                           ).then_inc(s["quant"], 1)

            sweep((lambda t: norm_stats(t, 0, "h0", N_H0), 0), (lambda t: norm(t, 0), 1),
                  (quantize, 1), (vE, 3), (rank, 4))

            def kb0(t):
                dve.wait_ge(s["kv"], t + 1)
                if t >= 2:
                    dve.wait_ge(s["S0"], t - 1)
                for m in range(DC):
                    at_ = 256 + 64 * m
                    last = v.scalar_tensor_tensor(
                        kbd0[:, t % 2, m, :].rearrange("p (n k) -> p n k", k=KK),
                        spread(ps[:, 1, at_:at_ + KK], 1, [128, HC, KK]), V("bk")[:, m:m + 1],
                        spread(C("head"), 2, [128, HC, KK]), ALU.add, ALU.mult)
                last.then_inc(s["kb0"], 1)

            def vt_(t):
                dve.wait_ge(s["kv"], t + 1)
                if t >= 2:
                    dve.wait_ge(s["vm0"], t - 1)
                v.tensor_tensor(vt[:, t % 2, :], ps[0:2 * KK, 1, 0:D], B("bv", 2 * KK), ALU.add).then_inc(s["vt"], 1)

            def softmax_top(t, S_ps, sm, pr, on, pt, name, width):
                dve.wait_ge(s[on], t + 1)
                l = link(dve, name, 2 * t)
                mx = sm[:, t % 2, 0, :].rearrange("p (c n) -> p c n", c=DC)
                l(v.tensor_reduce(mx, S_ps, AX.X, ALU.max))
                if t >= 3:
                    dve.wait_ge(s[pt], t - 2)
                l(v.tensor_tensor(pr[:, t % 3, :].rearrange("p (c n k) -> p c n k", c=DC, k=width), S_ps,
                                  spread(mx, 3, [R, DC, HC, width]), ALU.subtract), False)

            def softmax_sum(t, sm, pr, on, pn, name, width):
                dve.wait_ge(s[on], t + 1)
                l = link(dve, name, N_SUM * t)
                l(v.tensor_reduce(sm[:, t % 2, 1, :], pr[:, t % 3, :].rearrange("p (n k) -> p n k", k=width),
                                  AX.X, ALU.add))
                if t >= 2:
                    dve.wait_ge(s[pn], t - 1)
                l(v.reciprocal(sm[:, t % 2, 2, :], sm[:, t % 2, 1, :]), False)

            def residual(t, layer, bank, on, name):
                dve.wait_ge(s[on], t + 1)
                dve.wait_ge(s["hb"], layer * T + t + 1)
                v.tensor_tensor(h[:, t, :], ps[0:R, bank, 0:D], h[:, t, :], ALU.add).then_inc(s[name], 1)

            S0_ps = ps[0:R, 2:4, 0:HC * KK].rearrange("p c (n k) -> p c n k", k=KK)
            sweep((kb0, 0), (vt_, 0), (lambda t: softmax_top(t, S0_ps, sm0, pr0, "S0", "pt0", "smx0", KK), 1),
                  (lambda t: softmax_sum(t, sm0, pr0, "ex0", "pn0", "sum0", KK), 2),
                  (lambda t: residual(t, 0, 7, "op0", "h4"), 6))

            def xlo_(t):
                dve.wait_ge(s["xhi"], t + 1)
                v.tensor_tensor(xlo[:, t % 2, :, 0:R], ps[:, 0, 0:DC * RP].rearrange("p (c r) -> p c r", c=DC)[:, :, 0:R],
                                xhi[:, t % 2, :, 0:R].bitcast(F32), ALU.subtract).then_inc(s["xlo"], 1)

            def hlo_(t, half, on, name):
                dve.wait_ge(s[on], t + 1)
                f = slice(half * FC // 2, (half + 1) * FC // 2)
                v.scalar_tensor_tensor(hlo[:, t % 2, f, :].rearrange("p c r -> p (c r)"),
                                       ps[:, 1 + half, 0:FC // 2 * RP], 0.0,
                                       hhi[:, t % 2, f, :].rearrange("p c r -> p (c r)").bitcast(F32),
                                       ALU.max, ALU.subtract).then_inc(s[name], 1)

            sweep((lambda t: norm_stats(t, 1, "h4", 1), 0), (lambda t: norm(t, 1), 1), (xlo_, 2),
                  (lambda t: hlo_(t, 0, "hia", "loa"), 3), (lambda t: hlo_(t, 1, "hib", "lob"), 3),
                  (lambda t: residual(t, 1, 3, "w2", "h5"), 5))

            def rope(t):
                dve.wait_ge(s["qkv"], t + 1)
                if t >= 2:
                    dve.wait_ge(s["tq"], t - 1)
                n = 2 * H
                qk = ps[0:R, 5, :].rearrange("p (n e o) -> p n e o", n=n, o=2)
                v.tensor_tensor(rot[:, t % 2, 0, :].rearrange("p (n d) -> p n d", n=n),
                                ps[0:R, 5, :].rearrange("p (n d) -> p n d", n=n),
                                spread(C("cos", R), 1, [R, n, HD]), ALU.mult).then_inc(s["rope"], 1)
                v.tensor_tensor(rot[:, t % 2, 1, :].rearrange("p (n e o) -> p n e o", n=n, o=2), qk[:, :, :, ::-1],
                                C("sin", R).rearrange("p (e o) -> p e o", o=2).unsqueeze(1).broadcast_to([R, n, HD // 2, 2]),
                                ALU.mult).then_inc(s["rope"], 1)

            sweep((lambda t: norm_stats(t, 2, "h5", 1), 0), (lambda t: norm(t, 2), 1), (rope, 3))

            def kbB(t):
                dve.wait_ge(s["tke"], T)
                if t >= 2:
                    dve.wait_ge(s["S7"], t - 1)
                v.tensor_tensor(kbd7[:, t % 2, 1, :].rearrange("p (i n k) -> p i n k", i=IM, n=HC),
                                xT[:, t, 1, 0:R].rearrange("p (i k) -> p i k", i=IM).unsqueeze(2).broadcast_to([128, IM, HC, S]),
                                C("head").unsqueeze(1).unsqueeze(3).broadcast_to([128, IM, HC, S]),
                                ALU.mult).then_inc(s["kbB"], 1)

            def S7_ps(t):
                b = 2 * (t % 2)
                return ps[0:R, b:b + 2, 0:HC * S].rearrange("p c (n k) -> p c n k", k=S)

            sweep((kbB, 0), (lambda t: softmax_top(t, S7_ps(t), sm7, pr7, "S7", "pt7", "smx7", S), 1),
                  (lambda t: softmax_sum(t, sm7, pr7, "ex7", "pn7", "sum7", S), 2),
                  (lambda t: residual(t, 2, 7, "op7", "h7"), 6))

            def rw(t):
                l = link(dve, "rw", N_RW * t)
                dve.wait_ge(s["xn"], t + 3 * T + 1)
                l(v.tensor_tensor_reduce(junk[:], xa[:, t, 0:D], B("router_w"), 1.0, 0.0, ALU.mult, ALU.add,
                                         rk9[:, t % 2, 0:1]))
                l(v.tensor_scalar(xa[:, t, D:D + 1], rk9[:, t % 2, 0:1], V("router_b")[0:R, :], None, ALU.add))
                l(v.tensor_scalar(rk9[:, t % 2, 8:8 + S], C("tok", R), xa[:, t, D:D + 1], None, ALU.mult), False)

            def rank9(t):
                dve.wait_ge(s["G9"], t + 1)
                rk = rk9[:, t % 2, :]
                G = ps[0:R, 0, 64 * (t % 2):64 * (t % 2) + S]
                l = link(dve, "rank9", N_RANK9 * t)
                ranks(l, rk, G)
                l(v.tensor_scalar(rk[:, 45:45 + S], G, rk[:, 1:2], None, ALU.is_ge))
                l(v.tensor_reduce(rk[:, 3:4], rk[:, 45:45 + S], AX.X, ALU.add))
                if t >= 2:
                    dve.wait_ge(s["oht"], t - 1)
                a = (T - 1 - t) * IM * NSEL
                l(v.tensor_scalar(oh9[:, t % 2, :], C("slot1", R)[:, a:a + W3], rk[:, 2:3], None, ALU.is_equal), False)
                l(v.tensor_scalar(rk[:, 4:5], rk[:, 3:4], KSEL - 0.5, None, ALU.is_gt))
                v.scalar_tensor_tensor(h[:, t, :], xa[:, t, 0:D], rk[:, 4:5], h[:, t, :], ALU.mult,
                                       ALU.add).then_inc(s["base"], 1)

            sweep((lambda t: norm_stats(t, 3, "h7", 1), 0), (lambda t: norm(t, 3), 1), (rw, 2),
                  (rank9, 3))

            l = link(dve, "tv", 0)
            x_ = t_x[:, 0:D]
            dve.wait_ge(s["acc"], T)
            l(v.tensor_copy(t_x, ps[0:W3, 1, 0:XA]))
            l(v.tensor_copy(t_cmp[:, 0:W3], ps[0:S, 2, 0:W3]))
            v.tensor_tensor_reduce(t_hn, x_, x_, 1.0, 0.0, ALU.mult, ALU.add, t_sc[:, 1:2]).then_inc(s["sc"], 1)
            f = [t_f[:, i, :] for i in range(6)]
            turn = (6.28125, 0.0019350051879882812, 3.0199159819e-07)
            magic = 12582912.0
            l(v.tensor_scalar(f[0], C("inv", W3), t_x[:, D + 1:D + 2], None, ALU.mult))
            l(v.tensor_scalar(f[1], f[0], float(0.5 / np.pi), magic, ALU.mult, ALU.add))
            l(v.tensor_scalar(f[1], f[1], -magic, None, ALU.add))
            for part in turn:
                l(v.scalar_tensor_tensor(f[0], f[1], -part, f[0], ALU.mult, ALU.add))
            l(v.tensor_scalar(f[0], f[0], -3.1415925, 3.1415925, ALU.max, ALU.min))
            l(v.scalar_tensor_tensor(f[2], f[0], -1.0, f[0], ALU.mult, ALU.max))
            v.tensor_scalar(f[2], f[2], -1.0, float(np.pi / 2), ALU.mult, ALU.add).then_inc(s["t_ang"], 1)
            dve.wait_ge(s["sc"], 3)
            v.scalar_tensor_tensor(t_hn, x_, t_sc[:, 3:4], B("ln1", W3), ALU.mult, ALU.mult).then_inc(s["t_hn"], 1)
            dve.wait_ge(s["t_T"], 1)
            v.tensor_copy(t_cmp[:, W3:2 * W3], ps[0:S, 5, 0:W3]).then_inc(s["t_mrow"], 1)
            dve.wait_ge(s["t_sin"], 2)
            l(v.tensor_tensor(f[3], f[3], C("sign", W3), ALU.mult))
            dve.wait_ge(s["t_mm"], 1)
            l(v.scalar_tensor_tensor(t_mm, ps[0:W3, 5, 0:W3], 1.0 / SCALE, C("other1", W3), ALU.mult, ALU.add))
            dve.wait_ge(s["t_qkv"], 1)
            n = 2 * H
            l(v.tensor_tensor(t_rot[:, 0, :].rearrange("p (n d) -> p n d", n=n),
                              ps[0:W3, 6, :].rearrange("p (n d) -> p n d", n=n),
                              spread(f[4], 1, [W3, n, HD]), ALU.mult), False)
            l(v.tensor_tensor(t_rot[:, 1, :].rearrange("p (n a d) -> p n a d", n=n, a=2),
                              ps[0:W3, 6, :].rearrange("p (n a d) -> p n a d", n=n, a=2)[:, :, ::-1, :],
                              f[3].rearrange("p (a d) -> p a d", a=2).unsqueeze(1).broadcast_to([W3, n, 2, HD // 2]),
                              ALU.mult))
            v.tensor_tensor(t_rot[:, 0, :], t_rot[:, 0, :], t_rot[:, 1, :], ALU.add).then_inc(s["t_rot"], 1)
            dve.wait_ge(s["t_qkT"], 1)
            for m in range(DC):
                last = v.tensor_tensor(t_kbd[:, m, :].rearrange("p (n k) -> p n k", n=HC),
                                       spread(t_qkT[:, DC + m, :], 1, [128, HC, W3]),
                                       spread(C("head"), 2, [128, HC, W3]), ALU.mult)
            last.then_inc(s["t_kbd"], 1)
            dve.wait_ge(s["t_S"], 1)
            p3 = t_p.rearrange("p (n k) -> p n k", k=W3)
            p4 = t_p.rearrange("p (g n k) -> p g n k", g=4, k=W3)
            l(v.tensor_tensor(p4, ps[0:W3, 0:4, 0:4 * W3].rearrange("p g (n k) -> p g n k", k=W3),
                              t_mm.unsqueeze(1).unsqueeze(1).broadcast_to([W3, 4, 4, W3]), ALU.add))
            l(v.tensor_reduce(t_mx[:, 0, :], p3, AX.X, ALU.max))
            v.tensor_tensor(p3, p3, spread(t_mx[:, 0, :], 2, [W3, H, W3]), ALU.subtract).then_inc(s["t_sub"], 1)
            dve.wait_ge(s["t_exp"], 1)
            l(v.tensor_reduce(t_mx[:, 1, :], p3, AX.X, ALU.add))
            l(v.reciprocal(t_mx[:, 2, :], t_mx[:, 1, :]))
            dve.wait_ge(s["t_O"], 1)
            v.tensor_tensor(t_o.rearrange("p (n d) -> p n d", n=H), ps[0:W3, 0, 0:D].rearrange("p (n d) -> p n d", n=H),
                            spread(t_mx[:, 2, :], 2, [W3, H, HD]), ALU.mult).then_inc(s["t_o"], 1)
            dve.wait_ge(s["t_wo"], 1)
            l(v.tensor_tensor(t_x1, ps[0:W3, 2, 0:D], x_, ALU.add))
            v.tensor_tensor_reduce(t_hn, t_x1, t_x1, 1.0, 0.0, ALU.mult, ALU.add, t_sc[:, 5:6]).then_inc(s["sc"], 1)
            dve.wait_ge(s["sc"], 6)
            v.scalar_tensor_tensor(t_hn, t_x1, t_sc[:, 7:8], B("ln2", W3), ALU.mult, ALU.mult).then_inc(s["t_hn"], 1)
            dve.wait_ge(s["t_w2"], 1)
            l(v.tensor_tensor(t_y, ps[0:W3, 6, 0:D], t_x1, ALU.add))
            v.tensor_scalar(t_y, t_y, t_x[:, D:D + 1], None, ALU.mult).then_inc(s["t_y"], 1)
            for t in range(T):
                dve.wait_ge(s["t_put"], t + 1)
                v.tensor_tensor(h[:, t, :], ps[0:R, t % 4, 0:D], h[:, t, :], ALU.add).then_inc(s["fin"], 1)

        @block.scalar
        def _(act):
            a = nc.scalar

            def rows_of(bank, n, w=RP, used=R):
                return ps[:, bank, 0:n * w].rearrange("p (c r) -> p c r", c=n)[:, :, 0:used]

            def gw_(t):
                if t == 0:
                    act.wait_ge(s["wproj"], 16)
                    act.wait_ge(s["vec"], 16)
                    for c in range(PC):
                        last = a.activation(gW[:, c, :], w_proj[:, c, :], ACT.Copy, scale=V("ln1_g")[:, c:c + 1])
                    last.then_inc(s["gw"], 1)

            def xT1_(t):
                act.wait_ge(s["tr1"], t + 1)
                if t >= 2:
                    act.wait_ge(s["pj"], t - 1)
                a.copy(pT[:, t % 2, :, 0:R].rearrange("p (b c) r -> p b c r", b=2),
                       ps[:, 0:2, 0:3 * RP].rearrange("p b (c r) -> p b c r", c=3)[:, :, :, 0:R]).then_inc(s["xT1"], 1)

            sweep((gw_, 0), (xT1_, 0))

            def xT2_(t):
                act.wait_ge(s["T2"], t + 1)
                if t == 0:
                    act.wait_ge(s["pj"], T)
                a.copy(xT[:, t, :, 0:R], rows_of(4, DC)).then_inc(s["xT2"], 1)

            def hid(t):
                act.wait_ge(s["hidp"], t + 1)
                if t >= 2:
                    act.wait_ge(s["imp"], t - 1)
                a.activation(hT[:, t % 2, 0:R], ps[:, 5, 0:R], ACT.Relu, bias=V("bi1")).then_inc(s["hid"], 1)

            def xs_(t):
                act.wait_ge(s["gx"], t + 1)
                a.copy(xsT[:, t, :, :].rearrange("p c (n k) -> p c n k", n=2),
                       rows_of(7, DC, 64, KK).unsqueeze(2).broadcast_to([128, DC, 2, KK])).then_inc(s["xs"], 1)

            sweep((xT2_, 0), (hid, 1), (xs_, 4))

            def q0(t):
                act.wait_ge(s["q"], t + 1)
                if t == 0:
                    act.wait_ge(s["quant"], 2)
                if t >= 2:
                    act.wait_ge(s["S0"], t - 1)
                for m in range(DC):
                    last = a.activation(qT0[:, t % 2, m, 0:R], ps[:, 0, m * RP:m * RP + R], ACT.Identity,
                                        bias=V("bq")[:, m:m + 1])
                last.then_inc(s["q0"], 1)

            def exps(t, pr, on, name):
                act.wait_ge(s[on], 2 * (t + 1))
                a.activation(pr[:, t % 3, :], pr[:, t % 3, :], ACT.Exp, scale=SCALE).then_inc(s[name], 1)

            def probsT(t, dst, n_rows, on, free, name):
                act.wait_ge(s[on], t + 1)
                if t >= 2:
                    act.wait_ge(s[free], t - 1)
                a.copy(dst[:, t % 2, :, 0:R].rearrange("p (b c) r -> p b c r", b=2),
                       ps[0:n_rows, 4:6, 0:PAIRS // 2 * RP].rearrange("p b (c r) -> p b c r", b=2, r=RP)[:, :, :, 0:R]
                       ).then_inc(s[name], 1)

            def outT(t, dst, on, free, name):
                act.wait_ge(s[on], t + 1)
                if t >= 2:
                    act.wait_ge(s[free], t - 1)
                a.copy(dst[:, t % 2, :, 0:R], rows_of(6, DC)).then_inc(s[name], 1)

            sweep((q0, 0), (lambda t: exps(t, pr0, "smx0", "ex0"), 1),
                  (lambda t: probsT(t, PT0, 2 * KK, "pt0", "pv0", "PT0"), 3),
                  (lambda t: outT(t, oT0, "pv0", "op0", "oT0"), 4))

            def xhi_(t):
                act.wait_ge(s["T5"], t + 1)
                if t >= 2:
                    act.wait_ge(s["w1b"], t - 1)
                a.copy(xhi[:, t % 2, :, 0:R], rows_of(0, DC)).then_inc(s["xhi"], 1)

            def hhi_(t, half, on, name):
                act.wait_ge(s[on], t + 1)
                if t >= 2:
                    act.wait_ge(s["w2"], t - 1)
                f = slice(half * FC // 2, (half + 1) * FC // 2)
                a.activation(hhi[:, t % 2, f, :].rearrange("p c r -> p (c r)"), ps[:, 1 + half, 0:FC // 2 * RP],
                             ACT.Relu).then_inc(s[name], 1)

            sweep((xhi_, 0), (lambda t: hhi_(t, 0, "w1a", "hia"), 1), (lambda t: hhi_(t, 1, "w1b", "hib"), 1))

            def xT6_(t):
                act.wait_ge(s["T6"], t + 1)
                if t >= 2:
                    act.wait_ge(s["qkv"], t - 1)
                a.copy(xT6[:, t % 2, :, 0:R], rows_of(4, DC)).then_inc(s["xT6"], 1)

            def v6_(t):
                act.wait_ge(s["qkv"], t + 1)
                a.copy(v1[:, t, :], ps[0:R, 6, 0:D]).then_inc(s["v6"], 1)

            def tqe(t):
                act.wait_ge(s["tq"], t + 1)
                view = rows_of(7, 2 * DC)
                a.copy(q6[:, t, :, 0:R], view[:, 0:DC, :]).then_inc(s["tqe"], 1)
                a.copy(xT[:, t, :, 0:R], view[:, DC:2 * DC, :]).then_inc(s["tke"], 1)

            sweep((xT6_, 0), (v6_, 1), (tqe, 3))

            def qm7(t):
                act.wait_ge(s["tqe"], t + 1)
                if t == 0:
                    act.wait_ge(s["qz"], 1)
                if t >= 2:
                    act.wait_ge(s["S7"], t - 1)
                for m in range(DC):
                    flat = qTm[:, t % 2, m, :, :].rearrange("p i r -> p (i r)")
                    base = flat[:, 0:S]
                    dst = bass.AP(base.tensor, base.offset, [list(base.ap[0]), [RP + S, IM], [1, S]])
                    last = a.copy(dst, q6[:, t, m, 0:R].rearrange("p (i r) -> p i r", i=IM))
                last.then_inc(s["qm7"], 1)

            sweep((qm7, 0), (lambda t: exps(t, pr7, "smx7", "ex7"), 1),
                  (lambda t: probsT(t, PT7, 2 * S, "pt7", "pv7", "PT7"), 3),
                  (lambda t: outT(t, oT7, "pv7", "op7", "oT7"), 4))

            def ohte(t):
                act.wait_ge(s["oht"], t + 1)
                a.copy(ohT[:, t, 0:R], ps[0:W3, 3, 0:R]).then_inc(s["ohte"], 1)

            sweep((ohte, 0))
            act.wait_ge(s["t_ang"], 1)
            a.activation(t_f[:, 3, :], t_f[:, 0, :], ACT.Sin).then_inc(s["t_sin"], 1)
            a.activation(t_f[:, 4, :], t_f[:, 2, :], ACT.Sin).then_inc(s["t_sin"], 1)
            act.wait_ge(s["t_T"], 1)
            a.copy(t_hnT, ps[:, 4, 0:DC * W3].rearrange("p (c r) -> p c r", c=DC)).then_inc(s["t_hnT"], 1)
            act.wait_ge(s["t_qkv"], 1)
            a.copy(t_v, ps[0:W3, 7, 0:D]).then_inc(s["t_v"], 1)
            act.wait_ge(s["t_Tr"], 1)
            a.copy(t_qkT, ps[:, 4, 0:4 * W3].rearrange("p (c r) -> p c r", c=4)).then_inc(s["t_qkT"], 1)
            act.wait_ge(s["t_sub"], 1)
            a.activation(t_p, t_p, ACT.Exp, scale=SCALE).then_inc(s["t_exp"], 1)
            act.wait_ge(s["t_pT"], 1)
            a.copy(t_PT.rearrange("p (g n) -> p g n", g=4), ps[0:W3, 4:8, 0:4 * W3]).then_inc(s["t_PT"], 1)
            act.wait_ge(s["t_To"], 1)
            a.copy(t_oT, ps[:, 1, 0:DC * W3].rearrange("p (c r) -> p c r", c=DC)).then_inc(s["t_oT"], 1)
            act.wait_ge(s["t_T"], 2)
            a.copy(t_hnT, ps[:, 3, 0:DC * W3].rearrange("p (c r) -> p c r", c=DC)).then_inc(s["t_hnT"], 1)
            act.wait_ge(s["t_w1"], 1)
            a.activation(t_g.rearrange("p (b c) r -> p b (c r)", b=2), ps[:, 4:6, 0:4 * W3],
                         ACT.Gelu_apprx_tanh).then_inc(s["t_g"], 1)

        @block.tensor
        def _(pe):
            m_ = nc.tensor
            ident = C("ident")

            def transposes(bank, src, n, name, t_on=None):
                for c in range(n):
                    last = m_.transpose(ps[:, bank, c * RP:c * RP + R], src[:, c * 128:(c + 1) * 128], ident[0:R, 0:R])
                last.then_inc(s[name], 1)

            def tr1(t):
                pe.wait_ge(s["xh1"], t + 1)
                if t == 0:
                    pe.wait_ge(s["cst"], 16)
                if t >= 1:
                    pe.wait_ge(s["xT1"], t)
                for c in range(PC):
                    last = m_.transpose(ps[:, c // 3, (c % 3) * RP:(c % 3) * RP + R],
                                        pat[:, t % 3, c * 128:(c + 1) * 128], ident[0:R, 0:R])
                last.then_inc(s["tr1"], 1)
                if t == 0:
                    pe.wait_ge(s["wproj"], 16)
                    pe.wait_ge(s["vec"], 16)
                    for c in range(PC):
                        last = m_.matmul(ps[0:R, 4, 0:D], V("ln1_b")[:, c:c + 1].broadcast_to([128, R]),
                                         w_proj[:, c, :], start=(c == 0), stop=(c == PC - 1))
                    last.then_inc(s["biasps"], 1)

            def pj(t):
                pe.wait_ge(s["xT1"], t + 1)
                if t == 0:
                    pe.wait_ge(s["gw"], 1)
                if t >= 2:
                    pe.wait_ge(s["z"], N_Z * (t - 1))
                for c in range(PC):
                    last = m_.matmul(ps[0:R, 2 + t % 2, 0:D], pT[:, t % 2, c, 0:R], gW[:, c, :],
                                     start=(c == 0), stop=(c == PC - 1))
                last.then_inc(s["pj"], 1)

            sweep((tr1, 0), (pj, 1))

            def T2(t):
                pe.wait_ge(s["xn"], t + 1)
                if t == 0:
                    pe.wait_ge(s["bp0"], 1)
                    pe.wait_ge(s["absum"], 2)
                    pe.wait_ge(s["pool_set"], 2)
                    m_.matmul(ps[:, 7, 508:510], ones[:], gam[:, 0:2], start=True, stop=True).then_inc(s["gamps"], 1)
                if t >= 1:
                    pe.wait_ge(s["xT2"], t)
                transposes(4, xa[:, t, 0:D], DC, "T2")

            def hidp(t):
                pe.wait_ge(s["xT2"], t + 1)
                if t == 0:
                    pe.wait_ge(s["w0"], 16 * 5)
                if t >= 1:
                    pe.wait_ge(s["hid"], t)
                for c in range(DC):
                    last = m_.matmul(ps[:, 5, 0:R], wi1[:, c, :], xT[:, t, c, 0:R], start=(c == 0), stop=(c == DC - 1))
                last.then_inc(s["hidp"], 1)

            def imp(t):
                pe.wait_ge(s["hid"], t + 1)
                if t >= 1:
                    pe.wait_ge(s["vE"], N_VE * t)
                m_.matmul(ps[0:R, 6, 2 * (t % 2):2 * (t % 2) + 1], hT[:, t % 2, 0:R], V("wi2"), start=True,
                          stop=True).then_inc(s["imp"], 1)

            def G(t):
                pe.wait_ge(s["vE"], N_VE * (t + 1))
                if t >= 1:
                    pe.wait_ge(s["rank"], N_RANK * t)
                m_.matmul(ps[0:R, 2, 0:S], C("same", R), rk0[:, t % 2, 8:8 + S], start=True,
                          stop=True).then_inc(s["G"], 1)

            def gx(t):
                pe.wait_ge(s["rank"], N_RANK * (t + 1))
                if t == 0:
                    pe.wait_ge(s["thr"], 2)
                if t >= 1:
                    pe.wait_ge(s["xs"], t)
                for c in range(DC):
                    last = m_.matmul(ps[:, 7, 64 * c:64 * c + KK], xa[:, t, c * 128:(c + 1) * 128], oh0[:, t % 2, :],
                                     start=True, stop=True)
                last.then_inc(s["gx"], 1)

            sweep((T2, 0), (hidp, 1), (imp, 2), (G, 3), (gx, 4))

            def q_(t):
                pe.wait_ge(s["xs"], t + 1)
                if t == 0:
                    pe.wait_ge(s["zn"], T)
                    pe.wait_ge(s["xs"], T)
                if t >= 1:
                    pe.wait_ge(s["q0"], t)
                for m in range(DC):
                    cols = slice(m * 128, (m + 1) * 128)
                    for c in range(DC):
                        last = m_.matmul(ps[:, 0, m * RP:m * RP + R], wq0[:, c, cols], xT[:, t, c, 0:R],
                                         start=(c == 0), stop=(c == DC - 1))
                last.then_inc(s["q"], 1)

            def kv_(t):
                if t >= 1:
                    pe.wait_ge(s["vt"], t)
                    pe.wait_ge(s["kb0"], t)
                for m in range(DC):
                    for c in range(DC):
                        m_.matmul(ps[:, 1, 256 + 64 * m:256 + 64 * m + KK], wk0[:, c, m * 128:(m + 1) * 128],
                                  xsT[:, t, c, 0:KK], start=(c == 0), stop=(c == DC - 1))
                for c in range(DC):
                    last = m_.matmul(ps[0:2 * KK, 1, 0:D], xsT[:, t, c, :],
                                     wv0[:, c, :], start=(c == 0), stop=(c == DC - 1))
                last.then_inc(s["kv"], 1)

            def S0(t):
                pe.wait_ge(s["q0"], t + 1)
                pe.wait_ge(s["kb0"], t + 1)
                if t == 0:
                    pe.wait_ge(s["cast"], 3)
                if t >= 1:
                    pe.wait_ge(s["smx0"], 2 * t)
                for m in range(DC):
                    dst = ps[0:R, 2 + m, 0:HC * KK]
                    m_.matmul(dst, qT0[:, t % 2, m, 0:R], kbd0[:, t % 2, m, :], start=True, stop=False)
                    last = m_.matmul(dst, ident_b[:], other_b[:].unsqueeze(1).broadcast_to([R, HC, KK]),
                                     start=False, stop=True)
                last.then_inc(s["S0"], 1)

            def pT_(t, pr, w, on, free, name):
                pe.wait_ge(s[on], t + 1)
                if t >= 1:
                    pe.wait_ge(s[free], t)
                for p in range(PAIRS):
                    o = (p % 4) * RP
                    last = m_.transpose(ps[0:w, 4 + p // 4, o:o + R], pr[:, t % 3, p * w:(p + 1) * w], ident[0:R, 0:R])
                last.then_inc(s[name], 1)

            def pv0(t):
                pe.wait_ge(s["PT0"], t + 1)
                pe.wait_ge(s["vm0"], t + 1)
                if t >= 1:
                    pe.wait_ge(s["oT0"], t)
                for p in range(PAIRS):
                    q = 32 * (p % 4)
                    o = (p // 4) * RP
                    last = m_.matmul(ps[q:q + 32, 6, o:o + R], vm0[:, t % 3, 32 * p:32 * p + 32], PT0[:, t % 2, p, 0:R],
                                     start=True, stop=True)
                last.then_inc(s["pv0"], 1)

            def project(t, oT, w, on, free, name):
                pe.wait_ge(s[on], t + 1)
                if t >= 1:
                    pe.wait_ge(s[free], t)
                for c in range(DC):
                    last = m_.matmul(ps[0:R, 7, 0:D], oT[:, t % 2, c, 0:R], w[:, c, :], start=(c == 0), stop=(c == DC - 1))
                last.then_inc(s[name], 1)

            sweep((q_, 0), (kv_, 0), (S0, 1), (lambda t: pT_(t, pr0, 2 * KK, "pn0", "PT0", "pt0"), 3), (pv0, 4),
                  (lambda t: project(t, oT0, wo0, "oT0", "h4", "op0"), 5))

            def T5(t):
                pe.wait_ge(s["xn"], t + 1 * T + 1)
                if t == 0:
                    pe.wait_ge(s["q0"], T)
                    pe.wait_ge(s["kb0"], T)
                if t >= 1:
                    pe.wait_ge(s["xlo"], t)
                transposes(0, xa[:, t, 0:D], DC, "T5")

            def w1(t, half, free, name):
                pe.wait_ge(s["xlo"], t + 1)
                if t == 0:
                    pe.wait_ge(s["smx0"], 2 * T)
                    pe.wait_ge(s["vt"], T)
                    pe.wait_ge(s["quant"], 2)
                    pe.wait_ge(s["parts"], 7)
                    pe.wait_ge(s["pool_set"], 5)
                if t >= 1:
                    pe.wait_ge(s[free], t)
                for i in range(FC // 2):
                    f = half * FC // 2 + i
                    dst = ps[:, 1 + half, i * RP:(i + 1) * RP]
                    m_.matmul(dst, brow[:, f * 128:(f + 1) * 128], ones_b[:, 0:RP], start=True, stop=False)
                    for c in range(DC):
                        for x in (xhi, xlo):
                            last = m_.matmul(dst, w1q[:, c, f * 128:(f + 1) * 128], x[:, t % 2, c, :],
                                             start=False, stop=(c == DC - 1 and x is xlo))
                last.then_inc(s[name], 1)

            def w2(t):
                pe.wait_ge(s["loa"], t + 1)
                pe.wait_ge(s["lob"], t + 1)
                if t >= 1:
                    pe.wait_ge(s["h5"], t)
                for f in range(FC):
                    for x in (hhi, hlo):
                        last = m_.matmul(ps[0:R, 3, 0:D], x[:, t % 2, f, 0:R], w2q[:, f, :],
                                         start=(f == 0 and x is hhi), stop=(f == FC - 1 and x is hlo))
                last.then_inc(s["w2"], 1)

            sweep((T5, 0), (lambda t: w1(t, 0, "loa", "w1a"), 1), (lambda t: w1(t, 1, "lob", "w1b"), 1), (w2, 2))

            def T6(t):
                pe.wait_ge(s["xn"], t + 2 * T + 1)
                if t >= 1:
                    pe.wait_ge(s["xT6"], t)
                transposes(4, xa[:, t, 0:D], DC, "T6")

            def qkv(t):
                pe.wait_ge(s["xT6"], t + 1)
                if t == 0:
                    pe.wait_ge(s["wl1"], 32)
                if t >= 1:
                    pe.wait_ge(s["rope"], 2 * t)
                    pe.wait_ge(s["v6"], t)
                for bank, cols in ((5, slice(0, 2 * D)), (6, slice(2 * D, 3 * D))):
                    dst = ps[0:R, bank, 0:cols.stop - cols.start]
                    m_.matmul(dst, ones_b[:, 0:R], brow[:, F + cols.start:F + cols.stop], start=True, stop=False)
                    for c in range(DC):
                        last = m_.matmul(dst, xT6[:, t % 2, c, 0:R], wqkv[:, c, cols], start=False, stop=(c == DC - 1))
                last.then_inc(s["qkv"], 1)

            def tq(t):
                pe.wait_ge(s["rope_sum"], t + 1)
                if t >= 1:
                    pe.wait_ge(s["tke"], t)
                transposes(7, rot[:, t % 2, 0, :], 2 * DC, "tq")

            sweep((T6, 0), (qkv, 1), (tq, 3))

            def S7(t):
                pe.wait_ge(s["qm7"], t + 1)
                pe.wait_ge(s["kbA"], t + 1)
                pe.wait_ge(s["kbB"], t + 1)
                if t == 0:
                    pe.wait_ge(s["h5"], T)
                if t >= 2:
                    pe.wait_ge(s["smx7"], 2 * (t - 1))
                for m in range(DC):
                    dst = ps[0:R, 2 * (t % 2) + m, 0:HC * S]
                    for i in range(IM):
                        m_.matmul(dst, qTm[:, t % 2, m, i, 0:R], kbd7[:, t % 2, m, i * HC * S:(i + 1) * HC * S],
                                  start=(i == 0), stop=False)
                    last = m_.matmul(dst, ident_b[:], causal_b[:].unsqueeze(1).broadcast_to([R, HC, S]),
                                     start=False, stop=True)
                last.then_inc(s["S7"], 1)

            def pv7(t):
                pe.wait_ge(s["PT7"], t + 1)
                pe.wait_ge(s["vm7"], t + 1)
                if t >= 1:
                    pe.wait_ge(s["oT7"], t)
                for p in range(PAIRS):
                    q = 32 * (p % 4)
                    for i in range(IM):
                        o = (p // 4) * RP + i * S
                        a_ = i * D + 32 * p
                        last = m_.matmul(ps[q:q + 32, 6, o:o + S], vm7[:, t % 3, a_:a_ + 32],
                                         PT7[:, t % 2, p, i * S:(i + 1) * S], start=True, stop=True)
                last.then_inc(s["pv7"], 1)

            sweep((S7, 0), (lambda t: pT_(t, pr7, 2 * S, "pn7", "PT7", "pt7"), 2), (pv7, 3),
                  (lambda t: project(t, oT7, wp, "oT7", "h7", "op7"), 4))

            def G9(t):
                pe.wait_ge(s["rw"], N_RW * (t + 1))
                if t == 0:
                    pe.wait_ge(s["smx7"], 2 * T)
                if t >= 1:
                    pe.wait_ge(s["rank9"], N_RANK9 * t)
                m_.matmul(ps[0:R, 0, 64 * (t % 2):64 * (t % 2) + S], C("same", R), rk9[:, t % 2, 8:8 + S], start=True,
                          stop=True).then_inc(s["G9"], 1)

            def gather(t):
                pe.wait_ge(s["rank9"], N_RANK9 * (t + 1))
                if t == 0:
                    pe.wait_ge(s["aug"], 4)
                if t >= 1:
                    pe.wait_ge(s["ohte"], t)
                m_.matmul(ps[0:W3, 1, 0:XA], oh9[:, t % 2, :], xa[:, t, :], start=(t == 0), stop=(t == T - 1))
                m_.matmul(ps[0:S, 2, 0:W3], C("tok", R), oh9[:, t % 2, :], start=(t == 0), stop=(t == T - 1)
                          ).then_inc(s["acc"], 1)
                m_.transpose(ps[0:W3, 3, 0:R], oh9[:, t % 2, :], ident[0:R, 0:R]).then_inc(s["oht"], 1)

            sweep((G9, 0), (gather, 1))

            def turn(bank, src, w, n, name, at_=0):
                for c in range(n):
                    last = m_.transpose(ps[0:w, bank, at_ + c * W3:at_ + (c + 1) * W3], src[:, c * w:(c + 1) * w],
                                        ident[0:W3, 0:W3])
                if name:
                    last.then_inc(s[name], 1)

            pe.wait_ge(s["t_hn"], 1)
            turn(5, t_x[:, D + 2:XA], S, 1, None)
            turn(4, t_hn, 128, DC, "t_T")
            pe.wait_ge(s["t_mrow"], 1)
            m_.matmul(ps[0:W3, 5, 0:W3], t_cmp[:, W3:2 * W3], t_cmp[:, 0:W3], start=True, stop=True).then_inc(s["t_mm"], 1)
            pe.wait_ge(s["t_hnT"], 1)
            pe.wait_ge(s["w2nd"], 32)
            for bank, cols in ((6, slice(0, 2 * D)), (7, slice(2 * D, 3 * D))):
                for c in range(DC):
                    last = m_.matmul(ps[0:W3, bank, 0:cols.stop - cols.start], t_hnT[:, c, :], wqkv_l[:, c, cols],
                                     start=(c == 0), stop=(c == DC - 1))
            last.then_inc(s["t_qkv"], 1)
            pe.wait_ge(s["t_rot"], 1)
            turn(4, t_rot[:, 0, :], 128, 4, "t_Tr")
            pe.wait_ge(s["t_kbd"], 1)
            pe.wait_ge(s["ohte"], T)
            for g in range(4):
                last = m_.matmul(ps[0:W3, g, 0:4 * W3], t_qkT[:, g // 2, :],
                                 t_kbd[:, g // 2, (g % 2) * 4 * W3:(g % 2 + 1) * 4 * W3], start=True, stop=True)
            last.then_inc(s["t_S"], 1)
            pe.wait_ge(s["t_exp"], 1)
            pe.wait_ge(s["t_v"], 1)
            for g in range(4):
                turn(4 + g, t_p[:, g * 4 * W3:(g + 1) * 4 * W3], W3, 4, "t_pT" if g == 3 else None)
            pe.wait_ge(s["t_PT"], 1)
            for n in range(H):
                last = m_.matmul(ps[0:W3, 0, n * HD:(n + 1) * HD], t_PT[:, n * W3:(n + 1) * W3],
                                 t_v[:, n * HD:(n + 1) * HD], start=True, stop=True)
            last.then_inc(s["t_O"], 1)
            pe.wait_ge(s["t_o"], 1)
            turn(1, t_o, 128, DC, "t_To")
            pe.wait_ge(s["t_oT"], 1)
            for c in range(DC):
                last = m_.matmul(ps[0:W3, 2, 0:D], t_oT[:, c, :], wo_l[:, c, :], start=(c == 0), stop=(c == DC - 1))
            last.then_inc(s["t_wo"], 1)
            pe.wait_ge(s["t_hn"], 2)
            turn(3, t_hn, 128, DC, "t_T")
            pe.wait_ge(s["t_hnT"], 2)
            pe.wait_ge(s["wlast"], 32)
            for f in range(FC):
                for c in range(DC):
                    last = m_.matmul(ps[:, 4 + f // 4, (f % 4) * W3:(f % 4 + 1) * W3], w1raw[:, c, f * 128:(f + 1) * 128],
                                     t_hnT[:, c, :], start=(c == 0), stop=(c == DC - 1))
            last.then_inc(s["t_w1"], 1)
            pe.wait_ge(s["t_g"], 1)
            for f in range(FC):
                last = m_.matmul(ps[0:W3, 6, 0:D], t_g[:, f, :], w2raw[:, f, :], start=(f == 0), stop=(f == FC - 1))
            last.then_inc(s["t_w2"], 1)
            pe.wait_ge(s["t_y"], 1)
            for t in range(T):
                if t >= 4:
                    pe.wait_ge(s["fin"], t - 3)
                if t == 0:
                    pe.wait_ge(s["base"], T)
                m_.matmul(ps[0:R, t % 4, 0:D], ohT[:, t, 0:R], t_y, start=True, stop=True).then_inc(s["t_put"], 1)


def kernel(**inputs):
    import concourse.bacc as _bacc
    from concourse.bass_utils import run_bass_kernel_spmd as _run

    a = {k: np.ascontiguousarray(v) for k, v in inputs.items()}
    P_ = 16
    n = a["x"].shape[2] // P_
    x = a["x"].reshape(IMAGES, 3, n, P_, n, P_).transpose(0, 2, 4, 3, 5, 1).reshape(IMAGES, PATCHES, PD)
    patches = np.zeros((T * IM, S, PD), x.dtype)
    patches[:IMAGES, 1:] = x

    vectors = np.zeros((128, N_VEC), np.float32)
    p = np.arange(128)
    for name, src in (("ln1_g", "L0_tok_ln1_g"), ("ln1_b", "L0_tok_ln1_b"), ("bq", "L0_attn_bq"), ("bk", "L0_attn_bk"),
                      ("bi1", "L0_attn_bi1"), ("wi2", "L0_attn_wi2")):
        at, w = _vat[name]
        vectors[:, at:at + w] = a[src].reshape(w, 128).T
    vectors[:, _vat["bi2"][0]] = a["L0_attn_bi2"][0]
    vectors[:, _vat["router_b"][0]] = a["L1_ffn_router_b"][0]
    vectors[:, _vat["part1"][0]] = p >= 1
    vectors[:, _vat["part2"][0]] = p >= 2
    names = {"b_proj": "L0_tok_b_proj", "ln2_g": "L0_tok_ln2_g", "ln2_b": "L0_tok_ln2_b", "cls": "L0_tok_cls_token",
             "bv": "L0_attn_bv", "bo": "L0_attn_bo", "b2": "L0_ffn_b2", "bp": "L1_attn_bp",
             "router_w": "L1_ffn_router_w", "ln1": "L1_ffn_ln1", "ln2": "L1_ffn_ln2"}
    rows = np.concatenate([a[names[name]].reshape(1, D) for name in _rat], axis=1)
    wide_rows = np.concatenate([a[k].reshape(1, -1) for k in ("L0_ffn_b1", "L1_attn_bq", "L1_attn_bk", "L1_attn_bv")], axis=1)
    tensors = {
        "patches": patches.reshape(T * R, PD), "W_proj": a["L0_tok_W_proj"], "consts": shape_constants(),
        "vectors": vectors, "rows": rows, "wide_rows": wide_rows, "pos3": np.tile(a["L0_tok_pos_emb"][0], (IM, 1)),
        "wqT": a["L0_attn_wq"].T, "wkT": a["L0_attn_wk"].T, "wvT": a["L0_attn_wv"].T, "woT": a["L0_attn_wo"].T,
        "wi1T": a["L0_attn_wi1"].T, "W1T": a["L0_ffn_W1"].T, "W2T": a["L0_ffn_W2"].T,
        "wqkv1": np.concatenate([a["L1_attn_Wq"], a["L1_attn_Wk"], a["L1_attn_Wv"]], axis=1), "wp1": a["L1_attn_Wp"],
        "mask": a["L1_ffn_attention_mask"], "positions": a["L1_ffn_position_ids"],
        "wqkv2": np.concatenate([a["L1_ffn_wq"], a["L1_ffn_wk"], a["L1_ffn_wv"]], axis=1), "wo2": a["L1_ffn_wo"],
        "w1f": a["L1_ffn_w1"], "w2f": a["L1_ffn_w2"],
    }
    nc = _bacc.Bacc("TRN2", target_bir_lowering=False, num_devices=1)
    arrays, args = {}, {}
    for name, value in tensors.items():
        value = np.ascontiguousarray(value)
        arrays[f"in_{name}"] = value
        args[name] = nc.dram_tensor(f"in_{name}", value.shape, mybir.dt.from_np(value.dtype), kind="ExternalInput").ap()
    args["out"] = nc.dram_tensor("out", (ROWS, D), F32, kind="ExternalOutput").ap()
    vit_tower(nc, **args)
    r = _run(nc, [arrays], core_ids=[0])
    return r.results[0]["out"].reshape(IMAGES, S, D)
```

```python
from contextlib import ExitStack

import numpy as np

import concourse.bass as bass
from concourse import mybir

F32 = mybir.dt.float32
F32R = mybir.dt.float32r
BF16 = mybir.dt.bfloat16
I32 = mybir.dt.int32
ALU = mybir.AluOpType
ACT = mybir.ActivationFunctionType
AX = mybir.AxisListType

IMAGES, S, D, H, HD = 32, 37, 256, 16, 16
PATCHES, PD = 36, 768
IM = 3
R = IM * S
RP = R + 1
T = -(-IMAGES // IM)
ROWS = IMAGES * S
R_LAST = ROWS - (T - 1) * R
DC = D // 128
PC = PD // 128
HC = H // DC
K0 = max(1, int(S * 0.3))
KK = IM * K0
F = 4 * D
FC = F // 128
PAIRS = H // 2
KSEL = int(0.125 * S)
NSEL = KSEL - 1
W3 = IMAGES * NSEL
MB = 4
XA = D + 2 + S
SCALE = 1.0 / HD ** 0.5
LN_EPS = 1e-5
RMS_EPS = 1e-6
FAR = -1e30
CAUSAL = -1e10

_at = {}
_n = 0
for _name, _w in (("ident", 128), ("same", R), ("tok", S), ("before", S), ("slot0", KK),
                  ("slot1", 2 * W3 + 3), ("notcls", 1), ("iscls", 1), ("other0", KK),
                  ("causal", S), ("head", HC), ("pair0", 2), ("pair1", 2), ("cos", HD),
                  ("sin", HD), ("inv", HD), ("sign", HD), ("other1", W3)):
    _at[_name] = (_n, _w)
    _n += _w
N_CONST = _n
_vat = {}
_n = 0
for _name, _w in (("ln1_g", PC), ("ln1_b", PC), ("bq", DC), ("bk", DC), ("bi1", 1), ("wi2", 1),
                  ("bi2", 1), ("router_b", 1), ("part1", 1), ("part2", 1)):
    _vat[_name] = (_n, _w)
    _n += _w
N_VEC = _n
_rat = {}
_n = 0
for _name in ("b_proj", "ln2_g", "ln2_b", "cls", "router_w", "ln1", "ln2"):
    _rat[_name] = (_n, D)
    _n += D
N_ROW = _n
BQKV_AT = F
BO_AT, B2_AT, BP_AT, BV_AT = (F + (3 + _i) * D for _i in range(4))
N_ROWS = F + 7 * D

AT_CHOICE, AT_ATT0, AT_FFN, AT_QKV, AT_ATT1, AT_ROUTE = 5, 15, 25, 30, 39, 50


def shape_constants():
    c = np.zeros((128, N_CONST), np.float32)

    def put(name, a):
        at, w = _at[name]
        a = np.asarray(a, np.float32)
        c[:a.shape[0], at:at + w] = a

    p = np.arange(128)
    r = np.arange(R)
    im, tok = r // S, r % S
    put("ident", np.eye(128))
    put("same", im[:, None] == im[None, :])
    put("tok", tok[:, None] == np.arange(S))
    put("before", np.arange(S) < tok[:, None])
    k = np.arange(KK)
    put("slot0", np.where(im[:, None] == k // K0, k % K0, -1))
    put("other0", np.where(im[:, None] == k // K0, 0.0, FAR))
    g = np.arange(2 * W3 + 3) - (T - 1) * IM * NSEL
    put("slot1", np.where(im[:, None] == g // NSEL, g % NSEL, -1))
    put("notcls", (tok != 0)[:, None])
    put("iscls", (tok == 0)[:, None])
    put("causal", np.where(np.arange(S) <= tok[:, None], 0.0, CAUSAL))
    put("head", (p[:, None] % 128) // HD == np.arange(HC))
    put("pair0", (p[:2 * KK, None] // KK) == np.arange(2))
    put("pair1", (p[:2 * S, None] // S) == np.arange(2))
    half = HD // 2
    inv = (1.0 / np.float32(10000.0) ** (np.arange(half, dtype=np.float32) * np.float32(2.0 / HD))).astype(np.float32)
    ang = (tok.astype(np.float32)[:, None] * inv[None, :]).astype(np.float32)
    put("cos", np.repeat(np.cos(ang), 2, axis=1))
    put("sin", (np.sin(ang)[:, :, None] * np.array([-1.0, 1.0])).reshape(R, HD))
    put("inv", np.tile(np.concatenate([inv, inv]), (128, 1)))
    put("sign", np.tile(np.concatenate([-np.ones(half), np.ones(half)]), (128, 1)))
    w = np.arange(W3)
    put("other1", np.where(w[:, None] // NSEL == w // NSEL, 0.0, FAR))
    return c


def vit_tower(nc, patches, W_proj, consts, vectors, rows, wide_rows, pos3, wqT, wkT, wvT, woT, wi1T,
              W1T, W2T, wqkv1, wp1, mask, positions, wqkv2, wo2, w1f, w2f, out):
    with ExitStack() as ctx:
        def sb(name, shape, dt=F32):
            return ctx.enter_context(nc.sbuf_tensor(name, shape, dt))

        def sem(name):
            return ctx.enter_context(nc.semaphore(name))

        ps = ctx.enter_context(nc.psum_tensor("ps", [128, 8, 512], F32))

        cst = sb("cst", [128, N_CONST])
        vec = sb("vec", [128, N_VEC])
        row = sb("row", [128, N_ROW])
        pos = sb("pos", [R, D])
        early = sb("early", [128, PC * D + 4 * DC * D])
        wi1 = sb("wi1", [128, DC, 128])
        wide = sb("wide", [128, 2 * FC * D])
        w1q = sb("w1q", [128, DC, F], F32R)
        w2q = sb("w2q", [128, FC, D], F32R)
        wqkv = sb("wqkv", [128, DC, 3 * D])
        wp = sb("wp", [128, DC, D])
        wqkv_l = sb("wqkv_l", [128, DC, 3 * D])
        wo_l = sb("wo_l", [128, DC, D])
        maskrow = sb("maskrow", [R, 2, S])
        posi = sb("posi", [R, 2, 1], I32)

        ident_b = sb("ident_b", [R, R], BF16)
        other_b = sb("other_b", [R, KK], BF16)
        causal_b = sb("causal_b", [R, S], BF16)
        ones = sb("ones", [128, 128])
        ones_b = sb("ones_b", [3, 128], BF16)
        mhalf = sb("mhalf", [128, 1])
        bp0 = sb("bp0", [R, D])
        posb = sb("posb", [R, D])
        brow = sb("brow", [3, N_ROWS], BF16)
        gam = sb("gam", [128, 8])

        h = sb("h", [R, T, D])
        xa = sb("xa", [R, T, XA])
        xT = sb("xT", [128, T, DC, RP])
        q6 = sb("q6", [128, T, DC, RP])
        v1 = sb("v1", [R, T, D])
        ohT = sb("ohT", [W3, T, RP])
        st = sb("st", [R, T, 12])
        mv = sb("mv", [R, T, 2])
        rs = sb("rs", [R, T, 2])
        xhi = sb("xhi", [128, 2, DC, RP], F32R)
        xlo = sb("xlo", [128, 2, DC, RP], F32R)
        hhi = sb("hhi", [128, 2, FC, RP], F32R)
        hlo = sb("hlo", [128, 2, FC, RP], F32R)

        A_SIZE, B_SIZE = 6608, 3664
        arena_a = sb("arena_a", [128, A_SIZE])
        arena_b = sb("arena_b", [128, B_SIZE])

        def cut(whole, at, shape):
            n = int(np.prod(shape[1:]))
            ap = whole[0:shape[0], at[0]:at[0] + n]
            at[0] += n
            assert at[0] <= whole.shape[1], (at, whole.shape)
            if len(shape) == 2:
                return ap
            names = "abcd"[:len(shape) - 1]
            sizes = {x: v for x, v in zip(names, shape[1:])}
            return ap.rearrange(f"p ({' '.join(names)}) -> p {' '.join(names)}", **sizes)

        at = [0]
        w_proj = cut(early, at, [128, PC, D])
        wq0, wk0, wv0, wo0 = (cut(early, at, [128, DC, D]) for _ in range(4))
        kbd7 = cut(early, [0], [128, 2, DC, IM * HC * S])
        at = [0]
        w1raw = cut(wide, at, [128, DC, F])
        w2raw = cut(wide, at, [128, FC, D])
        at = [0]
        vm7 = cut(wide, at, [2 * S, 3, IM * D])
        PT7 = cut(wide, at, [2 * S, 2, PAIRS, RP])
        at = [0]
        pat = cut(arena_a, at, [R, 3, PD])
        pT = cut(arena_a, at, [128, 2, PC, RP])
        zb = cut(arena_a, at, [R, 2, D])
        zn = cut(arena_a, at, [R, 2, D])
        at = [0]
        qT0 = cut(arena_a, at, [128, 2, DC, RP])
        kbd0 = cut(arena_a, at, [128, 2, DC, HC * KK])
        vm0 = cut(arena_a, at, [2 * KK, 5, D])
        pr0 = cut(arena_a, at, [R, 3, H * KK])
        PT0 = cut(arena_a, at, [2 * KK, 2, PAIRS, RP])
        oT0 = cut(arena_a, at, [128, 2, DC, RP])
        sm0 = sb("sm0", [R, 2, 3, H])
        at = [0]
        xT6 = cut(arena_a, at, [128, 2, DC, RP])
        rot = cut(arena_a, at, [R, 2, 2, 2 * D])
        at = [0]
        hT = cut(arena_b, at, [128, 2, RP])
        rk0 = cut(arena_b, at, [R, 2, 8 + 4 * S])
        oh0 = cut(arena_b, at, [R, 2, KK])
        xsT = cut(arena_b, at, [128, T, DC, 2 * KK])
        at = [0]
        qTm = cut(arena_b, at, [128, 2, DC, IM, RP])
        pr7 = cut(arena_b, at, [R, 3, H * S])
        oT7 = cut(arena_b, at, [128, 2, DC, RP])
        sm7 = cut(arena_b, at, [R, 2, 3, H])

        names = """cst vec row pos wproj w0 w1raw w2raw wl1 mrow w2nd wlast brows stored
            pool_set cast posb biasps bp0 gw absum gamps thr low quant part_hi part_lo
            st1 rs1 xh1 tr1 xT1 pj z rs2 zn h0
            ln_stats0 ln_stats1 ln_stats2 ln_stats3 ln_scale0 ln_scale1 ln_scale2 ln_scale3 xn0 xn1 xn2 xn3 T2 xT2 hidp hid imp vE G rank gx xs
            q kv q0 kb0 vm0 S0 smx0 ex0 sum0 pn0 pt0 PT0 pv0 oT0 op0 h4
            T5 xhi xlo w1a w1b hia hib loa lob w2 h5
            T6 xT6 qkv rope rope_sum v6 tq tqe tke qz
            qm7 kbA kbB vm7 S7 smx7 ex7 sum7 pn7 pt7 PT7 pv7 oT7 op7 h7
            rw G9 rank9 acc oht ohte base aug
            tv sc fin t_ang t_sin t_hn t_T t_hnT t_mrow t_mm t_qkv t_v t_rot t_Tr t_qkT t_kbd t_S t_sub
            t_exp t_pT t_PT t_O t_o t_To t_oT t_wo t_w1 t_g t_w2 t_y t_put""".split()
        s = {n: sem(n) for n in names}
        s_pat = [sem(f"pat{i}") for i in range(3)]
        s_vrep = [sem(f"vrep{i}") for i in range(3)]
        N_ST1, N_RS1, N_Z, N_RS2, N_H0, N_LNA, N_LNR, N_VE, N_RANK, N_SUM, N_RW, N_RANK9 = \
            3, 2, 3, 3, 2, 2, 2, 2, 5, 2, 3, 8

        def C(name, rows=128):
            a, w = _at[name]
            return cst[0:rows, a:a + w]

        def V(name):
            a, w = _vat[name]
            return vec[:, a:a + w]

        def B(name, rows=R):
            a, w = _rat[name]
            return row[0:rows, a:a + w]

        def spread(ap, axis, shape):
            return ap.unsqueeze(axis).broadcast_to(shape)

        def link(eng, name, start):
            n = [start]

            def f(ins, wait=True):
                n[0] += 1
                ins.then_inc(s[name], 1)
                if wait:
                    eng.wait_ge(s[name], n[0])
            return f

        def sweep(*steps):
            steps = [x if len(x) == 3 else (*x, T) for x in steps]
            for turn in range(max(start + n for _, start, n in steps)):
                for step, start, n in steps:
                    if 0 <= turn - start < n:
                        step(turn - start)

        at = [0]
        t_x = cut(arena_a, at, [W3, XA])
        t_hn = cut(arena_a, at, [W3, D])
        t_hnT = cut(arena_a, at, [128, DC, W3])
        t_rot = cut(arena_a, at, [W3, 2, 2 * D])
        t_v = cut(arena_a, at, [W3, D])
        t_kbd = cut(arena_a, at, [128, DC, HC * W3])
        t_g = cut(arena_a, at, [128, FC, W3])
        t_cmp = cut(arena_a, at, [S, 2 * W3])
        junk = cut(arena_a, at, [R, D])
        rk9 = cut(arena_a, at, [R, 2, 12 + 4 * S])
        oh9 = cut(arena_a, at, [R, 2, W3])
        at = [0]
        t_p = cut(arena_b, at, [W3, H * W3])
        t_PT = cut(arena_b, at, [W3, H * W3])
        at = [0]
        xTflat = xT[:].rearrange("p t c r -> p (t c r)")
        t_qkT = cut(xTflat, at, [128, 4, W3])
        t_oT = cut(xTflat, at, [128, DC, W3])
        t_sc = cut(xTflat, at, [W3, 16])
        t_f = cut(xTflat, at, [W3, 6, HD])
        t_mm = cut(xTflat, at, [W3, W3])
        t_mx = cut(xTflat, at, [W3, 3, H])
        t_o = cut(xTflat, at, [W3, D])
        t_x1 = cut(xTflat, at, [W3, D])
        t_y = cut(xTflat, at, [W3, D])

        q6flat = q6[:].rearrange("p t c r -> p (t c r)")
        bias_rows = cut(v1[:].rearrange("p t d -> p (t d)"), [0], [3, N_ROWS])
        gW = cut(q6flat, [0], [128, PC, D])
        low = cut(q6flat, [0], [128, 2, F])

        block = ctx.enter_context(nc.Block())

        @block.sync
        def _(sp):
            def load(dst, src, on):
                sp.dma_start(dst, src).then_inc(on, 16)

            def matrix(dst, src, on):
                load(dst, src.rearrange("(c p) n -> p c n", p=128), s[on])

            def patch(t):
                if t >= 3:
                    sp.wait_ge(s["tr1"], t - 2)
                load(pat[:, t % 3, :], patches[t * R:(t + 1) * R, :], s_pat[t % 3])

            patch(0)
            load(cst[:], consts, s["cst"])
            load(vec[:], vectors, s["vec"])
            matrix(w_proj, W_proj, "wproj")
            patch(1)
            load(row[:], rows[0, :].partition_broadcast(128), s["row"])
            load(pos[:], pos3, s["pos"])
            patch(2)
            matrix(wi1[:], wi1T, "w0")
            for dst, src in ((wq0, wqT), (wk0, wkT), (wv0, wvT), (wo0, woT)):
                matrix(dst, src, "w0")
            load(bias_rows, wide_rows[0, :].partition_broadcast(3), s["brows"])
            patch(3)
            patch(4)
            matrix(w1raw, W1T, "w1raw")
            matrix(w2raw, W2T, "w2raw")
            for t in range(5, T):
                patch(t)
            matrix(wqkv[:], wqkv1, "wl1")
            matrix(wp[:], wp1, "wl1")
            for i in range(IM):
                a = slice(i * S, (i + 1) * S)
                for n, batch in ((0, i), (1, MB - 1)):
                    load(maskrow[a, n, :], mask[batch, 0, 0:S, 0:S], s["mrow"])
                    load(posi[a, n, :], positions[batch, 0:S].rearrange("(s a) -> s a", a=1), s["mrow"])
            matrix(wqkv_l[:], wqkv2, "w2nd")
            matrix(wo_l[:], wo2, "w2nd")
            for t in range(T):
                sp.wait_ge(s["v6"], t + 1)
                if t >= 3:
                    sp.wait_ge(s["pv7"], t - 2)
                else:
                    sp.wait_ge(s["quant"], 4)
                for i in range(IM):
                    for j in range(2):
                        load(vm7[j * S:(j + 1) * S, t % 3, i * D:(i + 1) * D],
                             v1[i * S:(i + 1) * S, t, :], s_vrep[t % 3])
            sp.wait_ge(s["pv7"], T)
            matrix(w1raw, w1f, "wlast")
            matrix(w2raw, w2f, "wlast")
            for t in range(T):
                n = R if t < T - 1 else R_LAST
                sp.wait_ge(s["fin"], t + 1)
                load(out[t * R:t * R + n, :], h[0:n, t, :], s["stored"])
            sp.wait_ge(s["stored"], 16 * T)

        @block.gpsimd
        def _(pool):
            g = nc.gpsimd

            def rsqrt(t, on, n_on, name, n_name, mask_cls=False):
                pool.wait_ge(s[on], n_on * (t + 1))
                l = link(pool, name, n_name * t)
                l(g.tensor_scalar(rs[:, t, 0:1], mv[:, t, 1:2], LN_EPS, None, ALU.add))
                l(g.tensor_tensor(rs[:, t, 1:2], rs[:, t, 0:1], mhalf[0:R, :], ALU.pow), mask_cls)
                if mask_cls:
                    l(g.tensor_scalar(rs[:, t, 1:2], rs[:, t, 1:2], C("notcls", R), None, ALU.mult), False)

            def ln_scale(layer):
                return lambda t: rsqrt(t, f"ln_stats{layer}", N_LNA, f"ln_scale{layer}", N_LNR)

            def pairs_apart(dst, src, name, rows_n, n, sem_name):
                g.tensor_tensor(dst.rearrange("p (n j d) -> p n j d", j=2, d=HD),
                                src.rearrange("p (n j d) -> p n j d", j=2, d=HD),
                                C(name, rows_n).unsqueeze(1).unsqueeze(3).broadcast_to([rows_n, n, 2, HD]),
                                ALU.mult).then_inc(s[sem_name], 1)

            g.memset(mhalf[:], -0.5).then_inc(s["pool_set"], 1)
            g.memset(ones[:], 1.0).then_inc(s["pool_set"], 1)
            g.memset(ones_b[:], 1.0).then_inc(s["pool_set"], 1)
            g.memset(xhi[:, :, :, R:RP].bitcast(F32), 0.0).then_inc(s["pool_set"], 1)
            g.memset(xlo[:, :, :, R:RP].bitcast(F32), 0.0).then_inc(s["pool_set"], 1)
            pool.wait_ge(s["pool_set"], 5)
            pool.wait_ge(s["cst"], 16)
            g.tensor_copy(ident_b[:], C("ident", R)[:, 0:R]).then_inc(s["cast"], 1)
            g.tensor_copy(other_b[:], C("other0", R)).then_inc(s["cast"], 1)
            g.tensor_copy(causal_b[:], C("causal", R)).then_inc(s["cast"], 1)

            def h0(t):
                if t == 0:
                    pool.wait_ge(s["row"], 16)
                    pool.wait_ge(s["pos"], 16)
                    l = link(pool, "posb", 0)
                    l(g.tensor_scalar(posb[:], B("ln2_b"), C("notcls", R), None, ALU.mult), False)
                    l(g.tensor_scalar(B("cls"), B("cls"), C("iscls", R), None, ALU.mult))
                    l(g.tensor_tensor(posb[:], posb[:], pos[:], ALU.add))
                    l(g.tensor_tensor(posb[:], posb[:], B("cls"), ALU.add))
                pool.wait_ge(s["zn"], t + 1)
                l = link(pool, "h0", N_H0 * t)
                l(g.tensor_tensor(zn[:, t % 2, :], zn[:, t % 2, :], B("ln2_g"), ALU.mult))
                l(g.tensor_tensor(h[:, t, :], zn[:, t % 2, :], posb[:], ALU.add), False)

            def low_(n):
                if n == 0:
                    pool.wait_ge(s["thr"], 2)
                    pool.wait_ge(s["pj"], T)
                if n >= 2:
                    pool.wait_ge(s["quant"], n - 1)
                g.tensor_scalar(low[:, n % 2, :], wide[:, n * F:(n + 1) * F], gam[:, 6 + n // 2:7 + n // 2], None,
                                ALU.is_lt).then_inc(s["low"], 1)

            def pn0(t):
                pool.wait_ge(s["sum0"], N_SUM * (t + 1))
                p3 = pr0[:, t % 3, :].rearrange("p (n k) -> p n k", k=KK)
                g.tensor_tensor(p3, p3, spread(sm0[:, t % 2, 2, :], 2, [R, H, KK]), ALU.mult).then_inc(s["pn0"], 1)

            def augment(n):
                if n == 0:
                    pool.wait_ge(s["mrow"], 16 * 4 * IM)
                a, b = ((0, 1), (1, T))[n]
                g.tensor_copy(xa[:, a:b, D + 1:D + 2], posi[:, n:n + 1, :].broadcast_to([R, b - a, 1])).then_inc(s["aug"], 1)
                g.tensor_copy(xa[:, a:b, D + 2:XA], maskrow[:, n:n + 1, :].broadcast_to([R, b - a, S])).then_inc(s["aug"], 1)

            def clear(n):
                pool.wait_ge(s["kv"], T)
                g.memset(qTm[:], 0.0).then_inc(s["qz"], 1)

            def rope_sum(t):
                pool.wait_ge(s["rope"], 2 * (t + 1))
                g.tensor_tensor(rot[:, t % 2, 0, :], rot[:, t % 2, 0, :], rot[:, t % 2, 1, :],
                                ALU.add).then_inc(s["rope_sum"], 1)

            def kbA(t):
                pool.wait_ge(s["tke"], t + 1)
                if t == 0:
                    pool.wait_ge(s["op0"], T)
                if t >= 2:
                    pool.wait_ge(s["S7"], t - 1)
                g.tensor_tensor(kbd7[:, t % 2, 0, :].rearrange("p (i n k) -> p i n k", i=IM, n=HC),
                                xT[:, t, 0, 0:R].rearrange("p (i k) -> p i k", i=IM).unsqueeze(2).broadcast_to([128, IM, HC, S]),
                                C("head").unsqueeze(1).unsqueeze(3).broadcast_to([128, IM, HC, S]),
                                ALU.mult).then_inc(s["kbA"], 1)

            def vm7_(t):
                pool.wait_ge(s_vrep[t % 3], 16 * 2 * IM * (t // 3 + 1))
                pairs_apart(vm7[:, t % 3, :], vm7[:, t % 3, :], "pair1", 2 * S, IM * PAIRS, "vm7")

            def pn7(t):
                pool.wait_ge(s["sum7"], N_SUM * (t + 1))
                p3 = pr7[:, t % 3, :].rearrange("p (n k) -> p n k", k=S)
                g.tensor_tensor(p3, p3, spread(sm7[:, t % 2, 2, :], 2, [R, H, S]), ALU.mult).then_inc(s["pn7"], 1)

            sweep((lambda t: rsqrt(t, "st1", N_ST1, "rs1", N_RS1), 0),
                  (lambda t: rsqrt(t, "z", N_Z, "rs2", N_RS2, True), 3), (h0, 4),
                  (ln_scale(0), AT_CHOICE), (low_, 15, 4),
                  (pn0, AT_ATT0 + 3), (augment, AT_FFN + 1, 2), (ln_scale(1), AT_FFN), (clear, AT_QKV + 1, 1),
                  (rope_sum, AT_QKV + 3), (ln_scale(2), AT_QKV),
                  (pn7, AT_ATT1 + 3), (vm7_, AT_ATT1 + 4), (kbA, AT_ATT1),
                  (ln_scale(3), AT_ROUTE))

            for i in range(2):
                pool.wait_ge(s["sc"], 1 + 3 * i)
                g.tensor_scalar(t_sc[:, 2 + 4 * i:3 + 4 * i], t_sc[:, 1 + 4 * i:2 + 4 * i], 1.0 / D, RMS_EPS,
                                ALU.mult, ALU.add).then_inc(s["sc"], 1)
                pool.wait_ge(s["sc"], 2 + 3 * i)
                g.tensor_tensor(t_sc[:, 3 + 4 * i:4 + 4 * i], t_sc[:, 2 + 4 * i:3 + 4 * i], mhalf[0:W3, :],
                                ALU.pow).then_inc(s["sc"], 1)

        @block.vector
        def _(dve):
            v = nc.vector

            def norm_stats(t, layer, on, n_on):
                dve.wait_ge(s[on], n_on * (t + 1))
                l = link(dve, f"ln_stats{layer}", N_LNA * t)
                l(v.bn_stats(st[:, t, 0:6], h[:, t, :]))
                l(v.bn_aggr(mv[:, t, :], st[:, t, 0:6]), False)

            def norm(t, layer):
                dve.wait_ge(s[f"ln_scale{layer}"], N_LNR * (t + 1))
                v.tensor_scalar(xa[:, t, 0:D], h[:, t, :], mv[:, t, 0:1], rs[:, t, 1:2],
                                ALU.subtract, ALU.mult).then_inc(s[f"xn{layer}"], 1)

            def ranks(l, rk, G):
                l(v.tensor_tensor_reduce(rk[:, 119:119 + S], G, C("tok", R), 1.0, 0.0, ALU.mult, ALU.add,
                                         rk[:, 1:2]))
                l(v.tensor_scalar(rk[:, 45:45 + S], G, rk[:, 1:2], None, ALU.is_gt), False)
                l(v.scalar_tensor_tensor(rk[:, 82:82 + S], G, rk[:, 1:2], C("before", R), ALU.is_equal, ALU.mult))
                l(v.tensor_tensor_reduce(rk[:, 119:119 + S], rk[:, 45:45 + S], rk[:, 82:82 + S], 1.0, 0.0,
                                         ALU.add, ALU.add, rk[:, 2:3]))

            def n1(t):
                dve.wait_ge(s_pat[t % 3], 16 * (t // 3 + 1))
                l = link(dve, "st1", N_ST1 * t)
                l(v.bn_stats(st[:, t, 0:6], pat[:, t % 3, 0:PD // 2]), False)
                l(v.bn_stats(st[:, t, 6:12], pat[:, t % 3, PD // 2:PD]))
                l(v.bn_aggr(mv[:, t, :], st[:, t, :]), False)

            def x1(t):
                dve.wait_ge(s["rs1"], N_RS1 * (t + 1))
                v.tensor_scalar(pat[:, t % 3, :], pat[:, t % 3, :], mv[:, t, 0:1], rs[:, t, 1:2],
                                ALU.subtract, ALU.mult).then_inc(s["xh1"], 1)

            def z(t):
                if t == 0:
                    dve.wait_ge(s["biasps"], 1)
                    dve.wait_ge(s["row"], 16)
                    v.tensor_tensor(bp0[:], ps[0:R, 4, 0:D], B("b_proj"), ALU.add).then_inc(s["bp0"], 1)
                    dve.wait_ge(s["bp0"], 1)
                dve.wait_ge(s["pj"], t + 1)
                if t >= 2:
                    dve.wait_ge(s["zn"], t - 1)
                l = link(dve, "z", N_Z * t)
                l(v.tensor_tensor(zb[:, t % 2, :], ps[0:R, 2 + t % 2, 0:D], bp0[:], ALU.add))
                l(v.bn_stats(st[:, t, 0:6], zb[:, t % 2, :]))
                l(v.bn_aggr(mv[:, t, :], st[:, t, 0:6]), False)

            def zn_(t):
                dve.wait_ge(s["rs2"], N_RS2 * (t + 1))
                if t >= 2:
                    dve.wait_ge(s["h0"], N_H0 * (t - 1))
                v.tensor_scalar(zn[:, t % 2, :], zb[:, t % 2, :], mv[:, t, 0:1], rs[:, t, 1:2],
                                ALU.subtract, ALU.mult).then_inc(s["zn"], 1)

            def absum(n):
                dve.wait_ge(s[("w1raw", "w2raw")[n]], 16)
                v.tensor_reduce(gam[:, n:n + 1], wide[:, n * 2 * F:(n + 1) * 2 * F], AX.X, ALU.add,
                                apply_absolute_value=True).then_inc(s["absum"], 1)

            def part_lo(n):
                dve.wait_ge(s["part_hi"], n + 1)
                v.scalar_tensor_tensor(bias_rows, brow[:], V(f"part{n + 1}")[0:3, :], bias_rows, ALU.mult,
                                       ALU.subtract).then_inc(s["part_lo"], 1)

            def vE(t):
                dve.wait_ge(s["imp"], t + 1)
                rk = rk0[:, t % 2, :]
                l = link(dve, "vE", N_VE * t)
                l(v.tensor_scalar(rk[:, 0:1], ps[0:R, 6, 256 + 2 * (t % 2):256 + 2 * (t % 2) + 1], V("bi2")[0:R, :],
                                  None, ALU.add))
                l(v.tensor_scalar(rk[:, 8:8 + S], C("tok", R), rk[:, 0:1], None, ALU.mult), False)

            def rank(t):
                dve.wait_ge(s["G"], t + 1)
                dve.wait_ge(s["imp"], min(t + 2, T))
                rk = rk0[:, t % 2, :]
                l = link(dve, "rank", N_RANK * t)
                ranks(l, rk, ps[0:R, 6, 0:S])
                if t >= 2:
                    dve.wait_ge(s["gx"], t - 1)
                l(v.tensor_scalar(oh0[:, t % 2, :], C("slot0", R), rk[:, 2:3], None, ALU.is_equal), False)

            def scales(n):
                dve.wait_ge(s["gamps"], 1)
                l = link(dve, "thr", 0)
                l(v.tensor_scalar(gam[:, 4:6], ps[:, 3, 508:510], 0.5 / (D * F), 0.5e-5, ALU.mult, ALU.add))
                l(v.tensor_scalar(gam[:, 6:8], gam[:, 4:6], -1.0, None, ALU.mult), False)

            def quantize(n):
                dve.wait_ge(s["low"], n + 1)
                dst = (w1q, w2q)[n // 2][:].rearrange("p c n -> p (c n)")
                v.scalar_tensor_tensor(dst[:, n % 2 * F:(n % 2 + 1) * F], wide[:, n * F:(n + 1) * F],
                                       gam[:, 4 + n // 2:5 + n // 2], low[:, n % 2, :], ALU.is_gt, ALU.subtract
                                       ).then_inc(s["quant"], 1)

            def kb0(t):
                dve.wait_ge(s["kv"], t + 1)
                if t == 0:
                    dve.wait_ge(s["h0"], N_H0 * T)
                if t >= 2:
                    dve.wait_ge(s["S0"], t - 1)
                for m in range(DC):
                    at_ = 256 + 64 * m
                    last = v.scalar_tensor_tensor(
                        kbd0[:, t % 2, m, :].rearrange("p (n k) -> p n k", k=KK),
                        spread(ps[:, 1, at_:at_ + KK], 1, [128, HC, KK]), V("bk")[:, m:m + 1],
                        spread(C("head"), 2, [128, HC, KK]), ALU.add, ALU.mult)
                last.then_inc(s["kb0"], 1)

            def vm0_(t):
                dve.wait_ge(s["kv"], t + 1)
                if t >= 5:
                    dve.wait_ge(s["pv0"], t - 4)
                v.tensor_tensor(vm0[:, t % 5, :].rearrange("p (n j d) -> p n j d", j=2, d=HD),
                                ps[0:2 * KK, 1, 0:D].rearrange("p (n j d) -> p n j d", j=2, d=HD),
                                C("pair0", 2 * KK).unsqueeze(1).unsqueeze(3).broadcast_to([2 * KK, PAIRS, 2, HD]),
                                ALU.mult).then_inc(s["vm0"], 1)

            def softmax_top(t, S_ps, sm, pr, on, pt, name, width):
                dve.wait_ge(s[on], t + 1)
                l = link(dve, name, 2 * t)
                mx = sm[:, t % 2, 0, :].rearrange("p (c n) -> p c n", c=DC)
                l(v.tensor_reduce(mx, S_ps, AX.X, ALU.max))
                if t >= 3:
                    dve.wait_ge(s[pt], t - 2)
                l(v.tensor_tensor(pr[:, t % 3, :].rearrange("p (c n k) -> p c n k", c=DC, k=width), S_ps,
                                  spread(mx, 3, [R, DC, HC, width]), ALU.subtract), False)

            def softmax_sum(t, sm, pr, on, pn, name, width):
                dve.wait_ge(s[on], t + 1)
                l = link(dve, name, N_SUM * t)
                l(v.tensor_reduce(sm[:, t % 2, 1, :], pr[:, t % 3, :].rearrange("p (n k) -> p n k", k=width),
                                  AX.X, ALU.add))
                if t >= 2:
                    dve.wait_ge(s[pn], t - 1)
                l(v.reciprocal(sm[:, t % 2, 2, :], sm[:, t % 2, 1, :]), False)

            def residual(t, layer, bank, on, name):
                dve.wait_ge(s[on], t + 1)
                v.tensor_tensor(h[:, t, :], ps[0:R, bank, 0:D], h[:, t, :], ALU.add).then_inc(s[name], 1)

            S0_ps = ps[0:R, 2:4, 0:HC * KK].rearrange("p c (n k) -> p c n k", k=KK)

            def xlo_(t):
                dve.wait_ge(s["xhi"], t + 1)
                v.tensor_tensor(xlo[:, t % 2, :, 0:R], ps[:, 0, 0:DC * RP].rearrange("p (c r) -> p c r", c=DC)[:, :, 0:R],
                                xhi[:, t % 2, :, 0:R].bitcast(F32), ALU.subtract).then_inc(s["xlo"], 1)

            def hlo_(t, half, on, name):
                dve.wait_ge(s[on], t + 1)
                f = slice(half * FC // 2, (half + 1) * FC // 2)
                v.scalar_tensor_tensor(hlo[:, t % 2, f, :].rearrange("p c r -> p (c r)"),
                                       ps[:, 1 + half, 0:FC // 2 * RP], 0.0,
                                       hhi[:, t % 2, f, :].rearrange("p c r -> p (c r)").bitcast(F32),
                                       ALU.max, ALU.subtract).then_inc(s[name], 1)

            def rope(t):
                dve.wait_ge(s["qkv"], t + 1)
                if t >= 2:
                    dve.wait_ge(s["tq"], t - 1)
                n = 2 * H
                qk = ps[0:R, 5, :].rearrange("p (n e o) -> p n e o", n=n, o=2)
                v.tensor_tensor(rot[:, t % 2, 0, :].rearrange("p (n d) -> p n d", n=n),
                                ps[0:R, 5, :].rearrange("p (n d) -> p n d", n=n),
                                spread(C("cos", R), 1, [R, n, HD]), ALU.mult).then_inc(s["rope"], 1)
                v.tensor_tensor(rot[:, t % 2, 1, :].rearrange("p (n e o) -> p n e o", n=n, o=2), qk[:, :, :, ::-1],
                                C("sin", R).rearrange("p (e o) -> p e o", o=2).unsqueeze(1).broadcast_to([R, n, HD // 2, 2]),
                                ALU.mult).then_inc(s["rope"], 1)

            def kbB(t):
                dve.wait_ge(s["tke"], t + 1)
                if t == 0:
                    dve.wait_ge(s["op0"], T)
                if t >= 2:
                    dve.wait_ge(s["S7"], t - 1)
                v.tensor_tensor(kbd7[:, t % 2, 1, :].rearrange("p (i n k) -> p i n k", i=IM, n=HC),
                                xT[:, t, 1, 0:R].rearrange("p (i k) -> p i k", i=IM).unsqueeze(2).broadcast_to([128, IM, HC, S]),
                                C("head").unsqueeze(1).unsqueeze(3).broadcast_to([128, IM, HC, S]),
                                ALU.mult).then_inc(s["kbB"], 1)

            def S7_ps(t):
                b = 2 * (t % 2)
                return ps[0:R, b:b + 2, 0:HC * S].rearrange("p c (n k) -> p c n k", k=S)

            def rw(t):
                l = link(dve, "rw", N_RW * t)
                dve.wait_ge(s["xn3"], t + 1)
                l(v.tensor_tensor_reduce(junk[:], xa[:, t, 0:D], B("router_w"), 1.0, 0.0, ALU.mult, ALU.add,
                                         rk9[:, t % 2, 0:1]))
                l(v.tensor_scalar(xa[:, t, D:D + 1], rk9[:, t % 2, 0:1], V("router_b")[0:R, :], None, ALU.add))
                l(v.tensor_scalar(rk9[:, t % 2, 8:8 + S], C("tok", R), xa[:, t, D:D + 1], None, ALU.mult), False)

            def rank9(t):
                dve.wait_ge(s["G9"], t + 1)
                rk = rk9[:, t % 2, :]
                G = ps[0:R, 0, 64 * (t % 2):64 * (t % 2) + S]
                l = link(dve, "rank9", N_RANK9 * t)
                ranks(l, rk, G)
                l(v.tensor_scalar(rk[:, 45:45 + S], G, rk[:, 1:2], None, ALU.is_ge))
                l(v.tensor_reduce(rk[:, 3:4], rk[:, 45:45 + S], AX.X, ALU.add))
                if t >= 2:
                    dve.wait_ge(s["oht"], t - 1)
                a = (T - 1 - t) * IM * NSEL
                l(v.tensor_scalar(oh9[:, t % 2, :], C("slot1", R)[:, a:a + W3], rk[:, 2:3], None, ALU.is_equal), False)
                l(v.tensor_scalar(rk[:, 4:5], rk[:, 3:4], KSEL - 0.5, None, ALU.is_gt))
                v.scalar_tensor_tensor(h[:, t, :], xa[:, t, 0:D], rk[:, 4:5], h[:, t, :], ALU.mult,
                                       ALU.add).then_inc(s["base"], 1)

            sweep((lambda t: residual(t, 2, 7, "op7", "h7"), AT_ATT1 + 7),
                  (lambda t: residual(t, 1, 3, "w2", "h5"), AT_FFN + 4),
                  (lambda t: residual(t, 0, 7, "op0", "h4"), AT_ATT0 + 7),
                  (x1, 1), (n1, 0), (z, 3), (zn_, 4), (absum, 8, 2), (part_lo, 7, 1), (lambda n: part_lo(1), 9, 1),
                  (lambda t: norm(t, 0), AT_CHOICE + 1), (lambda t: norm_stats(t, 0, "h0", N_H0), AT_CHOICE),
                  (vE, AT_CHOICE + 3), (rank, AT_CHOICE + 4), (scales, 14, 1), (quantize, 16, 4),
                  (lambda t: softmax_sum(t, sm0, pr0, "ex0", "pn0", "sum0", KK), AT_ATT0 + 3),
                  (kb0, AT_ATT0), (vm0_, AT_ATT0),
                  (lambda t: softmax_top(t, S0_ps, sm0, pr0, "S0", "pt0", "smx0", KK), AT_ATT0 + 1),
                  (lambda t: norm(t, 1), AT_FFN + 1), (lambda t: norm_stats(t, 1, "h4", 1), AT_FFN),
                  (lambda t: hlo_(t, 0, "hia", "loa"), AT_FFN + 2), (lambda t: hlo_(t, 1, "hib", "lob"), AT_FFN + 2),
                  (xlo_, AT_FFN + 1),
                  (lambda t: norm(t, 2), AT_QKV + 1), (lambda t: norm_stats(t, 2, "h5", 1), AT_QKV),
                  (rope, AT_QKV + 2),
                  (lambda t: softmax_sum(t, sm7, pr7, "ex7", "pn7", "sum7", S), AT_ATT1 + 3),
                  (lambda t: softmax_top(t, S7_ps(t), sm7, pr7, "S7", "pt7", "smx7", S), AT_ATT1 + 2),
                  (kbB, AT_ATT1),
                  (lambda t: norm(t, 3), AT_ROUTE + 1), (lambda t: norm_stats(t, 3, "h7", 1), AT_ROUTE),
                  (rank9, AT_ROUTE + 2), (rw, AT_ROUTE + 1))

            l = link(dve, "tv", 0)
            x_ = t_x[:, 0:D]
            dve.wait_ge(s["acc"], T)
            l(v.tensor_copy(t_x, ps[0:W3, 1, 0:XA]))
            l(v.tensor_copy(t_cmp[:, 0:W3], ps[0:S, 2, 0:W3]))
            v.tensor_tensor_reduce(t_hn, x_, x_, 1.0, 0.0, ALU.mult, ALU.add, t_sc[:, 1:2]).then_inc(s["sc"], 1)
            f = [t_f[:, i, :] for i in range(6)]
            turn = (6.28125, 0.0019350051879882812, 3.0199159819e-07)
            magic = 12582912.0
            l(v.tensor_scalar(f[0], C("inv", W3), t_x[:, D + 1:D + 2], None, ALU.mult))
            l(v.tensor_scalar(f[1], f[0], float(0.5 / np.pi), magic, ALU.mult, ALU.add))
            l(v.tensor_scalar(f[1], f[1], -magic, None, ALU.add))
            for part in turn:
                l(v.scalar_tensor_tensor(f[0], f[1], -part, f[0], ALU.mult, ALU.add))
            l(v.tensor_scalar(f[0], f[0], -3.1415925, 3.1415925, ALU.max, ALU.min))
            l(v.scalar_tensor_tensor(f[2], f[0], -1.0, f[0], ALU.mult, ALU.max))
            v.tensor_scalar(f[2], f[2], -1.0, float(np.pi / 2), ALU.mult, ALU.add).then_inc(s["t_ang"], 1)
            dve.wait_ge(s["sc"], 3)
            v.scalar_tensor_tensor(t_hn, x_, t_sc[:, 3:4], B("ln1", W3), ALU.mult, ALU.mult).then_inc(s["t_hn"], 1)
            dve.wait_ge(s["t_T"], 1)
            v.tensor_copy(t_cmp[:, W3:2 * W3], ps[0:S, 5, 0:W3]).then_inc(s["t_mrow"], 1)
            dve.wait_ge(s["t_sin"], 2)
            l(v.tensor_tensor(f[3], f[3], C("sign", W3), ALU.mult))
            dve.wait_ge(s["t_mm"], 1)
            l(v.scalar_tensor_tensor(t_mm, ps[0:W3, 5, 0:W3], 1.0 / SCALE, C("other1", W3), ALU.mult, ALU.add))
            dve.wait_ge(s["t_qkv"], 1)
            n = 2 * H
            l(v.tensor_tensor(t_rot[:, 0, :].rearrange("p (n d) -> p n d", n=n),
                              ps[0:W3, 6, :].rearrange("p (n d) -> p n d", n=n),
                              spread(f[4], 1, [W3, n, HD]), ALU.mult), False)
            l(v.tensor_tensor(t_rot[:, 1, :].rearrange("p (n a d) -> p n a d", n=n, a=2),
                              ps[0:W3, 6, :].rearrange("p (n a d) -> p n a d", n=n, a=2)[:, :, ::-1, :],
                              f[3].rearrange("p (a d) -> p a d", a=2).unsqueeze(1).broadcast_to([W3, n, 2, HD // 2]),
                              ALU.mult))
            v.tensor_tensor(t_rot[:, 0, :], t_rot[:, 0, :], t_rot[:, 1, :], ALU.add).then_inc(s["t_rot"], 1)
            dve.wait_ge(s["t_qkT"], 1)
            for m in range(DC):
                last = v.tensor_tensor(t_kbd[:, m, :].rearrange("p (n k) -> p n k", n=HC),
                                       spread(t_qkT[:, DC + m, :], 1, [128, HC, W3]),
                                       spread(C("head"), 2, [128, HC, W3]), ALU.mult)
            last.then_inc(s["t_kbd"], 1)
            dve.wait_ge(s["t_S"], 1)
            p3 = t_p.rearrange("p (n k) -> p n k", k=W3)
            p4 = t_p.rearrange("p (g n k) -> p g n k", g=4, k=W3)
            l(v.tensor_tensor(p4, ps[0:W3, 0:4, 0:4 * W3].rearrange("p g (n k) -> p g n k", k=W3),
                              t_mm.unsqueeze(1).unsqueeze(1).broadcast_to([W3, 4, 4, W3]), ALU.add))
            l(v.tensor_reduce(t_mx[:, 0, :], p3, AX.X, ALU.max))
            v.tensor_tensor(p3, p3, spread(t_mx[:, 0, :], 2, [W3, H, W3]), ALU.subtract).then_inc(s["t_sub"], 1)
            dve.wait_ge(s["t_exp"], 1)
            l(v.tensor_reduce(t_mx[:, 1, :], p3, AX.X, ALU.add))
            l(v.reciprocal(t_mx[:, 2, :], t_mx[:, 1, :]))
            dve.wait_ge(s["t_O"], 1)
            v.tensor_tensor(t_o.rearrange("p (n d) -> p n d", n=H), ps[0:W3, 0, 0:D].rearrange("p (n d) -> p n d", n=H),
                            spread(t_mx[:, 2, :], 2, [W3, H, HD]), ALU.mult).then_inc(s["t_o"], 1)
            dve.wait_ge(s["t_wo"], 1)
            l(v.tensor_tensor(t_x1, ps[0:W3, 2, 0:D], x_, ALU.add))
            v.tensor_tensor_reduce(t_hn, t_x1, t_x1, 1.0, 0.0, ALU.mult, ALU.add, t_sc[:, 5:6]).then_inc(s["sc"], 1)
            dve.wait_ge(s["sc"], 6)
            v.scalar_tensor_tensor(t_hn, t_x1, t_sc[:, 7:8], B("ln2", W3), ALU.mult, ALU.mult).then_inc(s["t_hn"], 1)
            dve.wait_ge(s["t_w2"], 1)
            l(v.tensor_tensor(t_y, ps[0:W3, 6, 0:D], t_x1, ALU.add))
            v.tensor_scalar(t_y, t_y, t_x[:, D:D + 1], None, ALU.mult).then_inc(s["t_y"], 1)
            for t in range(T):
                dve.wait_ge(s["t_put"], t + 1)
                v.tensor_tensor(h[:, t, :], ps[0:R, t % 4, 0:D], h[:, t, :], ALU.add).then_inc(s["fin"], 1)

        @block.scalar
        def _(act):
            a = nc.scalar

            def rows_of(bank, n, w=RP, used=R):
                return ps[:, bank, 0:n * w].rearrange("p (c r) -> p c r", c=n)[:, :, 0:used]

            def gw_(t):
                if t == 0:
                    act.wait_ge(s["wproj"], 16)
                    act.wait_ge(s["vec"], 16)
                    for c in range(PC):
                        last = a.activation(gW[:, c, :], w_proj[:, c, :], ACT.Copy, scale=V("ln1_g")[:, c:c + 1])
                    last.then_inc(s["gw"], 1)

            def xT1_(t):
                act.wait_ge(s["tr1"], t + 1)
                if t >= 2:
                    act.wait_ge(s["pj"], t - 1)
                a.copy(pT[:, t % 2, :, 0:R].rearrange("p (b c) r -> p b c r", b=2),
                       ps[:, 0:2, 0:3 * RP].rearrange("p b (c r) -> p b c r", c=3)[:, :, :, 0:R]).then_inc(s["xT1"], 1)

            def xT2_(t):
                act.wait_ge(s["T2"], t + 1)
                a.copy(xT[:, t, :, 0:R], rows_of(4, DC)).then_inc(s["xT2"], 1)

            def hid(t):
                act.wait_ge(s["hidp"], t + 1)
                if t >= 2:
                    act.wait_ge(s["imp"], t - 1)
                a.activation(hT[:, t % 2, 0:R], ps[:, 5, 0:R], ACT.Relu, bias=V("bi1")).then_inc(s["hid"], 1)

            def xs_(t):
                act.wait_ge(s["gx"], t + 1)
                a.copy(xsT[:, t, :, :].rearrange("p c (n k) -> p c n k", n=2),
                       rows_of(7, DC, 64, KK).unsqueeze(2).broadcast_to([128, DC, 2, KK])).then_inc(s["xs"], 1)

            def part_hi(n):
                if n == 0:
                    act.wait_ge(s["brows"], 16)
                else:
                    act.wait_ge(s["part_lo"], n)
                a.copy(brow[:], bias_rows).then_inc(s["part_hi"], 1)

            def q0(t):
                act.wait_ge(s["q"], t + 1)
                if t == 0:
                    act.wait_ge(s["h0"], N_H0 * T)
                if t >= 2:
                    act.wait_ge(s["S0"], t - 1)
                for m in range(DC):
                    last = a.activation(qT0[:, t % 2, m, 0:R], ps[:, 0, m * RP:m * RP + R], ACT.Identity,
                                        bias=V("bq")[:, m:m + 1])
                last.then_inc(s["q0"], 1)

            def exps(t, pr, on, name):
                act.wait_ge(s[on], 2 * (t + 1))
                a.activation(pr[:, t % 3, :], pr[:, t % 3, :], ACT.Exp, scale=SCALE).then_inc(s[name], 1)

            def probsT(t, dst, n_rows, on, free, name):
                act.wait_ge(s[on], t + 1)
                if t >= 2:
                    act.wait_ge(s[free], t - 1)
                a.copy(dst[:, t % 2, :, 0:R].rearrange("p (b c) r -> p b c r", b=2),
                       ps[0:n_rows, 4:6, 0:PAIRS // 2 * RP].rearrange("p b (c r) -> p b c r", b=2, r=RP)[:, :, :, 0:R]
                       ).then_inc(s[name], 1)

            def outT(t, dst, on, free, name):
                act.wait_ge(s[on], t + 1)
                if t >= 2:
                    act.wait_ge(s[free], t - 1)
                a.copy(dst[:, t % 2, :, 0:R], rows_of(6, DC)).then_inc(s[name], 1)

            def xhi_(t):
                act.wait_ge(s["T5"], t + 1)
                if t >= 2:
                    act.wait_ge(s["w1b"], t - 1)
                a.copy(xhi[:, t % 2, :, 0:R], rows_of(0, DC)).then_inc(s["xhi"], 1)

            def hhi_(t, half, on, name):
                act.wait_ge(s[on], t + 1)
                if t >= 2:
                    act.wait_ge(s["w2"], t - 1)
                f = slice(half * FC // 2, (half + 1) * FC // 2)
                a.activation(hhi[:, t % 2, f, :].rearrange("p c r -> p (c r)"), ps[:, 1 + half, 0:FC // 2 * RP],
                             ACT.Relu).then_inc(s[name], 1)

            def xT6_(t):
                act.wait_ge(s["T6"], t + 1)
                if t >= 2:
                    act.wait_ge(s["qkv"], t - 1)
                a.copy(xT6[:, t % 2, :, 0:R], rows_of(4, DC)).then_inc(s["xT6"], 1)

            def v6_(t):
                act.wait_ge(s["qkv"], t + 1)
                a.copy(v1[:, t, :], ps[0:R, 6, 0:D]).then_inc(s["v6"], 1)

            def tqe(t):
                act.wait_ge(s["tq"], t + 1)
                view = rows_of(7, 2 * DC)
                a.copy(q6[:, t, :, 0:R], view[:, 0:DC, :]).then_inc(s["tqe"], 1)
                a.copy(xT[:, t, :, 0:R], view[:, DC:2 * DC, :]).then_inc(s["tke"], 1)

            def qm7(t):
                act.wait_ge(s["tqe"], t + 1)
                if t == 0:
                    act.wait_ge(s["qz"], 1)
                if t >= 2:
                    act.wait_ge(s["S7"], t - 1)
                for m in range(DC):
                    flat = qTm[:, t % 2, m, :, :].rearrange("p i r -> p (i r)")
                    base = flat[:, 0:S]
                    dst = bass.AP(base.tensor, base.offset, [list(base.ap[0]), [RP + S, IM], [1, S]])
                    last = a.copy(dst, q6[:, t, m, 0:R].rearrange("p (i r) -> p i r", i=IM))
                last.then_inc(s["qm7"], 1)

            def ohte(t):
                act.wait_ge(s["oht"], t + 1)
                a.copy(ohT[:, t, 0:R], ps[0:W3, 3, 0:R]).then_inc(s["ohte"], 1)

            sweep((gw_, 0, 1), (xT1_, 1),
                  (part_hi, 6, 1), (lambda n: part_hi(1), 8, 1), (lambda n: part_hi(2), 10, 1),
                  (xs_, AT_CHOICE + 5), (xT2_, AT_CHOICE + 1), (hid, AT_CHOICE + 2),
                  (lambda t: exps(t, pr0, "smx0", "ex0"), AT_ATT0 + 2), (q0, AT_ATT0),
                  (lambda t: outT(t, oT0, "pv0", "op0", "oT0"), AT_ATT0 + 5),
                  (lambda t: probsT(t, PT0, 2 * KK, "pt0", "pv0", "PT0"), AT_ATT0 + 4),
                  (lambda t: hhi_(t, 0, "w1a", "hia"), AT_FFN + 2), (lambda t: hhi_(t, 1, "w1b", "hib"), AT_FFN + 2),
                  (xhi_, AT_FFN + 1),
                  (v6_, AT_QKV + 2), (xT6_, AT_QKV + 1), (tqe, AT_QKV + 3),
                  (qm7, AT_ATT1), (lambda t: outT(t, oT7, "pv7", "op7", "oT7"), AT_ATT1 + 5),
                  (lambda t: probsT(t, PT7, 2 * S, "pt7", "pv7", "PT7"), AT_ATT1 + 4),
                  (lambda t: exps(t, pr7, "smx7", "ex7"), AT_ATT1 + 2),
                  (ohte, AT_ROUTE + 3))
            act.wait_ge(s["t_ang"], 1)
            a.activation(t_f[:, 3, :], t_f[:, 0, :], ACT.Sin).then_inc(s["t_sin"], 1)
            a.activation(t_f[:, 4, :], t_f[:, 2, :], ACT.Sin).then_inc(s["t_sin"], 1)
            act.wait_ge(s["t_T"], 1)
            a.copy(t_hnT, ps[:, 4, 0:DC * W3].rearrange("p (c r) -> p c r", c=DC)).then_inc(s["t_hnT"], 1)
            act.wait_ge(s["t_qkv"], 1)
            a.copy(t_v, ps[0:W3, 7, 0:D]).then_inc(s["t_v"], 1)
            act.wait_ge(s["t_Tr"], 1)
            a.copy(t_qkT, ps[:, 4, 0:4 * W3].rearrange("p (c r) -> p c r", c=4)).then_inc(s["t_qkT"], 1)
            act.wait_ge(s["t_sub"], 1)
            a.activation(t_p, t_p, ACT.Exp, scale=SCALE).then_inc(s["t_exp"], 1)
            act.wait_ge(s["t_pT"], 1)
            a.copy(t_PT.rearrange("p (g n) -> p g n", g=4), ps[0:W3, 4:8, 0:4 * W3]).then_inc(s["t_PT"], 1)
            act.wait_ge(s["t_To"], 1)
            a.copy(t_oT, ps[:, 1, 0:DC * W3].rearrange("p (c r) -> p c r", c=DC)).then_inc(s["t_oT"], 1)
            act.wait_ge(s["t_T"], 2)
            a.copy(t_hnT, ps[:, 3, 0:DC * W3].rearrange("p (c r) -> p c r", c=DC)).then_inc(s["t_hnT"], 1)
            act.wait_ge(s["t_w1"], 1)
            a.activation(t_g.rearrange("p (b c) r -> p b (c r)", b=2), ps[:, 4:6, 0:4 * W3],
                         ACT.Gelu_apprx_tanh).then_inc(s["t_g"], 1)

        @block.tensor
        def _(pe):
            m_ = nc.tensor
            ident = C("ident")

            def transposes(bank, src, n, name, t_on=None):
                for c in range(n):
                    last = m_.transpose(ps[:, bank, c * RP:c * RP + R], src[:, c * 128:(c + 1) * 128], ident[0:R, 0:R])
                last.then_inc(s[name], 1)

            def add_bias(dst, rows_n, at_):
                m_.matmul(dst, ones_b[:, 0:rows_n], brow[:, at_:at_ + D], start=True, stop=False)

            def tr1(t):
                pe.wait_ge(s["xh1"], t + 1)
                if t == 0:
                    pe.wait_ge(s["cst"], 16)
                if t >= 1:
                    pe.wait_ge(s["xT1"], t)
                for c in range(PC):
                    last = m_.transpose(ps[:, c // 3, (c % 3) * RP:(c % 3) * RP + R],
                                        pat[:, t % 3, c * 128:(c + 1) * 128], ident[0:R, 0:R])
                last.then_inc(s["tr1"], 1)
                if t == 0:
                    pe.wait_ge(s["wproj"], 16)
                    pe.wait_ge(s["vec"], 16)
                    for c in range(PC):
                        last = m_.matmul(ps[0:R, 4, 0:D], V("ln1_b")[:, c:c + 1].broadcast_to([128, R]),
                                         w_proj[:, c, :], start=(c == 0), stop=(c == PC - 1))
                    last.then_inc(s["biasps"], 1)

            def pj(t):
                pe.wait_ge(s["xT1"], t + 1)
                if t == 0:
                    pe.wait_ge(s["gw"], 1)
                if t >= 2:
                    pe.wait_ge(s["z"], N_Z * (t - 1))
                for c in range(PC):
                    last = m_.matmul(ps[0:R, 2 + t % 2, 0:D], pT[:, t % 2, c, 0:R], gW[:, c, :],
                                     start=(c == 0), stop=(c == PC - 1))
                last.then_inc(s["pj"], 1)

            def T2(t):
                pe.wait_ge(s["xn0"], t + 1)
                if t == 0:
                    pe.wait_ge(s["bp0"], 1)
                if t >= 1:
                    pe.wait_ge(s["xT2"], t)
                transposes(4, xa[:, t, 0:D], DC, "T2")

            def hidp(t):
                pe.wait_ge(s["xT2"], t + 1)
                if t == 0:
                    pe.wait_ge(s["w0"], 16 * 5)
                if t >= 1:
                    pe.wait_ge(s["hid"], t)
                for c in range(DC):
                    last = m_.matmul(ps[:, 5, 0:R], wi1[:, c, :], xT[:, t, c, 0:R], start=(c == 0), stop=(c == DC - 1))
                last.then_inc(s["hidp"], 1)

            def imp(t):
                pe.wait_ge(s["hid"], t + 1)
                if t >= 1:
                    pe.wait_ge(s["vE"], N_VE * t)
                if t >= 2:
                    pe.wait_ge(s["rank"], N_RANK * (t - 1))
                m_.matmul(ps[0:R, 6, 256 + 2 * (t % 2):256 + 2 * (t % 2) + 1], hT[:, t % 2, 0:R], V("wi2"), start=True,
                          stop=True).then_inc(s["imp"], 1)

            def G(t):
                pe.wait_ge(s["vE"], N_VE * (t + 1))
                if t >= 1:
                    pe.wait_ge(s["rank"], N_RANK * t)
                m_.matmul(ps[0:R, 6, 0:S], C("same", R), rk0[:, t % 2, 8:8 + S], start=True,
                          stop=True).then_inc(s["G"], 1)

            def gx(t):
                pe.wait_ge(s["rank"], N_RANK * (t + 1))
                if t >= 1:
                    pe.wait_ge(s["xs"], t)
                for c in range(DC):
                    last = m_.matmul(ps[:, 7, 64 * c:64 * c + KK], xa[:, t, c * 128:(c + 1) * 128], oh0[:, t % 2, :],
                                     start=True, stop=True)
                last.then_inc(s["gx"], 1)

            def gamps(n):
                pe.wait_ge(s["absum"], 2)
                pe.wait_ge(s["pool_set"], 2)
                pe.wait_ge(s["z"], N_Z * T)
                m_.matmul(ps[:, 3, 508:510], ones[:], gam[:, 0:2], start=True, stop=True).then_inc(s["gamps"], 1)

            def q_(t):
                pe.wait_ge(s["xT2"], t + 1)
                if t == 0:
                    pe.wait_ge(s["xT1"], T)
                if t >= 1:
                    pe.wait_ge(s["q0"], t)
                for m in range(DC):
                    cols = slice(m * 128, (m + 1) * 128)
                    for c in range(DC):
                        last = m_.matmul(ps[:, 0, m * RP:m * RP + R], wq0[:, c, cols], xT[:, t, c, 0:R],
                                         start=(c == 0), stop=(c == DC - 1))
                last.then_inc(s["q"], 1)

            def kv_(t):
                pe.wait_ge(s["xs"], t + 1)
                if t == 0:
                    pe.wait_ge(s["part_hi"], 3)
                if t >= 1:
                    pe.wait_ge(s["vm0"], t)
                    pe.wait_ge(s["kb0"], t)
                for m in range(DC):
                    for c in range(DC):
                        m_.matmul(ps[:, 1, 256 + 64 * m:256 + 64 * m + KK], wk0[:, c, m * 128:(m + 1) * 128],
                                  xsT[:, t, c, 0:KK], start=(c == 0), stop=(c == DC - 1))
                add_bias(ps[0:2 * KK, 1, 0:D], 2 * KK, BV_AT)
                for c in range(DC):
                    last = m_.matmul(ps[0:2 * KK, 1, 0:D], xsT[:, t, c, :], wv0[:, c, :], start=False, stop=(c == DC - 1))
                last.then_inc(s["kv"], 1)

            def S0(t):
                pe.wait_ge(s["q0"], t + 1)
                pe.wait_ge(s["kb0"], t + 1)
                if t == 0:
                    pe.wait_ge(s["cast"], 3)
                    pe.wait_ge(s["thr"], 2)
                if t >= 1:
                    pe.wait_ge(s["smx0"], 2 * t)
                for m in range(DC):
                    dst = ps[0:R, 2 + m, 0:HC * KK]
                    m_.matmul(dst, qT0[:, t % 2, m, 0:R], kbd0[:, t % 2, m, :], start=True, stop=False)
                    last = m_.matmul(dst, ident_b[:], other_b[:].unsqueeze(1).broadcast_to([R, HC, KK]),
                                     start=False, stop=True)
                last.then_inc(s["S0"], 1)

            def pT_(t, pr, w, on, free, name, before):
                pe.wait_ge(s[on], t + 1)
                if t == 0:
                    for done, n in before:
                        pe.wait_ge(s[done], n)
                if t >= 1:
                    pe.wait_ge(s[free], t)
                for p in range(PAIRS):
                    o = (p % 4) * RP
                    last = m_.transpose(ps[0:w, 4 + p // 4, o:o + R], pr[:, t % 3, p * w:(p + 1) * w], ident[0:R, 0:R])
                last.then_inc(s[name], 1)

            def pv0(t):
                pe.wait_ge(s["PT0"], t + 1)
                pe.wait_ge(s["vm0"], t + 1)
                if t == 0:
                    pe.wait_ge(s["rank"], N_RANK * T)
                if t >= 1:
                    pe.wait_ge(s["oT0"], t)
                for p in range(PAIRS):
                    q = 32 * (p % 4)
                    o = (p // 4) * RP
                    last = m_.matmul(ps[q:q + 32, 6, o:o + R], vm0[:, t % 5, 32 * p:32 * p + 32], PT0[:, t % 2, p, 0:R],
                                     start=True, stop=True)
                last.then_inc(s["pv0"], 1)

            def project(t, oT, w, bias_at, on, free, name, before):
                pe.wait_ge(s[on], t + 1)
                if t == 0:
                    pe.wait_ge(s[before], T)
                if t >= 1:
                    pe.wait_ge(s[free], t)
                add_bias(ps[0:R, 7, 0:D], R, bias_at)
                for c in range(DC):
                    last = m_.matmul(ps[0:R, 7, 0:D], oT[:, t % 2, c, 0:R], w[:, c, :], start=False, stop=(c == DC - 1))
                last.then_inc(s[name], 1)

            def T5(t):
                pe.wait_ge(s["xn1"], t + 1)
                if t == 0:
                    pe.wait_ge(s["q0"], T)
                if t >= 1:
                    pe.wait_ge(s["xlo"], t)
                transposes(0, xa[:, t, 0:D], DC, "T5")

            def w1(t, half, free, name):
                pe.wait_ge(s["xlo"], t + 1)
                if t == 0:
                    pe.wait_ge(s["smx0"], 2 * T)
                    pe.wait_ge(s["vm0"], T)
                    pe.wait_ge(s["quant"], 4)
                    pe.wait_ge(s["pool_set"], 5)
                if t >= 1:
                    pe.wait_ge(s[free], t)
                for i in range(FC // 2):
                    f = half * FC // 2 + i
                    dst = ps[:, 1 + half, i * RP:(i + 1) * RP]
                    m_.matmul(dst, brow[:, f * 128:(f + 1) * 128], ones_b[:, 0:RP], start=True, stop=False)
                    for c in range(DC):
                        for x in (xhi, xlo):
                            last = m_.matmul(dst, w1q[:, c, f * 128:(f + 1) * 128], x[:, t % 2, c, :],
                                             start=False, stop=(c == DC - 1 and x is xlo))
                last.then_inc(s[name], 1)

            def w2(t):
                pe.wait_ge(s["loa"], t + 1)
                pe.wait_ge(s["lob"], t + 1)
                if t >= 1:
                    pe.wait_ge(s["h5"], t)
                add_bias(ps[0:R, 3, 0:D], R, B2_AT)
                for f in range(FC):
                    for x in (hhi, hlo):
                        last = m_.matmul(ps[0:R, 3, 0:D], x[:, t % 2, f, 0:R], w2q[:, f, :], start=False,
                                         stop=(f == FC - 1 and x is hlo))
                last.then_inc(s["w2"], 1)

            def T6(t):
                pe.wait_ge(s["xn2"], t + 1)
                if t == 0:
                    pe.wait_ge(s["PT0"], T)
                if t >= 1:
                    pe.wait_ge(s["xT6"], t)
                transposes(4, xa[:, t, 0:D], DC, "T6")

            def qkv(t):
                pe.wait_ge(s["xT6"], t + 1)
                if t == 0:
                    pe.wait_ge(s["wl1"], 32)
                    pe.wait_ge(s["oT0"], T)
                if t >= 1:
                    pe.wait_ge(s["rope"], 2 * t)
                    pe.wait_ge(s["v6"], t)
                for bank, cols in ((5, slice(0, 2 * D)), (6, slice(2 * D, 3 * D))):
                    dst = ps[0:R, bank, 0:cols.stop - cols.start]
                    m_.matmul(dst, ones_b[:, 0:R], brow[:, BQKV_AT + cols.start:BQKV_AT + cols.stop], start=True, stop=False)
                    for c in range(DC):
                        last = m_.matmul(dst, xT6[:, t % 2, c, 0:R], wqkv[:, c, cols], start=False, stop=(c == DC - 1))
                last.then_inc(s["qkv"], 1)

            def tq(t):
                pe.wait_ge(s["rope_sum"], t + 1)
                if t == 0:
                    pe.wait_ge(s["h4"], T)
                if t >= 1:
                    pe.wait_ge(s["tke"], t)
                transposes(7, rot[:, t % 2, 0, :], 2 * DC, "tq")

            def S7(t):
                pe.wait_ge(s["qm7"], t + 1)
                pe.wait_ge(s["kbA"], t + 1)
                pe.wait_ge(s["kbB"], t + 1)
                if t == 0:
                    pe.wait_ge(s["h5"], T)
                if t >= 2:
                    pe.wait_ge(s["smx7"], 2 * (t - 1))
                for m in range(DC):
                    dst = ps[0:R, 2 * (t % 2) + m, 0:HC * S]
                    for i in range(IM):
                        m_.matmul(dst, qTm[:, t % 2, m, i, 0:R], kbd7[:, t % 2, m, i * HC * S:(i + 1) * HC * S],
                                  start=(i == 0), stop=False)
                    last = m_.matmul(dst, ident_b[:], causal_b[:].unsqueeze(1).broadcast_to([R, HC, S]),
                                     start=False, stop=True)
                last.then_inc(s["S7"], 1)

            def pv7(t):
                pe.wait_ge(s["PT7"], t + 1)
                pe.wait_ge(s["vm7"], t + 1)
                if t == 0:
                    pe.wait_ge(s["v6"], T)
                if t >= 1:
                    pe.wait_ge(s["oT7"], t)
                for p in range(PAIRS):
                    q = 32 * (p % 4)
                    for i in range(IM):
                        o = (p // 4) * RP + i * S
                        a_ = i * D + 32 * p
                        last = m_.matmul(ps[q:q + 32, 6, o:o + S], vm7[:, t % 3, a_:a_ + 32],
                                         PT7[:, t % 2, p, i * S:(i + 1) * S], start=True, stop=True)
                last.then_inc(s["pv7"], 1)

            def G9(t):
                pe.wait_ge(s["rw"], N_RW * (t + 1))
                if t == 0:
                    pe.wait_ge(s["smx7"], 2 * T)
                if t >= 1:
                    pe.wait_ge(s["rank9"], N_RANK9 * t)
                m_.matmul(ps[0:R, 0, 64 * (t % 2):64 * (t % 2) + S], C("same", R), rk9[:, t % 2, 8:8 + S], start=True,
                          stop=True).then_inc(s["G9"], 1)

            def gather(t):
                pe.wait_ge(s["rank9"], N_RANK9 * (t + 1))
                if t == 0:
                    pe.wait_ge(s["aug"], 4)
                if t >= 1:
                    pe.wait_ge(s["ohte"], t)
                m_.matmul(ps[0:W3, 1, 0:XA], oh9[:, t % 2, :], xa[:, t, :], start=(t == 0), stop=(t == T - 1))
                m_.matmul(ps[0:S, 2, 0:W3], C("tok", R), oh9[:, t % 2, :], start=(t == 0), stop=(t == T - 1)
                          ).then_inc(s["acc"], 1)
                m_.transpose(ps[0:W3, 3, 0:R], oh9[:, t % 2, :], ident[0:R, 0:R]).then_inc(s["oht"], 1)

            sweep((tr1, 1), (pj, 2), (gamps, 13, 1),
                  (G, AT_CHOICE + 4), (imp, AT_CHOICE + 3), (gx, AT_CHOICE + 5), (hidp, AT_CHOICE + 2), (T2, AT_CHOICE + 1),
                  (S0, AT_ATT0 + 1),
                  (lambda t: pT_(t, pr0, 2 * KK, "pn0", "PT0", "pt0", (("xT2", T), ("hid", T))), AT_ATT0 + 4),
                  (pv0, AT_ATT0 + 5), (q_, AT_ATT0), (kv_, AT_ATT0),
                  (lambda t: project(t, oT0, wo0, BO_AT, "oT0", "h4", "op0", "xs"), AT_ATT0 + 6),
                  (lambda t: w1(t, 0, "loa", "w1a"), AT_FFN + 2), (lambda t: w1(t, 1, "lob", "w1b"), AT_FFN + 2),
                  (T5, AT_FFN + 1), (w2, AT_FFN + 3),
                  (qkv, AT_QKV + 2), (T6, AT_QKV + 1), (tq, AT_QKV + 3),
                  (S7, AT_ATT1 + 1),
                  (lambda t: pT_(t, pr7, 2 * S, "pn7", "PT7", "pt7", (("tqe", T), ("rope", 2 * T))), AT_ATT1 + 4),
                  (pv7, AT_ATT1 + 5), (lambda t: project(t, oT7, wp, BP_AT, "oT7", "h7", "op7", "tke"), AT_ATT1 + 6),
                  (G9, AT_ROUTE + 2), (gather, AT_ROUTE + 3))

            def turn(bank, src, w, n, name, at_=0):
                for c in range(n):
                    last = m_.transpose(ps[0:w, bank, at_ + c * W3:at_ + (c + 1) * W3], src[:, c * w:(c + 1) * w],
                                        ident[0:W3, 0:W3])
                if name:
                    last.then_inc(s[name], 1)

            pe.wait_ge(s["t_hn"], 1)
            turn(5, t_x[:, D + 2:XA], S, 1, None)
            turn(4, t_hn, 128, DC, "t_T")
            pe.wait_ge(s["t_mrow"], 1)
            m_.matmul(ps[0:W3, 5, 0:W3], t_cmp[:, W3:2 * W3], t_cmp[:, 0:W3], start=True, stop=True).then_inc(s["t_mm"], 1)
            pe.wait_ge(s["t_hnT"], 1)
            pe.wait_ge(s["w2nd"], 32)
            for bank, cols in ((6, slice(0, 2 * D)), (7, slice(2 * D, 3 * D))):
                for c in range(DC):
                    last = m_.matmul(ps[0:W3, bank, 0:cols.stop - cols.start], t_hnT[:, c, :], wqkv_l[:, c, cols],
                                     start=(c == 0), stop=(c == DC - 1))
            last.then_inc(s["t_qkv"], 1)
            pe.wait_ge(s["t_rot"], 1)
            turn(4, t_rot[:, 0, :], 128, 4, "t_Tr")
            pe.wait_ge(s["t_kbd"], 1)
            pe.wait_ge(s["ohte"], T)
            for g in range(4):
                last = m_.matmul(ps[0:W3, g, 0:4 * W3], t_qkT[:, g // 2, :],
                                 t_kbd[:, g // 2, (g % 2) * 4 * W3:(g % 2 + 1) * 4 * W3], start=True, stop=True)
            last.then_inc(s["t_S"], 1)
            pe.wait_ge(s["t_exp"], 1)
            pe.wait_ge(s["t_v"], 1)
            for g in range(4):
                turn(4 + g, t_p[:, g * 4 * W3:(g + 1) * 4 * W3], W3, 4, "t_pT" if g == 3 else None)
            pe.wait_ge(s["t_PT"], 1)
            for n in range(H):
                last = m_.matmul(ps[0:W3, 0, n * HD:(n + 1) * HD], t_PT[:, n * W3:(n + 1) * W3],
                                 t_v[:, n * HD:(n + 1) * HD], start=True, stop=True)
            last.then_inc(s["t_O"], 1)
            pe.wait_ge(s["t_o"], 1)
            turn(1, t_o, 128, DC, "t_To")
            pe.wait_ge(s["t_oT"], 1)
            for c in range(DC):
                last = m_.matmul(ps[0:W3, 2, 0:D], t_oT[:, c, :], wo_l[:, c, :], start=(c == 0), stop=(c == DC - 1))
            last.then_inc(s["t_wo"], 1)
            pe.wait_ge(s["t_hn"], 2)
            turn(3, t_hn, 128, DC, "t_T")
            pe.wait_ge(s["t_hnT"], 2)
            pe.wait_ge(s["wlast"], 32)
            for f in range(FC):
                for c in range(DC):
                    last = m_.matmul(ps[:, 4 + f // 4, (f % 4) * W3:(f % 4 + 1) * W3], w1raw[:, c, f * 128:(f + 1) * 128],
                                     t_hnT[:, c, :], start=(c == 0), stop=(c == DC - 1))
            last.then_inc(s["t_w1"], 1)
            pe.wait_ge(s["t_g"], 1)
            for f in range(FC):
                last = m_.matmul(ps[0:W3, 6, 0:D], t_g[:, f, :], w2raw[:, f, :], start=(f == 0), stop=(f == FC - 1))
            last.then_inc(s["t_w2"], 1)
            pe.wait_ge(s["t_y"], 1)
            for t in range(T):
                if t >= 4:
                    pe.wait_ge(s["fin"], t - 3)
                if t == 0:
                    pe.wait_ge(s["base"], T)
                m_.matmul(ps[0:R, t % 4, 0:D], ohT[:, t, 0:R], t_y, start=True, stop=True).then_inc(s["t_put"], 1)


def kernel(**inputs):
    import concourse.bacc as _bacc
    from concourse.bass_utils import run_bass_kernel_spmd as _run

    a = {k: np.ascontiguousarray(v) for k, v in inputs.items()}
    P_ = 16
    n = a["x"].shape[2] // P_
    x = a["x"].reshape(IMAGES, 3, n, P_, n, P_).transpose(0, 2, 4, 3, 5, 1).reshape(IMAGES, PATCHES, PD)
    patches = np.zeros((T * IM, S, PD), x.dtype)
    patches[:IMAGES, 1:] = x

    vectors = np.zeros((128, N_VEC), np.float32)
    p = np.arange(128)
    for name, src in (("ln1_g", "L0_tok_ln1_g"), ("ln1_b", "L0_tok_ln1_b"), ("bq", "L0_attn_bq"), ("bk", "L0_attn_bk"),
                      ("bi1", "L0_attn_bi1"), ("wi2", "L0_attn_wi2")):
        at, w = _vat[name]
        vectors[:, at:at + w] = a[src].reshape(w, 128).T
    vectors[:, _vat["bi2"][0]] = a["L0_attn_bi2"][0]
    vectors[:, _vat["router_b"][0]] = a["L1_ffn_router_b"][0]
    vectors[:, _vat["part1"][0]] = p >= 1
    vectors[:, _vat["part2"][0]] = p >= 2
    names = {"b_proj": "L0_tok_b_proj", "ln2_g": "L0_tok_ln2_g", "ln2_b": "L0_tok_ln2_b", "cls": "L0_tok_cls_token",
             "router_w": "L1_ffn_router_w", "ln1": "L1_ffn_ln1", "ln2": "L1_ffn_ln2"}
    rows = np.concatenate([a[names[name]].reshape(1, D) for name in _rat], axis=1)
    wide_rows = np.concatenate([a[k].reshape(1, -1) for k in ("L0_ffn_b1", "L1_attn_bq", "L1_attn_bk", "L1_attn_bv", "L0_attn_bo",
                                                      "L0_ffn_b2", "L1_attn_bp", "L0_attn_bv")], axis=1)
    tensors = {
        "patches": patches.reshape(T * R, PD), "W_proj": a["L0_tok_W_proj"], "consts": shape_constants(),
        "vectors": vectors, "rows": rows, "wide_rows": wide_rows, "pos3": np.tile(a["L0_tok_pos_emb"][0], (IM, 1)),
        "wqT": a["L0_attn_wq"].T, "wkT": a["L0_attn_wk"].T, "wvT": a["L0_attn_wv"].T, "woT": a["L0_attn_wo"].T,
        "wi1T": a["L0_attn_wi1"].T, "W1T": a["L0_ffn_W1"].T, "W2T": a["L0_ffn_W2"].T,
        "wqkv1": np.concatenate([a["L1_attn_Wq"], a["L1_attn_Wk"], a["L1_attn_Wv"]], axis=1), "wp1": a["L1_attn_Wp"],
        "mask": a["L1_ffn_attention_mask"], "positions": a["L1_ffn_position_ids"],
        "wqkv2": np.concatenate([a["L1_ffn_wq"], a["L1_ffn_wk"], a["L1_ffn_wv"]], axis=1), "wo2": a["L1_ffn_wo"],
        "w1f": a["L1_ffn_w1"], "w2f": a["L1_ffn_w2"],
    }
    nc = _bacc.Bacc("TRN2", target_bir_lowering=False, num_devices=1)
    arrays, args = {}, {}
    for name, value in tensors.items():
        value = np.ascontiguousarray(value)
        arrays[f"in_{name}"] = value
        args[name] = nc.dram_tensor(f"in_{name}", value.shape, mybir.dt.from_np(value.dtype), kind="ExternalInput").ap()
    args["out"] = nc.dram_tensor("out", (ROWS, D), F32, kind="ExternalOutput").ap()
    vit_tower(nc, **args)
    r = _run(nc, [arrays], core_ids=[0])
    return r.results[0]["out"].reshape(IMAGES, S, D)
```

```python
from contextlib import ExitStack

import numpy as np

import concourse.bass as bass
from concourse import mybir

F32 = mybir.dt.float32
F32R = mybir.dt.float32r
BF16 = mybir.dt.bfloat16
I32 = mybir.dt.int32
ALU = mybir.AluOpType
ACT = mybir.ActivationFunctionType
AX = mybir.AxisListType

IMAGES, S, D, H, HD = 32, 37, 256, 16, 16
PATCHES, PD = 36, 768
IM = 3
R = IM * S
RP = R + 1
T = -(-IMAGES // IM)
ROWS = IMAGES * S
R_LAST = ROWS - (T - 1) * R
DC = D // 128
PC = PD // 128
HC = H // DC
K0 = max(1, int(S * 0.3))
KK = IM * K0
F = 4 * D
FC = F // 128
PAIRS = H // 2
KSEL = int(0.125 * S)
NSEL = KSEL - 1
W3 = IMAGES * NSEL
MB = 4
WEIGHT_AT, POSITION_AT, MASK_AT, TOKEN_AT, XA = D, D + 1, D + 2, D + 2 + S, D + 2 + 2 * S
SCALE = 1.0 / HD ** 0.5
LN_EPS = 1e-5
RMS_EPS = 1e-6
FAR = -1e30
CAUSAL = -1e10

_at = {}
_n = 0
for _name, _w in (("ident", 128), ("same", R), ("tok", S), ("before", S), ("slot0", KK),
                  ("slot1", 2 * W3 + 3), ("notcls", 1), ("iscls", 1), ("other0", KK),
                  ("causal", S), ("head", HC), ("pair0", 2), ("pair1", 2), ("cos", HD),
                  ("sin", HD), ("inv", HD), ("sign", HD), ("next1", W3), ("next2", W3)):
    _at[_name] = (_n, _w)
    _n += _w
N_CONST = _n
_vat = {}
_n = 0
for _name, _w in (("ln1_g", PC), ("ln1_b", PC), ("bq", DC), ("bk", DC), ("bi1", 1), ("wi2", 1),
                  ("bi2", 1), ("router_b", 1), ("part1", 1), ("part2", 1)):
    _vat[_name] = (_n, _w)
    _n += _w
N_VEC = _n
_rat = {}
_n = 0
for _name in ("b_proj", "ln2_g", "ln2_b", "cls", "router_w", "ln1", "ln2"):
    _rat[_name] = (_n, D)
    _n += D
N_ROW = _n
BQKV_AT = F
BO_AT, B2_AT, BP_AT, BV_AT = (F + (3 + _i) * D for _i in range(4))
N_ROWS = F + 7 * D

AT_CHOICE, AT_ATT0, AT_FFN, AT_QKV, AT_ATT1, AT_ROUTE = 8, 17, 27, 32, 44, 50


def shape_constants():
    c = np.zeros((128, N_CONST), np.float32)

    def put(name, a):
        at, w = _at[name]
        a = np.asarray(a, np.float32)
        c[:a.shape[0], at:at + w] = a

    p = np.arange(128)
    r = np.arange(R)
    im, tok = r // S, r % S
    put("ident", np.eye(128))
    put("same", im[:, None] == im[None, :])
    put("tok", tok[:, None] == np.arange(S))
    put("before", np.arange(S) < tok[:, None])
    k = np.arange(KK)
    put("slot0", np.where(im[:, None] == k // K0, k % K0, -1))
    put("other0", np.where(im[:, None] == k // K0, 0.0, FAR))
    g = np.arange(2 * W3 + 3) - (T - 1) * IM * NSEL
    put("slot1", np.where(im[:, None] == g // NSEL, g % NSEL, -1))
    put("notcls", (tok != 0)[:, None])
    put("iscls", (tok == 0)[:, None])
    put("causal", np.where(np.arange(S) <= tok[:, None], 0.0, CAUSAL))
    put("head", (p[:, None] % 128) // HD == np.arange(HC))
    put("pair0", (p[:2 * KK, None] // KK) == np.arange(2))
    put("pair1", (p[:2 * S, None] // S) == np.arange(2))
    half = HD // 2
    inv = (1.0 / np.float32(10000.0) ** (np.arange(half, dtype=np.float32) * np.float32(2.0 / HD))).astype(np.float32)
    ang = (tok.astype(np.float32)[:, None] * inv[None, :]).astype(np.float32)
    put("cos", np.repeat(np.cos(ang), 2, axis=1))
    put("sin", (np.sin(ang)[:, :, None] * np.array([-1.0, 1.0])).reshape(R, HD))
    put("inv", np.tile(np.concatenate([inv, inv]), (128, 1)))
    put("sign", np.tile(np.concatenate([-np.ones(half), np.ones(half)]), (128, 1)))
    w = np.arange(W3)
    for j in range(1, NSEL):
        put(f"next{j}", w[:, None] == w // NSEL * NSEL + (w + j) % NSEL)
    return c


def vit_tower(nc, patches, W_proj, consts, vectors, rows, wide_rows, pos3, wqT, wkT, wvT, woT, wi1T,
              W1T, W2T, wqkv1, wp1, mask, positions, wqkv2, wo2, w1f, w2f, out):
    with ExitStack() as ctx:
        def sb(name, shape, dt=F32):
            return ctx.enter_context(nc.sbuf_tensor(name, shape, dt))

        def sem(name):
            return ctx.enter_context(nc.semaphore(name))

        ps = ctx.enter_context(nc.psum_tensor("ps", [128, 8, 512], F32))

        cst = sb("cst", [128, N_CONST])
        vec = sb("vec", [128, N_VEC])
        row = sb("row", [128, N_ROW])
        pos = sb("pos", [R, D])
        early = sb("early", [128, PC * D + 4 * DC * D])
        wi1 = sb("wi1", [128, DC, 128])
        wide = sb("wide", [128, 2 * FC * D])
        w1q = sb("w1q", [128, DC, F], F32R)
        w2q = sb("w2q", [128, FC, D], F32R)
        wqkv = sb("wqkv", [128, DC, 3 * D])
        wp = sb("wp", [128, DC, D])
        wqkv_l = sb("wqkv_l", [128, DC, 3 * D])
        wo_l = sb("wo_l", [128, DC, D])
        maskrow = sb("maskrow", [R, 2, S])
        posi = sb("posi", [R, 2, 1], I32)

        ident_b = sb("ident_b", [R, R], BF16)
        other_b = sb("other_b", [R, KK], BF16)
        causal_b = sb("causal_b", [R, S], BF16)
        ones = sb("ones", [128, 128])
        ones_b = sb("ones_b", [3, 2 * RP], BF16)
        mhalf = sb("mhalf", [128, 1])
        bp0 = sb("bp0", [R, D])
        posb = sb("posb", [R, D])
        brow = sb("brow", [3, N_ROWS], BF16)
        gam = sb("gam", [128, 8])

        h = sb("h", [R, T, D])
        xa = sb("xa", [R, T, XA])
        xT = sb("xT", [128, T, DC, RP])
        q6 = sb("q6", [128, T, DC, RP])
        v1 = sb("v1", [R, T, D])
        ohT = sb("ohT", [W3, T, RP])
        st = sb("st", [R, T, 12])
        mv = sb("mv", [R, T, 2])
        rs = sb("rs", [R, T, 2])
        xhi = sb("xhi", [128, 2, DC, 2, RP], F32R)
        xlo = sb("xlo", [128, 2, DC, 2, RP], F32R)
        hhi = sb("hhi", [128, FC, 2, RP], F32R)
        hlo = sb("hlo", [128, FC, 2, RP], F32R)

        A_SIZE, B_SIZE = 6608, 3664
        arena_a = sb("arena_a", [128, A_SIZE])
        arena_b = sb("arena_b", [128, B_SIZE])

        def cut(whole, at, shape):
            n = int(np.prod(shape[1:]))
            ap = whole[0:shape[0], at[0]:at[0] + n]
            at[0] += n
            assert at[0] <= whole.shape[1], (at, whole.shape)
            if len(shape) == 2:
                return ap
            names = "abcd"[:len(shape) - 1]
            sizes = {x: v for x, v in zip(names, shape[1:])}
            return ap.rearrange(f"p ({' '.join(names)}) -> p {' '.join(names)}", **sizes)

        at = [0]
        w_proj = cut(early, at, [128, PC, D])
        wq0, wk0, wv0, wo0 = (cut(early, at, [128, DC, D]) for _ in range(4))
        kbd7 = cut(early, [0], [128, 2, DC, IM * HC * S])
        at = [0]
        w1raw = cut(wide, at, [128, DC, F])
        w2raw = cut(wide, at, [128, FC, D])
        at = [0]
        vm7 = cut(wide, at, [2 * S, 3, IM * D])
        PT7 = cut(wide, at, [2 * S, 2, PAIRS, RP])
        at = [0]
        pat = cut(arena_a, at, [R, 3, PD])
        pT = cut(arena_a, at, [128, 2, PC, RP])
        zb = cut(arena_a, at, [R, 2, D])
        zn = cut(arena_a, at, [R, 2, D])
        at = [0]
        qT0 = cut(arena_a, at, [128, 2, DC, RP])
        kbd0 = cut(arena_a, at, [128, 2, DC, HC * KK])
        vm0 = cut(arena_a, at, [2 * KK, 5, D])
        pr0 = cut(arena_a, at, [R, 3, H * KK])
        PT0 = cut(arena_a, at, [2 * KK, 2, PAIRS, RP])
        oT0 = cut(arena_a, at, [128, 2, DC, RP])
        sm0 = sb("sm0", [R, 2, 3, H])
        at = [0]
        xT6 = cut(arena_a, at, [128, 2, DC, RP])
        rot = cut(arena_a, at, [R, 2, 2, 2 * D])
        at = [0]
        hT = cut(arena_b, at, [128, 2, RP])
        rk0 = cut(arena_b, at, [R, 2, 8 + 4 * S])
        oh0 = cut(arena_b, at, [R, 2, KK])
        xsT = cut(arena_b, at, [128, T, DC, 2 * KK])
        at = [0]
        qTm = cut(arena_b, at, [128, 2, DC, IM, RP])
        pr7 = cut(arena_b, at, [R, 3, H * S])
        oT7 = cut(arena_b, at, [128, 2, DC, RP])
        sm7 = cut(arena_b, at, [R, 2, 3, H])

        names = """cst vec row pos wproj w0 w1raw w2raw wl1 mrow w2nd wlast brows stored
            pool_set cast posb biasps bp0 gw absum gamps thr low quant part_hi part_lo
            st1 rs1 xh1 tr1 xT1 pj z rs2 zn h0
            ln_stats0 ln_stats1 ln_stats2 ln_stats3 ln_scale0 ln_scale1 ln_scale2 ln_scale3 xn0 xn1 xn2 xn3 T2 xT2 hidp hid imp vE G rank gx xs
            q kv q0 kb0 vm0 S0 smx0 ex0 sum0 pn0 pt0 PT0 pv0 oT0 op0 h4
            T5 xhi xlo w1a w1b hia hib loa lob w2 h5
            T6 xT6 qkv rope rope_sum v6 tq tqe tke qz
            qm7 kbA kbB vm7 S7 smx7 ex7 sum7 pn7 pt7 PT7 pv7 oT7 op7 h7
            rw G9 rank9 acc oht ohte base aug
            tv sc fin t_ang t_sin t_hn t_T t_hnT t_tok t_qkv t_v t_rot t_kn t_vn t_sub
            t_exp t_o t_To t_oT t_wo t_w1 t_g t_w2 t_y t_put""".split()
        s = {n: sem(n) for n in names}
        s_pat = [sem(f"pat{i}") for i in range(3)]
        s_vrep = [sem(f"vrep{i}") for i in range(3)]
        N_ST1, N_RS1, N_Z, N_RS2, N_H0, N_LNA, N_LNR, N_VE, N_RANK, N_SUM, N_RW, N_RANK9 = \
            3, 2, 3, 4, 2, 2, [2, 2, 2, 3], 2, 5, 2, 3, 8
        ACT_NORMS = (3,)

        def C(name, rows=128):
            a, w = _at[name]
            return cst[0:rows, a:a + w]

        def V(name):
            a, w = _vat[name]
            return vec[:, a:a + w]

        def B(name, rows=R):
            a, w = _rat[name]
            return row[0:rows, a:a + w]

        def spread(ap, axis, shape):
            return ap.unsqueeze(axis).broadcast_to(shape)

        def link(eng, name, start):
            n = [start]

            def f(ins, wait=True):
                n[0] += 1
                ins.then_inc(s[name], 1)
                if wait:
                    eng.wait_ge(s[name], n[0])
            return f

        def sweep(*steps):
            steps = [x if len(x) == 3 else (*x, T) for x in steps]
            for turn in range(max(start + n for _, start, n in steps)):
                for step, start, n in steps:
                    if 0 <= turn - start < n:
                        step(turn - start)

        def only(step, n):
            return lambda t: step(t) if t % 2 == n else None

        def quarter(t, n):
            pair, c = t // 2, 2 * (2 * (t % 2) + n)
            tiles = min(2, T - 2 * pair)
            return ((slice(None), slice(c, c + 2), slice(0, tiles), slice(None)),
                    ps[:, 1 + n, 0:4 * RP].rearrange("p (c n r) -> p c n r", c=2, n=2)[:, :, 0:tiles, :])

        at = [0]
        t_x = cut(arena_a, at, [W3, XA])
        t_hn = cut(arena_a, at, [W3, D])
        t_hnT = cut(arena_a, at, [128, DC, W3])
        t_qkv = cut(arena_a, at, [W3, 3, D])
        t_rot = cut(arena_a, at, [W3, 2 * D])
        t_g = cut(arena_a, at, [128, FC, W3])
        junk = cut(arena_a, at, [R, D])
        rk9 = cut(arena_a, at, [R, 2, 12 + 4 * S])
        oh9 = cut(arena_a, at, [R, 2, W3])
        at = [0]
        t_p = cut(arena_b, at, [W3, NSEL, D])
        t_pv = cut(arena_b, at, [W3, NSEL, D])
        at = [0]
        xTflat = xT[:].rearrange("p t c r -> p (t c r)")
        t_oT = cut(xTflat, at, [128, DC, W3])
        t_sc = cut(xTflat, at, [W3, 16])
        t_f = cut(xTflat, at, [W3, 6, HD])
        t_mm = cut(xTflat, at, [W3, NSEL])
        t_s = cut(xTflat, at, [W3, NSEL, H])
        t_mx = cut(xTflat, at, [W3, 3, H])
        t_s3 = cut(xTflat, at, [W3, S])
        t_o = cut(xTflat, at, [W3, D])
        t_x1 = cut(xTflat, at, [W3, D])
        t_y = cut(xTflat, at, [W3, D])

        q6flat = q6[:].rearrange("p t c r -> p (t c r)")
        bias_rows = cut(v1[:].rearrange("p t d -> p (t d)"), [0], [3, N_ROWS])
        gW = cut(q6flat, [0], [128, PC, D])
        low = cut(q6flat, [0], [128, 2, F])

        block = ctx.enter_context(nc.Block())

        @block.sync
        def _(sp):
            def load(dst, src, on):
                sp.dma_start(dst, src).then_inc(on, 16)

            def matrix(dst, src, on):
                load(dst, src.rearrange("(c p) n -> p c n", p=128), s[on])

            def patch(t):
                if t >= 3:
                    sp.wait_ge(s["tr1"], t - 2)
                load(pat[:, t % 3, :], patches[t * R:(t + 1) * R, :], s_pat[t % 3])

            patch(0)
            load(cst[:], consts, s["cst"])
            load(vec[:], vectors, s["vec"])
            matrix(w_proj, W_proj, "wproj")
            patch(1)
            load(row[:], rows[0, :].partition_broadcast(128), s["row"])
            load(pos[:], pos3, s["pos"])
            patch(2)
            matrix(wi1[:], wi1T, "w0")
            for dst, src in ((wq0, wqT), (wk0, wkT), (wv0, wvT), (wo0, woT)):
                matrix(dst, src, "w0")
            load(bias_rows, wide_rows[0, :].partition_broadcast(3), s["brows"])
            patch(3)
            patch(4)
            matrix(w1raw, W1T, "w1raw")
            matrix(w2raw, W2T, "w2raw")
            for t in range(5, T):
                patch(t)
            matrix(wqkv[:], wqkv1, "wl1")
            matrix(wp[:], wp1, "wl1")
            for i in range(IM):
                a = slice(i * S, (i + 1) * S)
                for n, batch in ((0, i), (1, MB - 1)):
                    load(maskrow[a, n, :], mask[batch, 0, 0:S, 0:S], s["mrow"])
                    load(posi[a, n, :], positions[batch, 0:S].rearrange("(s a) -> s a", a=1), s["mrow"])
            matrix(wqkv_l[:], wqkv2, "w2nd")
            matrix(wo_l[:], wo2, "w2nd")
            for t in range(T):
                sp.wait_ge(s["v6"], t + 1)
                if t >= 3:
                    sp.wait_ge(s["pv7"], t - 2)
                else:
                    sp.wait_ge(s["quant"], 4)
                for i in range(IM):
                    for j in range(2):
                        load(vm7[j * S:(j + 1) * S, t % 3, i * D:(i + 1) * D],
                             v1[i * S:(i + 1) * S, t, :], s_vrep[t % 3])
            sp.wait_ge(s["pv7"], T)
            matrix(w1raw, w1f, "wlast")
            matrix(w2raw, w2f, "wlast")
            for t in range(T):
                n = R if t < T - 1 else R_LAST
                sp.wait_ge(s["fin"], t + 1)
                load(out[t * R:t * R + n, :], h[0:n, t, :], s["stored"])
            sp.wait_ge(s["stored"], 16 * T)

        @block.gpsimd
        def _(pool):
            g = nc.gpsimd

            def rsqrt(t, on, n_on, name, n_name, mask_cls=False, shift=False):
                pool.wait_ge(s[on], n_on * (t + 1))
                l = link(pool, name, n_name * t)
                l(g.tensor_scalar(rs[:, t, 0:1], mv[:, t, 1:2], LN_EPS, None, ALU.add))
                l(g.tensor_tensor(rs[:, t, 1:2], rs[:, t, 0:1], mhalf[0:R, :], ALU.pow), mask_cls or shift)
                if mask_cls:
                    l(g.tensor_scalar(rs[:, t, 1:2], rs[:, t, 1:2], C("notcls", R), None, ALU.mult), shift)
                if shift:
                    l(g.tensor_scalar(rs[:, t, 0:1], mv[:, t, 0:1], rs[:, t, 1:2], -1.0, ALU.mult, ALU.mult), False)

            def ln_scale(layer):
                return lambda t: rsqrt(t, f"ln_stats{layer}", N_LNA, f"ln_scale{layer}", N_LNR[layer],
                                       shift=layer in ACT_NORMS)

            def pairs_apart(dst, src, name, rows_n, n, sem_name):
                g.tensor_tensor(dst.rearrange("p (n j d) -> p n j d", j=2, d=HD),
                                src.rearrange("p (n j d) -> p n j d", j=2, d=HD),
                                C(name, rows_n).unsqueeze(1).unsqueeze(3).broadcast_to([rows_n, n, 2, HD]),
                                ALU.mult).then_inc(s[sem_name], 1)

            g.memset(mhalf[:], -0.5).then_inc(s["pool_set"], 1)
            g.memset(ones[:], 1.0).then_inc(s["pool_set"], 1)
            g.memset(ones_b[:], 1.0).then_inc(s["pool_set"], 1)
            g.memset(xhi[:, :, :, :, R:RP].bitcast(F32), 0.0).then_inc(s["pool_set"], 1)
            g.memset(xlo[:, :, :, :, R:RP].bitcast(F32), 0.0).then_inc(s["pool_set"], 1)
            pool.wait_ge(s["pool_set"], 5)
            pool.wait_ge(s["cst"], 16)
            g.tensor_copy(ident_b[:], C("ident", R)[:, 0:R]).then_inc(s["cast"], 1)
            g.tensor_copy(other_b[:], C("other0", R)).then_inc(s["cast"], 1)
            g.tensor_copy(causal_b[:], C("causal", R)).then_inc(s["cast"], 1)

            def h0(t):
                if t == 0:
                    pool.wait_ge(s["row"], 16)
                    pool.wait_ge(s["pos"], 16)
                    l = link(pool, "posb", 0)
                    l(g.tensor_scalar(posb[:], B("ln2_b"), C("notcls", R), None, ALU.mult), False)
                    l(g.tensor_scalar(B("cls"), B("cls"), C("iscls", R), None, ALU.mult))
                    l(g.tensor_tensor(posb[:], posb[:], pos[:], ALU.add))
                    l(g.tensor_tensor(posb[:], posb[:], B("cls"), ALU.add))
                pool.wait_ge(s["zn"], t + 1)
                l = link(pool, "h0", N_H0 * t)
                l(g.tensor_tensor(zn[:, t % 2, :], zn[:, t % 2, :], B("ln2_g"), ALU.mult))
                l(g.tensor_tensor(h[:, t, :], zn[:, t % 2, :], posb[:], ALU.add), False)

            def low_(n):
                if n == 0:
                    pool.wait_ge(s["thr"], 2)
                    pool.wait_ge(s["pj"], T)
                if n >= 2:
                    pool.wait_ge(s["quant"], n - 1)
                g.tensor_scalar(low[:, n % 2, :], wide[:, n * F:(n + 1) * F], gam[:, 6 + n // 2:7 + n // 2], None,
                                ALU.is_lt).then_inc(s["low"], 1)

            def pn0(t):
                pool.wait_ge(s["sum0"], N_SUM * (t + 1))
                p3 = pr0[:, t % 3, :].rearrange("p (n k) -> p n k", k=KK)
                g.tensor_tensor(p3, p3, spread(sm0[:, t % 2, 2, :], 2, [R, H, KK]), ALU.mult).then_inc(s["pn0"], 1)

            def augment(n):
                if n == 0:
                    pool.wait_ge(s["mrow"], 16 * 4 * IM)
                a, b = ((0, 1), (1, T))[n]
                g.tensor_copy(xa[:, a:b, POSITION_AT:MASK_AT], posi[:, n:n + 1, :].broadcast_to([R, b - a, 1])).then_inc(s["aug"], 1)
                g.tensor_copy(xa[:, a:b, TOKEN_AT:XA], C("tok", R).unsqueeze(1).broadcast_to([R, b - a, S])).then_inc(s["aug"], 1)
                g.tensor_copy(xa[:, a:b, MASK_AT:TOKEN_AT], maskrow[:, n:n + 1, :].broadcast_to([R, b - a, S])).then_inc(s["aug"], 1)

            def clear(n):
                pool.wait_ge(s["kv"], T)
                g.memset(qTm[:], 0.0).then_inc(s["qz"], 1)

            def rope_sum(t):
                pool.wait_ge(s["rope"], 2 * (t + 1))
                g.tensor_tensor(rot[:, t % 2, 0, :], rot[:, t % 2, 0, :], rot[:, t % 2, 1, :],
                                ALU.add).then_inc(s["rope_sum"], 1)

            def kbA(t):
                pool.wait_ge(s["tke"], t + 1)
                if t == 0:
                    pool.wait_ge(s["op0"], T)
                if t >= 2:
                    pool.wait_ge(s["S7"], t - 1)
                g.tensor_tensor(kbd7[:, t % 2, 0, :].rearrange("p (i n k) -> p i n k", i=IM, n=HC),
                                xT[:, t, 0, 0:R].rearrange("p (i k) -> p i k", i=IM).unsqueeze(2).broadcast_to([128, IM, HC, S]),
                                C("head").unsqueeze(1).unsqueeze(3).broadcast_to([128, IM, HC, S]),
                                ALU.mult).then_inc(s["kbA"], 1)

            def vm7_(t):
                pool.wait_ge(s_vrep[t % 3], 16 * 2 * IM * (t // 3 + 1))
                pairs_apart(vm7[:, t % 3, :], vm7[:, t % 3, :], "pair1", 2 * S, IM * PAIRS, "vm7")

            def pn7(t):
                pool.wait_ge(s["sum7"], N_SUM * (t + 1))
                p3 = pr7[:, t % 3, :].rearrange("p (n k) -> p n k", k=S)
                g.tensor_tensor(p3, p3, spread(sm7[:, t % 2, 2, :], 2, [R, H, S]), ALU.mult).then_inc(s["pn7"], 1)

            sweep((lambda t: rsqrt(t, "st1", N_ST1, "rs1", N_RS1), 0),
                  (lambda t: rsqrt(t, "z", N_Z, "rs2", N_RS2, True, True), 3), (h0, 4), (ln_scale(0), AT_CHOICE),
                  (pn0, AT_ATT0 + 4), (low_, 15, 4), (ln_scale(1), AT_FFN), (ln_scale(2), AT_QKV - 1),
                  (rope_sum, AT_QKV + 2), (clear, AT_QKV + 1, 1), (pn7, AT_ATT1 + 3), (augment, AT_FFN + 1, 2),
                  (vm7_, AT_ATT1 + 3), (kbA, AT_ATT1 - 1), (ln_scale(3), AT_ROUTE))

            for i in range(2):
                pool.wait_ge(s["sc"], 1 + 3 * i)
                g.tensor_scalar(t_sc[:, 2 + 4 * i:3 + 4 * i], t_sc[:, 1 + 4 * i:2 + 4 * i], 1.0 / D, RMS_EPS,
                                ALU.mult, ALU.add).then_inc(s["sc"], 1)
                pool.wait_ge(s["sc"], 2 + 3 * i)
                g.tensor_tensor(t_sc[:, 3 + 4 * i:4 + 4 * i], t_sc[:, 2 + 4 * i:3 + 4 * i], mhalf[0:W3, :],
                                ALU.pow).then_inc(s["sc"], 1)

        @block.vector
        def _(dve):
            v = nc.vector

            def norm_stats(t, layer, on, n_on):
                dve.wait_ge(s[on], n_on * (t + 1))
                l = link(dve, f"ln_stats{layer}", N_LNA * t)
                l(v.bn_stats(st[:, t, 0:6], h[:, t, :]))
                l(v.bn_aggr(mv[:, t, :], st[:, t, 0:6]), False)

            def norm(t, layer):
                dve.wait_ge(s[f"ln_scale{layer}"], N_LNR[layer] * (t + 1))
                v.tensor_scalar(xa[:, t, 0:D], h[:, t, :], mv[:, t, 0:1], rs[:, t, 1:2],
                                ALU.subtract, ALU.mult).then_inc(s[f"xn{layer}"], 1)

            def ranks(l, rk, G):
                l(v.tensor_tensor_reduce(rk[:, 119:119 + S], G, C("tok", R), 1.0, 0.0, ALU.mult, ALU.add,
                                         rk[:, 1:2]))
                l(v.tensor_scalar(rk[:, 45:45 + S], G, rk[:, 1:2], None, ALU.is_gt), False)
                l(v.scalar_tensor_tensor(rk[:, 82:82 + S], G, rk[:, 1:2], C("before", R), ALU.is_equal, ALU.mult))
                l(v.tensor_tensor_reduce(rk[:, 119:119 + S], rk[:, 45:45 + S], rk[:, 82:82 + S], 1.0, 0.0,
                                         ALU.add, ALU.add, rk[:, 2:3]))

            def n1(t):
                dve.wait_ge(s_pat[t % 3], 16 * (t // 3 + 1))
                l = link(dve, "st1", N_ST1 * t)
                l(v.bn_stats(st[:, t, 0:6], pat[:, t % 3, 0:PD // 2]), False)
                l(v.bn_stats(st[:, t, 6:12], pat[:, t % 3, PD // 2:PD]))
                l(v.bn_aggr(mv[:, t, :], st[:, t, :]), False)

            def x1(t):
                dve.wait_ge(s["rs1"], N_RS1 * (t + 1))
                v.tensor_scalar(pat[:, t % 3, :], pat[:, t % 3, :], mv[:, t, 0:1], rs[:, t, 1:2],
                                ALU.subtract, ALU.mult).then_inc(s["xh1"], 1)

            def z(t):
                if t == 0:
                    dve.wait_ge(s["biasps"], 1)
                    dve.wait_ge(s["row"], 16)
                    v.tensor_tensor(bp0[:], ps[0:R, 4, 0:D], B("b_proj"), ALU.add).then_inc(s["bp0"], 1)
                    dve.wait_ge(s["bp0"], 1)
                dve.wait_ge(s["pj"], t + 1)
                if t >= 2:
                    dve.wait_ge(s["zn"], t - 1)
                l = link(dve, "z", N_Z * t)
                l(v.tensor_tensor(zb[:, t % 2, :], ps[0:R, 2 + t % 2, 0:D], bp0[:], ALU.add))
                l(v.bn_stats(st[:, t, 0:6], zb[:, t % 2, :]))
                l(v.bn_aggr(mv[:, t, :], st[:, t, 0:6]), False)

            def absum(n):
                dve.wait_ge(s[("w1raw", "w2raw")[n]], 16)
                v.tensor_reduce(gam[:, n:n + 1], wide[:, n * 2 * F:(n + 1) * 2 * F], AX.X, ALU.add,
                                apply_absolute_value=True).then_inc(s["absum"], 1)

            def part_lo(n):
                dve.wait_ge(s["part_hi"], n + 1)
                v.scalar_tensor_tensor(bias_rows, brow[:], V(f"part{n + 1}")[0:3, :], bias_rows, ALU.mult,
                                       ALU.subtract).then_inc(s["part_lo"], 1)

            def vE(t):
                dve.wait_ge(s["imp"], t + 1)
                rk = rk0[:, t % 2, :]
                l = link(dve, "vE", N_VE * t)
                l(v.tensor_scalar(rk[:, 0:1], ps[0:R, 6, 256 + 2 * (t % 2):256 + 2 * (t % 2) + 1], V("bi2")[0:R, :],
                                  None, ALU.add))
                l(v.tensor_scalar(rk[:, 8:8 + S], C("tok", R), rk[:, 0:1], None, ALU.mult), False)

            def rank(t):
                dve.wait_ge(s["G"], t + 1)
                dve.wait_ge(s["imp"], min(t + 2, T))
                rk = rk0[:, t % 2, :]
                l = link(dve, "rank", N_RANK * t)
                ranks(l, rk, ps[0:R, 6, 0:S])
                if t >= 2:
                    dve.wait_ge(s["gx"], t - 1)
                l(v.tensor_scalar(oh0[:, t % 2, :], C("slot0", R), rk[:, 2:3], None, ALU.is_equal), False)

            def scales(n):
                dve.wait_ge(s["gamps"], 1)
                l = link(dve, "thr", 0)
                l(v.tensor_scalar(gam[:, 4:6], ps[:, 3, 508:510], 0.5 / (D * F), 0.5e-5, ALU.mult, ALU.add))
                l(v.tensor_scalar(gam[:, 6:8], gam[:, 4:6], -1.0, None, ALU.mult), False)

            def quantize(n):
                dve.wait_ge(s["low"], n + 1)
                dst = (w1q, w2q)[n // 2][:].rearrange("p c n -> p (c n)")
                v.scalar_tensor_tensor(dst[:, n % 2 * F:(n % 2 + 1) * F], wide[:, n * F:(n + 1) * F],
                                       gam[:, 4 + n // 2:5 + n // 2], low[:, n % 2, :], ALU.is_gt, ALU.subtract
                                       ).then_inc(s["quant"], 1)

            def kb0(t):
                dve.wait_ge(s["kv"], t + 1)
                if t == 0:
                    dve.wait_ge(s["h0"], N_H0 * T)
                if t >= 2:
                    dve.wait_ge(s["S0"], t - 1)
                for m in range(DC):
                    at_ = 256 + 64 * m
                    last = v.scalar_tensor_tensor(
                        kbd0[:, t % 2, m, :].rearrange("p (n k) -> p n k", k=KK),
                        spread(ps[:, 1, at_:at_ + KK], 1, [128, HC, KK]), V("bk")[:, m:m + 1],
                        spread(C("head"), 2, [128, HC, KK]), ALU.add, ALU.mult)
                last.then_inc(s["kb0"], 1)

            def vm0_(t):
                dve.wait_ge(s["kv"], t + 1)
                if t >= 5:
                    dve.wait_ge(s["pv0"], t - 4)
                v.tensor_tensor(vm0[:, t % 5, :].rearrange("p (n j d) -> p n j d", j=2, d=HD),
                                ps[0:2 * KK, 1, 0:D].rearrange("p (n j d) -> p n j d", j=2, d=HD),
                                C("pair0", 2 * KK).unsqueeze(1).unsqueeze(3).broadcast_to([2 * KK, PAIRS, 2, HD]),
                                ALU.mult).then_inc(s["vm0"], 1)

            def softmax_top(t, S_ps, sm, pr, on, pt, name, width):
                dve.wait_ge(s[on], t + 1)
                l = link(dve, name, 2 * t)
                mx = sm[:, t % 2, 0, :].rearrange("p (c n) -> p c n", c=DC)
                l(v.tensor_reduce(mx, S_ps, AX.X, ALU.max))
                if t >= 3:
                    dve.wait_ge(s[pt], t - 2)
                l(v.tensor_tensor(pr[:, t % 3, :].rearrange("p (c n k) -> p c n k", c=DC, k=width), S_ps,
                                  spread(mx, 3, [R, DC, HC, width]), ALU.subtract), False)

            def softmax_sum(t, sm, pr, on, pn, name, width):
                dve.wait_ge(s[on], t + 1)
                l = link(dve, name, N_SUM * t)
                l(v.tensor_reduce(sm[:, t % 2, 1, :], pr[:, t % 3, :].rearrange("p (n k) -> p n k", k=width),
                                  AX.X, ALU.add))
                if t >= 2:
                    dve.wait_ge(s[pn], t - 1)
                l(v.reciprocal(sm[:, t % 2, 2, :], sm[:, t % 2, 1, :]), False)

            def residual(t, layer, bank, on, name):
                dve.wait_ge(s[on], t + 1)
                v.tensor_tensor(h[:, t, :], ps[0:R, bank, 0:D], h[:, t, :], ALU.add).then_inc(s[name], 1)

            S0_ps = ps[0:R, 2:4, 0:HC * KK].rearrange("p c (n k) -> p c n k", k=KK)

            def xlo_(t):
                dve.wait_ge(s["xhi"], t + 1)
                v.tensor_tensor(xlo[:, t // 2 % 2, :, t % 2, 0:R], ps[:, 0, 0:DC * RP].rearrange("p (c r) -> p c r", c=DC)[:, :, 0:R],
                                xhi[:, t // 2 % 2, :, t % 2, 0:R].bitcast(F32), ALU.subtract).then_inc(s["xlo"], 1)

            def hlo_(t, n, on, name):
                dve.wait_ge(s[on], t + 1)
                at_, src = quarter(t, n)
                v.scalar_tensor_tensor(hlo[at_], src, 0.0, hhi[at_].bitcast(F32), ALU.max, ALU.subtract
                                       ).then_inc(s[name], 1)

            def rope(t):
                dve.wait_ge(s["qkv"], t + 1)
                if t >= 2:
                    dve.wait_ge(s["tq"], t - 1)
                n = 2 * H
                qk = ps[0:R, 5, :].rearrange("p (n e o) -> p n e o", n=n, o=2)
                v.tensor_tensor(rot[:, t % 2, 0, :].rearrange("p (n d) -> p n d", n=n),
                                ps[0:R, 5, :].rearrange("p (n d) -> p n d", n=n),
                                spread(C("cos", R), 1, [R, n, HD]), ALU.mult).then_inc(s["rope"], 1)
                v.tensor_tensor(rot[:, t % 2, 1, :].rearrange("p (n e o) -> p n e o", n=n, o=2), qk[:, :, :, ::-1],
                                C("sin", R).rearrange("p (e o) -> p e o", o=2).unsqueeze(1).broadcast_to([R, n, HD // 2, 2]),
                                ALU.mult).then_inc(s["rope"], 1)

            def kbB(t):
                dve.wait_ge(s["tke"], t + 1)
                if t == 0:
                    dve.wait_ge(s["op0"], T)
                if t >= 2:
                    dve.wait_ge(s["S7"], t - 1)
                v.tensor_tensor(kbd7[:, t % 2, 1, :].rearrange("p (i n k) -> p i n k", i=IM, n=HC),
                                xT[:, t, 1, 0:R].rearrange("p (i k) -> p i k", i=IM).unsqueeze(2).broadcast_to([128, IM, HC, S]),
                                C("head").unsqueeze(1).unsqueeze(3).broadcast_to([128, IM, HC, S]),
                                ALU.mult).then_inc(s["kbB"], 1)

            S7_ps = ps[0:R, 0:DC, 0:HC * S].rearrange("p c (n k) -> p c n k", k=S)

            def rw(t):
                l = link(dve, "rw", N_RW * t)
                dve.wait_ge(s["xn3"], t + 1)
                l(v.tensor_tensor_reduce(junk[:], xa[:, t, 0:D], B("router_w"), 1.0, 0.0, ALU.mult, ALU.add,
                                         rk9[:, t % 2, 0:1]))
                l(v.tensor_scalar(xa[:, t, D:D + 1], rk9[:, t % 2, 0:1], V("router_b")[0:R, :], None, ALU.add))
                l(v.tensor_scalar(rk9[:, t % 2, 8:8 + S], C("tok", R), xa[:, t, D:D + 1], None, ALU.mult), False)

            def ohte(t):
                dve.wait_ge(s["oht"], t + 1)
                dve.wait_ge(s["G9"], min(t + 2, T))
                v.tensor_copy(ohT[:, t, 0:R], ps[0:W3, 3, 128:128 + R]).then_inc(s["ohte"], 1)

            def rank9(t):
                dve.wait_ge(s["G9"], t + 1)
                rk = rk9[:, t % 2, :]
                G = ps[0:R, 3, 64 * (t % 2):64 * (t % 2) + S]
                l = link(dve, "rank9", N_RANK9 * t)
                ranks(l, rk, G)
                l(v.tensor_scalar(rk[:, 45:45 + S], G, rk[:, 1:2], None, ALU.is_ge))
                l(v.tensor_reduce(rk[:, 3:4], rk[:, 45:45 + S], AX.X, ALU.add))
                if t >= 2:
                    dve.wait_ge(s["oht"], t - 1)
                a = (T - 1 - t) * IM * NSEL
                l(v.tensor_scalar(oh9[:, t % 2, :], C("slot1", R)[:, a:a + W3], rk[:, 2:3], None, ALU.is_equal), False)
                l(v.tensor_scalar(rk[:, 4:5], rk[:, 3:4], KSEL - 0.5, None, ALU.is_gt))
                v.scalar_tensor_tensor(h[:, t, :], xa[:, t, 0:D], rk[:, 4:5], h[:, t, :], ALU.mult,
                                       ALU.add).then_inc(s["base"], 1)

            h5 = lambda t: residual(t, 1, 3, "w2", "h5")
            sweep((lambda t: norm(t, 2), AT_QKV + 1), (lambda t: norm(t, 1), AT_FFN + 1), (only(h5, 1), AT_FFN + 5),
                  (only(h5, 0), AT_FFN + 5), (x1, 1), (lambda t: residual(t, 2, 7, "op7", "h7"), AT_ATT1 + 6),
                  (lambda t: residual(t, 0, 7, "op0", "h4"), AT_ATT0 + 7), (kb0, AT_ATT0 + 1), (vm0_, AT_ATT0 + 1),
                  (kbB, AT_ATT1), (n1, 0), (z, 3), (lambda n: part_lo(1), 9, 1), (absum, 11, 2), (part_lo, 7, 1),
                  (lambda t: norm(t, 0), AT_CHOICE + 1), (lambda t: norm_stats(t, 0, "h0", N_H0), AT_CHOICE),
                  (lambda t: norm_stats(t, 1, "h4", 1), AT_FFN), (lambda t: norm_stats(t, 2, "h5", 1), AT_QKV),
                  (lambda t: norm_stats(t, 3, "h7", 1), AT_ROUTE), (ohte, AT_ROUTE + 4), (rank, AT_CHOICE + 4),
                  (rank9, AT_ROUTE + 3), (rw, AT_ROUTE + 1), (vE, AT_CHOICE + 3), (scales, 14, 1), (quantize, 16, 4),
                  (lambda t: softmax_top(t, S7_ps, sm7, pr7, "S7", "pt7", "smx7", S), AT_ATT1 + 1),
                  (lambda t: softmax_sum(t, sm7, pr7, "ex7", "pn7", "sum7", S), AT_ATT1 + 2),
                  (lambda t: softmax_sum(t, sm0, pr0, "ex0", "pn0", "sum0", KK), AT_ATT0 + 3), (xlo_, AT_FFN + 1),
                  (rope, AT_QKV + 2), (lambda t: hlo_(t, 0, "hia", "loa"), AT_FFN + 3, T + 1),
                  (lambda t: hlo_(t, 1, "hib", "lob"), AT_FFN + 3, T + 1),
                  (lambda t: softmax_top(t, S0_ps, sm0, pr0, "S0", "pt0", "smx0", KK), AT_ATT0 + 2))

            l = link(dve, "tv", 0)
            x_ = t_x[:, 0:D]
            dve.wait_ge(s["acc"], T)
            l(v.tensor_copy(t_x, ps[0:W3, 2, 0:XA]))
            v.tensor_tensor_reduce(t_hn, x_, x_, 1.0, 0.0, ALU.mult, ALU.add, t_sc[:, 1:2]).then_inc(s["sc"], 1)
            f = [t_f[:, i, :] for i in range(6)]
            turn = (6.28125, 0.0019350051879882812, 3.0199159819e-07)
            magic = 12582912.0
            l(v.tensor_scalar(f[0], C("inv", W3), t_x[:, POSITION_AT:MASK_AT], None, ALU.mult))
            l(v.tensor_scalar(f[1], f[0], float(0.5 / np.pi), magic, ALU.mult, ALU.add))
            l(v.tensor_scalar(f[1], f[1], -magic, None, ALU.add))
            for part in turn:
                l(v.scalar_tensor_tensor(f[0], f[1], -part, f[0], ALU.mult, ALU.add))
            l(v.tensor_scalar(f[0], f[0], -3.1415925, 3.1415925, ALU.max, ALU.min))
            l(v.scalar_tensor_tensor(f[2], f[0], -1.0, f[0], ALU.mult, ALU.max))
            v.tensor_scalar(f[2], f[2], -1.0, float(np.pi / 2), ALU.mult, ALU.add).then_inc(s["t_ang"], 1)
            dve.wait_ge(s["sc"], 3)
            v.scalar_tensor_tensor(t_hn, x_, t_sc[:, 3:4], B("ln1", W3), ALU.mult, ALU.mult).then_inc(s["t_hn"], 1)
            l(v.tensor_tensor_reduce(t_s3, t_x[:, TOKEN_AT:XA], t_x[:, MASK_AT:TOKEN_AT], 1.0 / SCALE, 0.0, ALU.mult,
                                     ALU.add, t_mm[:, 0:1]))
            dve.wait_ge(s["t_tok"], 1)
            for j in range(1, NSEL):
                l(v.tensor_tensor_reduce(t_s3, ps[0:W3, 5, (j - 1) * S:j * S], t_x[:, MASK_AT:TOKEN_AT], 1.0 / SCALE, 0.0,
                                         ALU.mult, ALU.add, t_mm[:, j:j + 1]))
            dve.wait_ge(s["t_sin"], 2)
            l(v.tensor_tensor(f[3], f[3], C("sign", W3), ALU.mult))
            dve.wait_ge(s["t_qkv"], 1)
            n = 2 * H
            qk = t_qkv[:, 0:2, :].rearrange("p a d -> p (a d)")
            l(v.tensor_tensor(qk.rearrange("p (n d) -> p n d", n=n), ps[0:W3, 6, :].rearrange("p (n d) -> p n d", n=n),
                              spread(f[4], 1, [W3, n, HD]), ALU.mult), False)
            l(v.tensor_tensor(t_rot.rearrange("p (n a d) -> p n a d", n=n, a=2),
                              ps[0:W3, 6, :].rearrange("p (n a d) -> p n a d", n=n, a=2)[:, :, ::-1, :],
                              f[3].rearrange("p (a d) -> p a d", a=2).unsqueeze(1).broadcast_to([W3, n, 2, HD // 2]),
                              ALU.mult))
            v.tensor_tensor(qk, qk, t_rot, ALU.add).then_inc(s["t_rot"], 1)
            dve.wait_ge(s["t_rot"], 1)
            q = t_qkv[:, 0, :]
            l(v.tensor_tensor(t_p[:, 0, :], q, t_qkv[:, 1, :], ALU.mult), False)
            dve.wait_ge(s["t_kn"], 1)
            l(v.tensor_tensor(t_p[:, 1:NSEL, :], ps[0:W3, 0, :].rearrange("p (j d) -> p j d", d=D),
                              spread(q, 1, [W3, NSEL - 1, D]), ALU.mult))
            l(v.tensor_reduce(t_s, t_p.rearrange("p j (n d) -> p j n d", n=H), AX.X, ALU.add))
            l(v.tensor_tensor(t_s, t_s, spread(t_mm, 2, [W3, NSEL, H]), ALU.add))
            l(v.tensor_reduce(t_mx[:, 0, :], t_s.rearrange("p j n -> p n j"), AX.X, ALU.max))
            v.tensor_tensor(t_s, t_s, spread(t_mx[:, 0, :], 1, [W3, NSEL, H]), ALU.subtract).then_inc(s["t_sub"], 1)
            dve.wait_ge(s["t_exp"], 1)
            l(v.tensor_reduce(t_mx[:, 1, :], t_s.rearrange("p j n -> p n j"), AX.X, ALU.add))
            l(v.reciprocal(t_mx[:, 2, :], t_mx[:, 1, :]))
            l(v.tensor_tensor(t_s, t_s, spread(t_mx[:, 2, :], 1, [W3, NSEL, H]), ALU.mult))
            l(v.tensor_tensor(t_pv[:, 0, :].rearrange("p (n d) -> p n d", n=H),
                              t_qkv[:, 2, :].rearrange("p (n d) -> p n d", n=H),
                              spread(t_s[:, 0, :], 2, [W3, H, HD]), ALU.mult), False)
            dve.wait_ge(s["t_vn"], 1)
            l(v.tensor_tensor(t_pv[:, 1:NSEL, :].rearrange("p j (n d) -> p j n d", n=H),
                              ps[0:W3, 1, :].rearrange("p (j n d) -> p j n d", j=NSEL - 1, n=H),
                              spread(t_s[:, 1:NSEL, :], 3, [W3, NSEL - 1, H, HD]), ALU.mult))
            v.tensor_reduce(t_o, t_pv.rearrange("p j d -> p d j"), AX.X, ALU.add).then_inc(s["t_o"], 1)
            dve.wait_ge(s["t_wo"], 1)
            l(v.tensor_tensor(t_x1, ps[0:W3, 2, 0:D], x_, ALU.add))
            v.tensor_tensor_reduce(t_hn, t_x1, t_x1, 1.0, 0.0, ALU.mult, ALU.add, t_sc[:, 5:6]).then_inc(s["sc"], 1)
            dve.wait_ge(s["sc"], 6)
            v.scalar_tensor_tensor(t_hn, t_x1, t_sc[:, 7:8], B("ln2", W3), ALU.mult, ALU.mult).then_inc(s["t_hn"], 1)
            dve.wait_ge(s["t_w2"], 1)
            l(v.tensor_tensor(t_y, ps[0:W3, 6, 0:D], t_x1, ALU.add))
            v.tensor_scalar(t_y, t_y, t_x[:, WEIGHT_AT:POSITION_AT], None, ALU.mult).then_inc(s["t_y"], 1)
            for t in range(T):
                dve.wait_ge(s["t_put"], t + 1)
                v.tensor_tensor(h[:, t, :], ps[0:R, t % 4, 0:D], h[:, t, :], ALU.add).then_inc(s["fin"], 1)

        @block.scalar
        def _(act):
            a = nc.scalar

            def rows_of(bank, n, w=RP, used=R):
                return ps[:, bank, 0:n * w].rearrange("p (c r) -> p c r", c=n)[:, :, 0:used]

            def gw_(t):
                if t == 0:
                    act.wait_ge(s["wproj"], 16)
                    act.wait_ge(s["vec"], 16)
                    for c in range(PC):
                        last = a.activation(gW[:, c, :], w_proj[:, c, :], ACT.Copy, scale=V("ln1_g")[:, c:c + 1])
                    last.then_inc(s["gw"], 1)

            def zn_(t):
                act.wait_ge(s["rs2"], N_RS2 * (t + 1))
                if t >= 2:
                    act.wait_ge(s["h0"], N_H0 * (t - 1))
                a.activation(zn[:, t % 2, :], zb[:, t % 2, :], ACT.Identity, bias=rs[:, t, 0:1],
                             scale=rs[:, t, 1:2]).then_inc(s["zn"], 1)

            def norm(t, layer):
                act.wait_ge(s[f"ln_scale{layer}"], N_LNR[layer] * (t + 1))
                a.activation(xa[:, t, 0:D], h[:, t, :], ACT.Identity, bias=rs[:, t, 0:1],
                             scale=rs[:, t, 1:2]).then_inc(s[f"xn{layer}"], 1)

            def xT1_(t):
                act.wait_ge(s["tr1"], t + 1)
                if t >= 2:
                    act.wait_ge(s["pj"], t - 1)
                a.copy(pT[:, t % 2, :, 0:R].rearrange("p (b c) r -> p b c r", b=2),
                       ps[:, 0:2, 0:3 * RP].rearrange("p b (c r) -> p b c r", c=3)[:, :, :, 0:R]).then_inc(s["xT1"], 1)

            def xT2_(t):
                act.wait_ge(s["T2"], t + 1)
                a.copy(xT[:, t, :, 0:R], rows_of(4, DC)).then_inc(s["xT2"], 1)

            def hid(t):
                act.wait_ge(s["hidp"], t + 1)
                if t >= 2:
                    act.wait_ge(s["imp"], t - 1)
                a.activation(hT[:, t % 2, 0:R], ps[:, 5, 0:R], ACT.Relu, bias=V("bi1")).then_inc(s["hid"], 1)

            def xs_(t):
                act.wait_ge(s["gx"], t + 1)
                a.copy(xsT[:, t, :, :].rearrange("p c (n k) -> p c n k", n=2),
                       rows_of(7, DC, 64, KK).unsqueeze(2).broadcast_to([128, DC, 2, KK])).then_inc(s["xs"], 1)

            def part_hi(n):
                if n == 0:
                    act.wait_ge(s["brows"], 16)
                else:
                    act.wait_ge(s["part_lo"], n)
                a.copy(brow[:], bias_rows).then_inc(s["part_hi"], 1)

            def q0(t):
                act.wait_ge(s["q"], t + 1)
                if t == 0:
                    act.wait_ge(s["h0"], N_H0 * T)
                if t >= 2:
                    act.wait_ge(s["S0"], t - 1)
                for m in range(DC):
                    last = a.activation(qT0[:, t % 2, m, 0:R], ps[:, 0, m * RP:m * RP + R], ACT.Identity,
                                        bias=V("bq")[:, m:m + 1])
                last.then_inc(s["q0"], 1)

            def exps(t, pr, on, name):
                act.wait_ge(s[on], 2 * (t + 1))
                a.activation(pr[:, t % 3, :], pr[:, t % 3, :], ACT.Exp, scale=SCALE).then_inc(s[name], 1)

            def probsT(t, dst, n_rows, on, free, name):
                act.wait_ge(s[on], t + 1)
                if t >= 2:
                    act.wait_ge(s[free], t - 1)
                a.copy(dst[:, t % 2, :, 0:R].rearrange("p (b c) r -> p b c r", b=2),
                       ps[0:n_rows, 4:6, 0:PAIRS // 2 * RP].rearrange("p b (c r) -> p b c r", b=2, r=RP)[:, :, :, 0:R]
                       ).then_inc(s[name], 1)

            def outT(t, dst, on, free, name):
                act.wait_ge(s[on], t + 1)
                if t >= 2:
                    act.wait_ge(s[free], t - 1)
                a.copy(dst[:, t % 2, :, 0:R], rows_of(6, DC)).then_inc(s[name], 1)

            def xhi_(t):
                act.wait_ge(s["T5"], t + 1)
                if t >= 4:
                    act.wait_ge(s["w1b"], 2 * (t // 2) - 2)
                a.copy(xhi[:, t // 2 % 2, :, t % 2, 0:R], rows_of(0, DC)).then_inc(s["xhi"], 1)

            def hhi_(t, n, on, name):
                act.wait_ge(s[on], t + 1)
                if t >= 2:
                    act.wait_ge(s["w2"], 2 * (t // 2))
                at_, src = quarter(t, n)
                a.activation(hhi[at_], src, ACT.Relu).then_inc(s[name], 1)

            def xT6_(t):
                act.wait_ge(s["T6"], t + 1)
                if t >= 2:
                    act.wait_ge(s["qkv"], t - 1)
                a.copy(xT6[:, t % 2, :, 0:R], rows_of(4, DC)).then_inc(s["xT6"], 1)

            def v6_(t):
                act.wait_ge(s["qkv"], t + 1)
                a.copy(v1[:, t, :], ps[0:R, 6, 0:D]).then_inc(s["v6"], 1)

            def tqe(t):
                act.wait_ge(s["tq"], t + 1)
                view = rows_of(7, 2 * DC)
                a.copy(q6[:, t, :, 0:R], view[:, 0:DC, :]).then_inc(s["tqe"], 1)
                a.copy(xT[:, t, :, 0:R], view[:, DC:2 * DC, :]).then_inc(s["tke"], 1)

            def qm7(t):
                act.wait_ge(s["tqe"], t + 1)
                if t == 0:
                    act.wait_ge(s["qz"], 1)
                if t >= 2:
                    act.wait_ge(s["S7"], t - 1)
                for m in range(DC):
                    flat = qTm[:, t % 2, m, :, :].rearrange("p i r -> p (i r)")
                    base = flat[:, 0:S]
                    dst = bass.AP(base.tensor, base.offset, [list(base.ap[0]), [RP + S, IM], [1, S]])
                    last = a.copy(dst, q6[:, t, m, 0:R].rearrange("p (i r) -> p i r", i=IM))
                last.then_inc(s["qm7"], 1)

            sweep((gw_, 0, 1), (lambda t: norm(t, 3), AT_ROUTE + 1), (xT1_, 1), (zn_, 4), (part_hi, 6, 1),
                  (lambda n: part_hi(1), 8, 1), (lambda n: part_hi(2), 9, 1), (q0, AT_ATT0 + 1),
                  (xs_, AT_CHOICE + 6), (lambda t: probsT(t, PT0, 2 * KK, "pt0", "pv0", "PT0"), AT_ATT0 + 5),
                  (xT2_, AT_CHOICE + 1), (hid, AT_CHOICE + 2), (lambda t: exps(t, pr0, "smx0", "ex0"), AT_ATT0 + 3),
                  (lambda t: outT(t, oT0, "pv0", "op0", "oT0"), AT_ATT0 + 6), (xT6_, AT_QKV + 1), (xhi_, AT_FFN + 1),
                  (v6_, AT_QKV + 2), (lambda t: hhi_(t, 0, "w1a", "hia"), AT_FFN + 3, T + 1),
                  (lambda t: hhi_(t, 1, "w1b", "hib"), AT_FFN + 3, T + 1),
                  (lambda t: probsT(t, PT7, 2 * S, "pt7", "pv7", "PT7"), AT_ATT1 + 4), (tqe, AT_QKV + 3),
                  (lambda t: outT(t, oT7, "pv7", "op7", "oT7"), AT_ATT1 + 5),
                  (lambda t: exps(t, pr7, "smx7", "ex7"), AT_ATT1 + 2), (qm7, AT_ATT1))
            act.wait_ge(s["t_ang"], 1)
            a.activation(t_f[:, 3, :], t_f[:, 0, :], ACT.Sin).then_inc(s["t_sin"], 1)
            a.activation(t_f[:, 4, :], t_f[:, 2, :], ACT.Sin).then_inc(s["t_sin"], 1)
            act.wait_ge(s["t_T"], 1)
            a.copy(t_hnT, ps[:, 4, 0:DC * W3].rearrange("p (c r) -> p c r", c=DC)).then_inc(s["t_hnT"], 1)
            act.wait_ge(s["t_qkv"], 1)
            a.copy(t_qkv[:, 2, :], ps[0:W3, 7, 0:D]).then_inc(s["t_v"], 1)
            act.wait_ge(s["t_sub"], 1)
            a.activation(t_s, t_s, ACT.Exp, scale=SCALE).then_inc(s["t_exp"], 1)
            act.wait_ge(s["t_To"], 1)
            a.copy(t_oT, ps[:, 4, 0:DC * W3].rearrange("p (c r) -> p c r", c=DC)).then_inc(s["t_oT"], 1)
            act.wait_ge(s["t_T"], 2)
            a.copy(t_hnT, ps[:, 3, 0:DC * W3].rearrange("p (c r) -> p c r", c=DC)).then_inc(s["t_hnT"], 1)
            act.wait_ge(s["t_w1"], 1)
            a.activation(t_g.rearrange("p (b c) r -> p b (c r)", b=2), ps[:, 4:6, 0:4 * W3],
                         ACT.Gelu_apprx_tanh).then_inc(s["t_g"], 1)

        @block.tensor
        def _(pe):
            m_ = nc.tensor
            ident = C("ident")

            def transposes(bank, src, n, name, t_on=None):
                for c in range(n):
                    last = m_.transpose(ps[:, bank, c * RP:c * RP + R], src[:, c * 128:(c + 1) * 128], ident[0:R, 0:R])
                last.then_inc(s[name], 1)

            def add_bias(dst, rows_n, at_):
                m_.matmul(dst, ones_b[:, 0:rows_n], brow[:, at_:at_ + D], start=True, stop=False)

            def keep_warm(n):
                for _ in range(n):
                    m_.matmul(ps[:, 7, 0:128], ones[:], ones[:], start=True, stop=True)

            pe.wait_ge(s["pool_set"], 2)

            def tr1(t):
                pe.wait_ge(s["xh1"], t + 1)
                if t == 0:
                    pe.wait_ge(s["cst"], 16)
                if t >= 1:
                    pe.wait_ge(s["xT1"], t)
                for c in range(PC):
                    last = m_.transpose(ps[:, c // 3, (c % 3) * RP:(c % 3) * RP + R],
                                        pat[:, t % 3, c * 128:(c + 1) * 128], ident[0:R, 0:R])
                last.then_inc(s["tr1"], 1)
                if t == 0:
                    pe.wait_ge(s["wproj"], 16)
                    pe.wait_ge(s["vec"], 16)
                    for c in range(PC):
                        last = m_.matmul(ps[0:R, 4, 0:D], V("ln1_b")[:, c:c + 1].broadcast_to([128, R]),
                                         w_proj[:, c, :], start=(c == 0), stop=(c == PC - 1))
                    last.then_inc(s["biasps"], 1)

            def pj(t):
                pe.wait_ge(s["xT1"], t + 1)
                if t == 0:
                    pe.wait_ge(s["gw"], 1)
                if t >= 2:
                    pe.wait_ge(s["z"], N_Z * (t - 1))
                for c in range(PC):
                    last = m_.matmul(ps[0:R, 2 + t % 2, 0:D], pT[:, t % 2, c, 0:R], gW[:, c, :],
                                     start=(c == 0), stop=(c == PC - 1))
                last.then_inc(s["pj"], 1)

            def T2(t):
                pe.wait_ge(s["xn0"], t + 1)
                if t == 0:
                    pe.wait_ge(s["bp0"], 1)
                if t >= 1:
                    pe.wait_ge(s["xT2"], t)
                transposes(4, xa[:, t, 0:D], DC, "T2")

            def hidp(t):
                pe.wait_ge(s["xT2"], t + 1)
                if t == 0:
                    pe.wait_ge(s["w0"], 16 * 5)
                if t >= 1:
                    pe.wait_ge(s["hid"], t)
                for c in range(DC):
                    last = m_.matmul(ps[:, 5, 0:R], wi1[:, c, :], xT[:, t, c, 0:R], start=(c == 0), stop=(c == DC - 1))
                last.then_inc(s["hidp"], 1)

            def imp(t):
                pe.wait_ge(s["hid"], t + 1)
                if t >= 1:
                    pe.wait_ge(s["vE"], N_VE * t)
                if t >= 2:
                    pe.wait_ge(s["rank"], N_RANK * (t - 1))
                m_.matmul(ps[0:R, 6, 256 + 2 * (t % 2):256 + 2 * (t % 2) + 1], hT[:, t % 2, 0:R], V("wi2"), start=True,
                          stop=True).then_inc(s["imp"], 1)

            def G(t):
                pe.wait_ge(s["vE"], N_VE * (t + 1))
                if t >= 1:
                    pe.wait_ge(s["rank"], N_RANK * t)
                m_.matmul(ps[0:R, 6, 0:S], C("same", R), rk0[:, t % 2, 8:8 + S], start=True,
                          stop=True).then_inc(s["G"], 1)

            def gx(t):
                pe.wait_ge(s["rank"], N_RANK * (t + 1))
                if t >= 1:
                    pe.wait_ge(s["xs"], t)
                for c in range(DC):
                    last = m_.matmul(ps[:, 7, 64 * c:64 * c + KK], xa[:, t, c * 128:(c + 1) * 128], oh0[:, t % 2, :],
                                     start=True, stop=True)
                last.then_inc(s["gx"], 1)

            def gamps(n):
                pe.wait_ge(s["absum"], 2)
                pe.wait_ge(s["pool_set"], 2)
                pe.wait_ge(s["z"], N_Z * T)
                m_.matmul(ps[:, 3, 508:510], ones[:], gam[:, 0:2], start=True, stop=True).then_inc(s["gamps"], 1)

            def q_(t):
                pe.wait_ge(s["xT2"], t + 1)
                if t == 0:
                    pe.wait_ge(s["xT1"], T)
                if t >= 1:
                    pe.wait_ge(s["q0"], t)
                for m in range(DC):
                    cols = slice(m * 128, (m + 1) * 128)
                    for c in range(DC):
                        last = m_.matmul(ps[:, 0, m * RP:m * RP + R], wq0[:, c, cols], xT[:, t, c, 0:R],
                                         start=(c == 0), stop=(c == DC - 1))
                last.then_inc(s["q"], 1)

            def kv_(t):
                pe.wait_ge(s["xs"], t + 1)
                if t == 0:
                    pe.wait_ge(s["part_hi"], 3)
                if t >= 1:
                    pe.wait_ge(s["vm0"], t)
                    pe.wait_ge(s["kb0"], t)
                for m in range(DC):
                    for c in range(DC):
                        m_.matmul(ps[:, 1, 256 + 64 * m:256 + 64 * m + KK], wk0[:, c, m * 128:(m + 1) * 128],
                                  xsT[:, t, c, 0:KK], start=(c == 0), stop=(c == DC - 1))
                add_bias(ps[0:2 * KK, 1, 0:D], 2 * KK, BV_AT)
                for c in range(DC):
                    last = m_.matmul(ps[0:2 * KK, 1, 0:D], xsT[:, t, c, :], wv0[:, c, :], start=False, stop=(c == DC - 1))
                last.then_inc(s["kv"], 1)

            def S0(t):
                pe.wait_ge(s["q0"], t + 1)
                pe.wait_ge(s["kb0"], t + 1)
                if t == 0:
                    pe.wait_ge(s["cast"], 3)
                    pe.wait_ge(s["thr"], 2)
                if t >= 1:
                    pe.wait_ge(s["smx0"], 2 * t)
                for m in range(DC):
                    dst = ps[0:R, 2 + m, 0:HC * KK]
                    m_.matmul(dst, qT0[:, t % 2, m, 0:R], kbd0[:, t % 2, m, :], start=True, stop=False)
                    last = m_.matmul(dst, ident_b[:], other_b[:].unsqueeze(1).broadcast_to([R, HC, KK]),
                                     start=False, stop=True)
                last.then_inc(s["S0"], 1)

            def pT_(t, pr, w, on, free, name, before):
                pe.wait_ge(s[on], t + 1)
                if t == 0:
                    for done, n in before:
                        pe.wait_ge(s[done], n)
                if t >= 1:
                    pe.wait_ge(s[free], t)
                for p in range(PAIRS):
                    o = (p % 4) * RP
                    last = m_.transpose(ps[0:w, 4 + p // 4, o:o + R], pr[:, t % 3, p * w:(p + 1) * w], ident[0:R, 0:R])
                last.then_inc(s[name], 1)

            def pv0(t):
                pe.wait_ge(s["PT0"], t + 1)
                pe.wait_ge(s["vm0"], t + 1)
                if t == 0:
                    pe.wait_ge(s["rank"], N_RANK * T)
                if t >= 1:
                    pe.wait_ge(s["oT0"], t)
                for p in range(PAIRS):
                    q = 32 * (p % 4)
                    o = (p // 4) * RP
                    last = m_.matmul(ps[q:q + 32, 6, o:o + R], vm0[:, t % 5, 32 * p:32 * p + 32], PT0[:, t % 2, p, 0:R],
                                     start=True, stop=True)
                last.then_inc(s["pv0"], 1)

            def project(t, oT, w, bias_at, on, free, name, before):
                pe.wait_ge(s[on], t + 1)
                if t == 0:
                    pe.wait_ge(s[before], T)
                if t >= 1:
                    pe.wait_ge(s[free], t)
                add_bias(ps[0:R, 7, 0:D], R, bias_at)
                for c in range(DC):
                    last = m_.matmul(ps[0:R, 7, 0:D], oT[:, t % 2, c, 0:R], w[:, c, :], start=False, stop=(c == DC - 1))
                last.then_inc(s[name], 1)

            def T5(t):
                pe.wait_ge(s["xn1"], t + 1)
                if t == 0:
                    pe.wait_ge(s["q0"], T)
                if t >= 1:
                    pe.wait_ge(s["xlo"], t)
                transposes(0, xa[:, t, 0:D], DC, "T5")

            def w1(t, n, free, name):
                pair = t // 2
                tiles = min(2, T - 2 * pair)
                pe.wait_ge(s["xlo"], 2 * pair + tiles)
                if t == 0:
                    pe.wait_ge(s["smx0"], 2 * T)
                    pe.wait_ge(s["vm0"], T)
                    pe.wait_ge(s["quant"], 4)
                    pe.wait_ge(s["pool_set"], 5)
                if t >= 1:
                    pe.wait_ge(s[free], t)
                for i in range(2):
                    f = 2 * (2 * (t % 2) + n) + i
                    dst = ps[:, 1 + n, 2 * i * RP:(2 * i + tiles) * RP]
                    m_.matmul(dst, brow[:, f * 128:(f + 1) * 128], ones_b[:, 0:tiles * RP], start=True, stop=False)
                    for c in range(DC):
                        for x in (xhi, xlo):
                            last = m_.matmul(dst, w1q[:, c, f * 128:(f + 1) * 128],
                                             x[:, pair % 2, c, 0:tiles, :].rearrange("p n r -> p (n r)"),
                                             start=False, stop=(c == DC - 1 and x is xlo))
                last.then_inc(s[name], 1)

            def w2(t):
                pe.wait_ge(s["loa"], 2 * (t // 2) + 2)
                pe.wait_ge(s["lob"], 2 * (t // 2) + 2)
                if t >= 1:
                    pe.wait_ge(s["h5"], t)
                add_bias(ps[0:R, 3, 0:D], R, B2_AT)
                for f in range(FC):
                    for x in (hhi, hlo):
                        last = m_.matmul(ps[0:R, 3, 0:D], x[:, f, t % 2, 0:R], w2q[:, f, :], start=False,
                                         stop=(f == FC - 1 and x is hlo))
                last.then_inc(s["w2"], 1)

            def T6(t):
                pe.wait_ge(s["xn2"], t + 1)
                if t == 0:
                    pe.wait_ge(s["PT0"], T)
                if t >= 1:
                    pe.wait_ge(s["xT6"], t)
                transposes(4, xa[:, t, 0:D], DC, "T6")

            def qkv(t):
                pe.wait_ge(s["xT6"], t + 1)
                if t == 0:
                    pe.wait_ge(s["wl1"], 32)
                    pe.wait_ge(s["oT0"], T)
                if t >= 1:
                    pe.wait_ge(s["rope"], 2 * t)
                    pe.wait_ge(s["v6"], t)
                for bank, cols in ((5, slice(0, 2 * D)), (6, slice(2 * D, 3 * D))):
                    dst = ps[0:R, bank, 0:cols.stop - cols.start]
                    m_.matmul(dst, ones_b[:, 0:R], brow[:, BQKV_AT + cols.start:BQKV_AT + cols.stop], start=True, stop=False)
                    for c in range(DC):
                        last = m_.matmul(dst, xT6[:, t % 2, c, 0:R], wqkv[:, c, cols], start=False, stop=(c == DC - 1))
                last.then_inc(s["qkv"], 1)

            def tq(t):
                pe.wait_ge(s["rope_sum"], t + 1)
                if t == 0:
                    pe.wait_ge(s["h4"], T)
                if t >= 1:
                    pe.wait_ge(s["tke"], t)
                transposes(7, rot[:, t % 2, 0, :], 2 * DC, "tq")

            def S7(t):
                pe.wait_ge(s["qm7"], t + 1)
                pe.wait_ge(s["kbA"], t + 1)
                pe.wait_ge(s["kbB"], t + 1)
                if t == 0:
                    pe.wait_ge(s["h5"], T)
                if t >= 1:
                    pe.wait_ge(s["smx7"], 2 * t)
                for m in range(DC):
                    dst = ps[0:R, m, 0:HC * S]
                    for i in range(IM):
                        m_.matmul(dst, qTm[:, t % 2, m, i, 0:R], kbd7[:, t % 2, m, i * HC * S:(i + 1) * HC * S],
                                  start=(i == 0), stop=False)
                    last = m_.matmul(dst, ident_b[:], causal_b[:].unsqueeze(1).broadcast_to([R, HC, S]),
                                     start=False, stop=True)
                last.then_inc(s["S7"], 1)

            def pv7(t):
                pe.wait_ge(s["PT7"], t + 1)
                pe.wait_ge(s["vm7"], t + 1)
                if t == 0:
                    pe.wait_ge(s["v6"], T)
                if t >= 1:
                    pe.wait_ge(s["oT7"], t)
                for p in range(PAIRS):
                    q = 32 * (p % 4)
                    for i in range(IM):
                        o = (p // 4) * RP + i * S
                        a_ = i * D + 32 * p
                        last = m_.matmul(ps[q:q + 32, 6, o:o + S], vm7[:, t % 3, a_:a_ + 32],
                                         PT7[:, t % 2, p, i * S:(i + 1) * S], start=True, stop=True)
                last.then_inc(s["pv7"], 1)

            def G9(t):
                pe.wait_ge(s["rw"], N_RW * (t + 1))
                if t == 0:
                    pe.wait_ge(s["h5"], T)
                if t >= 1:
                    pe.wait_ge(s["rank9"], N_RANK9 * t)
                if t >= 2:
                    pe.wait_ge(s["ohte"], t - 1)
                m_.matmul(ps[0:R, 3, 64 * (t % 2):64 * (t % 2) + S], C("same", R), rk9[:, t % 2, 8:8 + S], start=True,
                          stop=True).then_inc(s["G9"], 1)

            def gather(t):
                pe.wait_ge(s["rank9"], N_RANK9 * (t + 1))
                if t == 0:
                    pe.wait_ge(s["aug"], 6)
                if t >= 1:
                    pe.wait_ge(s["ohte"], t)
                m_.matmul(ps[0:W3, 2, 0:XA], oh9[:, t % 2, :], xa[:, t, :], start=(t == 0), stop=(t == T - 1)
                          ).then_inc(s["acc"], 1)
                m_.transpose(ps[0:W3, 3, 128:128 + R], oh9[:, t % 2, :], ident[0:R, 0:R]).then_inc(s["oht"], 1)

            sweep((S7, AT_ATT1 + 1), (S0, AT_ATT0 + 2), (tr1, 1), (only(w2, 0), AT_FFN + 5), (T6, AT_QKV + 1),
                  (T5, AT_FFN + 1), (qkv, AT_QKV + 2), (only(w2, 1), AT_FFN + 4),
                  (lambda t: w1(t, 0, "loa", "w1a"), AT_FFN + 3, T + 1),
                  (lambda t: w1(t, 1, "lob", "w1b"), AT_FFN + 3, T + 1), (pj, 2), (gamps, 13, 1), (G, AT_CHOICE + 4),
                  (imp, AT_CHOICE + 3), (gx, AT_CHOICE + 5), (T2, AT_CHOICE + 1),
                  (lambda t: pT_(t, pr0, 2 * KK, "pn0", "PT0", "pt0", (("xT2", T), ("hid", T))), AT_ATT0 + 4),
                  (pv0, AT_ATT0 + 5), (hidp, AT_CHOICE + 2), (q_, AT_ATT0), (kv_, AT_ATT0),
                  (lambda t: project(t, oT0, wo0, BO_AT, "oT0", "h4", "op0", "xs"), AT_ATT0 + 6), (tq, AT_QKV + 3),
                  (lambda t: pT_(t, pr7, 2 * S, "pn7", "PT7", "pt7", (("xT6", T), ("rope", 2 * T))), AT_ATT1 + 3),
                  (lambda t: project(t, oT7, wp, BP_AT, "oT7", "h7", "op7", "tke"), AT_ATT1 + 5),
                  (gather, AT_ROUTE + 3), (G9, AT_ROUTE + 2), (pv7, AT_ATT1 + 4))

            def turn(bank, src, w, n, name, at_=0):
                for c in range(n):
                    last = m_.transpose(ps[0:w, bank, at_ + c * W3:at_ + (c + 1) * W3], src[:, c * w:(c + 1) * w],
                                        ident[0:W3, 0:W3])
                if name:
                    last.then_inc(s[name], 1)

            keep_warm(14)
            pe.wait_ge(s["t_hn"], 1)
            turn(4, t_hn, 128, DC, "t_T")

            def next_ones(bank, src, w, name):
                for j in range(1, NSEL):
                    last = m_.matmul(ps[0:W3, bank, (j - 1) * w:j * w], C(f"next{j}", W3), src, start=True, stop=True)
                last.then_inc(s[name], 1)

            next_ones(5, t_x[:, TOKEN_AT:XA], S, "t_tok")
            pe.wait_ge(s["t_hnT"], 1)
            pe.wait_ge(s["w2nd"], 32)
            for bank, cols in ((6, slice(0, 2 * D)), (7, slice(2 * D, 3 * D))):
                for c in range(DC):
                    last = m_.matmul(ps[0:W3, bank, 0:cols.stop - cols.start], t_hnT[:, c, :], wqkv_l[:, c, cols],
                                     start=(c == 0), stop=(c == DC - 1))
            last.then_inc(s["t_qkv"], 1)
            pe.wait_ge(s["t_v"], 1)
            next_ones(1, t_qkv[:, 2, :], D, "t_vn")
            pe.wait_ge(s["t_rot"], 1)
            next_ones(0, t_qkv[:, 1, :], D, "t_kn")
            keep_warm(22)
            pe.wait_ge(s["t_o"], 1)
            turn(4, t_o, 128, DC, "t_To")
            pe.wait_ge(s["t_oT"], 1)
            for c in range(DC):
                last = m_.matmul(ps[0:W3, 2, 0:D], t_oT[:, c, :], wo_l[:, c, :], start=(c == 0), stop=(c == DC - 1))
            last.then_inc(s["t_wo"], 1)
            keep_warm(8)
            pe.wait_ge(s["t_hn"], 2)
            turn(3, t_hn, 128, DC, "t_T")
            pe.wait_ge(s["t_hnT"], 2)
            pe.wait_ge(s["wlast"], 32)
            for f in range(FC):
                for c in range(DC):
                    last = m_.matmul(ps[:, 4 + f // 4, (f % 4) * W3:(f % 4 + 1) * W3], w1raw[:, c, f * 128:(f + 1) * 128],
                                     t_hnT[:, c, :], start=(c == 0), stop=(c == DC - 1))
            last.then_inc(s["t_w1"], 1)
            keep_warm(4)
            pe.wait_ge(s["t_g"], 1)
            for f in range(FC):
                last = m_.matmul(ps[0:W3, 6, 0:D], t_g[:, f, :], w2raw[:, f, :], start=(f == 0), stop=(f == FC - 1))
            last.then_inc(s["t_w2"], 1)
            keep_warm(4)
            pe.wait_ge(s["t_y"], 1)
            for t in range(T):
                if t >= 4:
                    pe.wait_ge(s["fin"], t - 3)
                if t == 0:
                    pe.wait_ge(s["base"], T)
                m_.matmul(ps[0:R, t % 4, 0:D], ohT[:, t, 0:R], t_y, start=True, stop=True).then_inc(s["t_put"], 1)


def kernel(**inputs):
    import concourse.bacc as _bacc
    from concourse.bass_utils import run_bass_kernel_spmd as _run

    a = {k: np.ascontiguousarray(v) for k, v in inputs.items()}
    P_ = 16
    n = a["x"].shape[2] // P_
    x = a["x"].reshape(IMAGES, 3, n, P_, n, P_).transpose(0, 2, 4, 3, 5, 1).reshape(IMAGES, PATCHES, PD)
    patches = np.zeros((T * IM, S, PD), x.dtype)
    patches[:IMAGES, 1:] = x

    vectors = np.zeros((128, N_VEC), np.float32)
    p = np.arange(128)
    for name, src in (("ln1_g", "L0_tok_ln1_g"), ("ln1_b", "L0_tok_ln1_b"), ("bq", "L0_attn_bq"), ("bk", "L0_attn_bk"),
                      ("bi1", "L0_attn_bi1"), ("wi2", "L0_attn_wi2")):
        at, w = _vat[name]
        vectors[:, at:at + w] = a[src].reshape(w, 128).T
    vectors[:, _vat["bi2"][0]] = a["L0_attn_bi2"][0]
    vectors[:, _vat["router_b"][0]] = a["L1_ffn_router_b"][0]
    vectors[:, _vat["part1"][0]] = p >= 1
    vectors[:, _vat["part2"][0]] = p >= 2
    names = {"b_proj": "L0_tok_b_proj", "ln2_g": "L0_tok_ln2_g", "ln2_b": "L0_tok_ln2_b", "cls": "L0_tok_cls_token",
             "router_w": "L1_ffn_router_w", "ln1": "L1_ffn_ln1", "ln2": "L1_ffn_ln2"}
    rows = np.concatenate([a[names[name]].reshape(1, D) for name in _rat], axis=1)
    wide_rows = np.concatenate([a[k].reshape(1, -1) for k in ("L0_ffn_b1", "L1_attn_bq", "L1_attn_bk", "L1_attn_bv", "L0_attn_bo",
                                                      "L0_ffn_b2", "L1_attn_bp", "L0_attn_bv")], axis=1)
    tensors = {
        "patches": patches.reshape(T * R, PD), "W_proj": a["L0_tok_W_proj"], "consts": shape_constants(),
        "vectors": vectors, "rows": rows, "wide_rows": wide_rows, "pos3": np.tile(a["L0_tok_pos_emb"][0], (IM, 1)),
        "wqT": a["L0_attn_wq"].T, "wkT": a["L0_attn_wk"].T, "wvT": a["L0_attn_wv"].T, "woT": a["L0_attn_wo"].T,
        "wi1T": a["L0_attn_wi1"].T, "W1T": a["L0_ffn_W1"].T, "W2T": a["L0_ffn_W2"].T,
        "wqkv1": np.concatenate([a["L1_attn_Wq"], a["L1_attn_Wk"], a["L1_attn_Wv"]], axis=1), "wp1": a["L1_attn_Wp"],
        "mask": a["L1_ffn_attention_mask"], "positions": a["L1_ffn_position_ids"],
        "wqkv2": np.concatenate([a["L1_ffn_wq"], a["L1_ffn_wk"], a["L1_ffn_wv"]], axis=1), "wo2": a["L1_ffn_wo"],
        "w1f": a["L1_ffn_w1"], "w2f": a["L1_ffn_w2"],
    }
    nc = _bacc.Bacc("TRN2", target_bir_lowering=False, num_devices=1)
    arrays, args = {}, {}
    for name, value in tensors.items():
        value = np.ascontiguousarray(value)
        arrays[f"in_{name}"] = value
        args[name] = nc.dram_tensor(f"in_{name}", value.shape, mybir.dt.from_np(value.dtype), kind="ExternalInput").ap()
    args["out"] = nc.dram_tensor("out", (ROWS, D), F32, kind="ExternalOutput").ap()
    vit_tower(nc, **args)
    r = _run(nc, [arrays], core_ids=[0])
    return r.results[0]["out"].reshape(IMAGES, S, D)
```
